# Optimizing a Trainium2 kernel written in Bass

```python
import numpy as np
import jax
import jax.numpy as jnp

def _softmax(x, axis=-1):
    return jax.nn.softmax(x, axis=axis)

def _gelu(x):
    return jax.nn.gelu(x, approximate=True)

def _silu(x):
    return jax.nn.silu(x)

def _sigmoid(x):
    return jax.nn.sigmoid(x)

def _layernorm(x, axis=-1, eps=1e-05):
    m = jnp.mean(x, axis=axis, keepdims=True)
    v = jnp.var(x, axis=axis, keepdims=True)
    return (x - m) / jnp.sqrt(v + eps)

def _scatter_add(tgt, idx, src, axis=0):
    return tgt.at[idx].add(src)

def _segment_sum(src, seg, n):
    return jax.ops.segment_sum(src, seg, n)
kernel_name = 'mk_gnn_preln_d4_gnn_r64_c431f0'

def setup_inputs(seed: int=0):
    np.random.seed(seed)
    _w = jnp.asarray

    def _rec_inputs():
        import jax
        import jax.numpy as jnp
        _gk = jax.random.key(seed)
        x = -0.0003713 + 1 * jax.random.normal(jax.random.fold_in(_gk, 1), (50000, 128), jnp.float32)
        src = jax.random.randint(jax.random.fold_in(_gk, 2), (25000,), 0, 50000, jnp.int32)
        dst = jax.random.randint(jax.random.fold_in(_gk, 3), (25000,), 0, 50000, jnp.int32)
        _o = jnp.argsort(dst, stable=True)
        src = src[_o]
        dst = dst[_o]
        edge_attr_128 = -4.21973e-05 + 0.999841 * jax.random.normal(jax.random.fold_in(_gk, 12), (25000, 128), jnp.float32)
        return (x, src, dst, edge_attr_128)
    x, src, dst, edge_attr_128 = _rec_inputs()

    def _L0_gnn_setup():
        import jax, jax.numpy as jnp
        import numpy as np
        EMB_DIM = 128
        N_NODES = 100000
        N_EDGES = 9375
        BN_EPS = 1e-05
        key = jax.random.key(seed)
        ks = jax.random.split(key, 10)
        d = EMB_DIM
        lim = 1.0 / np.sqrt(d)
        return {'node_feats': jax.random.normal(ks[0], (N_NODES, d), dtype=jnp.float32), 'edge_feats': jax.random.normal(ks[1], (N_EDGES, d), dtype=jnp.float32), 'W1': jax.random.uniform(ks[2], (d, d), jnp.float32, -lim, lim), 'b1': jax.random.uniform(ks[3], (d,), jnp.float32, -lim, lim), 'W2': jax.random.uniform(ks[4], (d, d), jnp.float32, -lim, lim), 'b2': jax.random.uniform(ks[5], (d,), jnp.float32, -lim, lim), 'gamma': jnp.ones((d,), jnp.float32), 'beta': jnp.zeros((d,), jnp.float32), 'src': jax.random.randint(ks[6], (N_EDGES,), 0, N_NODES, dtype=jnp.int32), 'dst': jax.random.randint(ks[7], (N_EDGES,), 0, N_NODES, dtype=jnp.int32)}
    _L0_gnn_all = _L0_gnn_setup()
    _L0_gnn_in = {k: v for k, v in _L0_gnn_all.items() if k in ('W1', 'b1', 'W2', 'b2', 'gamma', 'beta')}
    del _L0_gnn_all

    def _L1_gnn_setup():
        import jax, jax.numpy as jnp
        import numpy as np
        N = 20000
        E = 5000
        D = 128
        H = 4
        NEG_SLOPE = 0.2
        LN_EPS = 1e-05

        def gatv2_conv(x, src, dst, Wl, Wr, att, bias):
            n = x.shape[0]
            xl = (x @ Wl).reshape(n, H, D)
            xr = (x @ Wr).reshape(n, H, D)
            m = jax.nn.leaky_relu(xl[src] + xr[dst], NEG_SLOPE)
            e = jnp.einsum('ehd,hd->eh', m, att)
            e_max = jax.ops.segment_max(e, dst, num_segments=n)
            ex = jnp.exp(e - e_max[dst])
            denom = jax.ops.segment_sum(ex, dst, num_segments=n)
            alpha = ex / (denom[dst] + 1e-16)
            out = jax.ops.segment_sum(alpha[:, :, None] * xl[src], dst, num_segments=n)
            return out.mean(axis=1) + bias

        def layer_norm(x, g, b):
            mu = x.mean(axis=-1, keepdims=True)
            var = ((x - mu) ** 2).mean(axis=-1, keepdims=True)
            return (x - mu) * jax.lax.rsqrt(var + LN_EPS) * g + b
        key = jax.random.key(seed)
        ks = jax.random.split(key, 12)
        s = 0.05
        w = lambda k, shp: jax.random.normal(k, shp, jnp.float32) * s
        return {'x': jax.random.normal(ks[0], (N, D), jnp.float32), 'src': jax.random.randint(ks[1], (E,), 0, N, jnp.int32), 'dst': jax.random.randint(ks[2], (E,), 0, N, jnp.int32), 'Wl1': w(ks[3], (D, H * D)), 'Wr1': w(ks[4], (D, H * D)), 'att1': w(ks[5], (H, D)), 'b1': jnp.zeros((D,), jnp.float32), 'g1': jnp.ones((D,), jnp.float32), 'be1': jnp.zeros((D,), jnp.float32), 'Wl2': w(ks[6], (D, H * D)), 'Wr2': w(ks[7], (D, H * D)), 'att2': w(ks[8], (H, D)), 'b2': jnp.zeros((D,), jnp.float32), 'g2': jnp.ones((D,), jnp.float32), 'be2': jnp.zeros((D,), jnp.float32)}
    _L1_gnn_all = _L1_gnn_setup()
    _L1_gnn_in = {k: v for k, v in _L1_gnn_all.items() if k in ('Wl1', 'Wr1', 'att1', 'b1', 'g1', 'be1', 'Wl2', 'Wr2', 'att2', 'b2', 'g2', 'be2')}
    del _L1_gnn_all

    def _L2_gnn_setup():
        import jax, jax.numpy as jnp
        import numpy as np
        LEAKY_SLOPE = 0.2
        N_NODES = 50000
        N_EDGES = 12500
        IN_DIM = 128
        OUT_DIM = 64
        HEADS = 4
        MLP_HID = 256
        MLP_OUT = 128

        def _gat_forward(node_embeddings, src, dst, W_n, a_src, a_dst, mlp_W1, mlp_b1, mlp_W2, mlp_b2):
            N = node_embeddings.shape[0]
            h = jnp.einsum('nc,hcd->nhd', node_embeddings, W_n)
            s_src = jnp.einsum('nhd,hd->nh', h, a_src)
            s_dst = jnp.einsum('nhd,hd->nh', h, a_dst)
            e = jax.nn.leaky_relu(s_src[src] + s_dst[dst], negative_slope=LEAKY_SLOPE)
            e_max = jax.ops.segment_max(e, dst, num_segments=N)
            ex = jnp.exp(e - e_max[dst])
            den = jax.ops.segment_sum(ex, dst, num_segments=N)
            m = h[src]
            num = jax.ops.segment_sum(ex[:, :, None] * m, dst, num_segments=N)
            safe_den = jnp.where(den > 0, den, 1.0)
            head_out = jax.nn.relu(num / safe_den[:, :, None])
            concat = head_out.reshape(N, -1)
            hidden = jax.nn.relu(concat @ mlp_W1 + mlp_b1)
            return hidden @ mlp_W2 + mlp_b2
        key = jax.random.key(seed)
        ks = jax.random.split(key, 10)
        node_embeddings = jax.random.normal(ks[0], (N_NODES, IN_DIM), dtype=jnp.float32)
        src = jax.random.randint(ks[1], (N_EDGES,), 0, N_NODES, dtype=jnp.int32)
        dst = jax.random.randint(ks[2], (N_EDGES,), 0, N_NODES, dtype=jnp.int32)
        W_n = jax.random.normal(ks[3], (HEADS, IN_DIM, OUT_DIM), dtype=jnp.float32) * (1.0 / np.sqrt(IN_DIM))
        a_src = jax.random.normal(ks[4], (HEADS, OUT_DIM), dtype=jnp.float32) * (1.0 / np.sqrt(OUT_DIM))
        a_dst = jax.random.normal(ks[5], (HEADS, OUT_DIM), dtype=jnp.float32) * (1.0 / np.sqrt(OUT_DIM))
        mlp_W1 = jax.random.normal(ks[6], (HEADS * OUT_DIM, MLP_HID), dtype=jnp.float32) * (1.0 / np.sqrt(HEADS * OUT_DIM))
        mlp_b1 = jnp.zeros((MLP_HID,), dtype=jnp.float32)
        mlp_W2 = jax.random.normal(ks[7], (MLP_HID, MLP_OUT), dtype=jnp.float32) * (1.0 / np.sqrt(MLP_HID))
        mlp_b2 = jnp.zeros((MLP_OUT,), dtype=jnp.float32)
        return {'node_embeddings': node_embeddings, 'src': src, 'dst': dst, 'W_n': W_n, 'a_src': a_src, 'a_dst': a_dst, 'mlp_W1': mlp_W1, 'mlp_b1': mlp_b1, 'mlp_W2': mlp_W2, 'mlp_b2': mlp_b2}
    _L2_gnn_all = _L2_gnn_setup()
    _L2_gnn_in = {k: v for k, v in _L2_gnn_all.items() if k in ('W_n', 'a_src', 'a_dst', 'mlp_W1', 'mlp_b1', 'mlp_W2', 'mlp_b2')}
    del _L2_gnn_all

    def _L3_gnn_setup():
        import jax, jax.numpy as jnp
        import numpy as np
        N_NODES = 100000
        WEIGHT = 0.5
        key = jax.random.key(seed)
        k1, k2 = jax.random.split(key)
        x = jax.random.normal(k1, (N_NODES, 128), dtype=jnp.float32)
        edge_index = jax.random.randint(k2, (2, 25000), 0, N_NODES, dtype=jnp.int64)
        return {'x': x, 'edge_index': edge_index}
    _L3_gnn_all = _L3_gnn_setup()
    _L3_gnn_in = {k: v for k, v in _L3_gnn_all.items() if k in ()}
    del _L3_gnn_all
    return {'x': x, 'src': src, 'dst': dst, 'edge_attr_128': edge_attr_128, 'L0_gnn_W1': _L0_gnn_in['W1'], 'L0_gnn_b1': _L0_gnn_in['b1'], 'L0_gnn_W2': _L0_gnn_in['W2'], 'L0_gnn_b2': _L0_gnn_in['b2'], 'L0_gnn_gamma': _L0_gnn_in['gamma'], 'L0_gnn_beta': _L0_gnn_in['beta'], 'L1_gnn_Wl1': _L1_gnn_in['Wl1'], 'L1_gnn_Wr1': _L1_gnn_in['Wr1'], 'L1_gnn_att1': _L1_gnn_in['att1'], 'L1_gnn_b1': _L1_gnn_in['b1'], 'L1_gnn_g1': _L1_gnn_in['g1'], 'L1_gnn_be1': _L1_gnn_in['be1'], 'L1_gnn_Wl2': _L1_gnn_in['Wl2'], 'L1_gnn_Wr2': _L1_gnn_in['Wr2'], 'L1_gnn_att2': _L1_gnn_in['att2'], 'L1_gnn_b2': _L1_gnn_in['b2'], 'L1_gnn_g2': _L1_gnn_in['g2'], 'L1_gnn_be2': _L1_gnn_in['be2'], 'L2_gnn_W_n': _L2_gnn_in['W_n'], 'L2_gnn_a_src': _L2_gnn_in['a_src'], 'L2_gnn_a_dst': _L2_gnn_in['a_dst'], 'L2_gnn_mlp_W1': _L2_gnn_in['mlp_W1'], 'L2_gnn_mlp_b1': _L2_gnn_in['mlp_b1'], 'L2_gnn_mlp_W2': _L2_gnn_in['mlp_W2'], 'L2_gnn_mlp_b2': _L2_gnn_in['mlp_b2']}

def reference(x, src, dst, edge_attr_128, L0_gnn_W1, L0_gnn_b1, L0_gnn_W2, L0_gnn_b2, L0_gnn_gamma, L0_gnn_beta, L1_gnn_Wl1, L1_gnn_Wr1, L1_gnn_att1, L1_gnn_b1, L1_gnn_g1, L1_gnn_be1, L1_gnn_Wl2, L1_gnn_Wr2, L1_gnn_att2, L1_gnn_b2, L1_gnn_g2, L1_gnn_be2, L2_gnn_W_n, L2_gnn_a_src, L2_gnn_a_dst, L2_gnn_mlp_W1, L2_gnn_mlp_b1, L2_gnn_mlp_W2, L2_gnn_mlp_b2):
    import jax
    import jax.numpy as jnp

    def _L0_gnn_ref(node_feats, edge_feats, W1, b1, W2, b2, gamma, beta, src, dst):
        import jax, jax.numpy as jnp
        import numpy as np
        EMB_DIM = 128
        N_NODES = 100000
        N_EDGES = 9375
        BN_EPS = 1e-05
        n_nodes = node_feats.shape[0]
        msg = jax.nn.relu(node_feats[src] + edge_feats)
        agg = jax.ops.segment_sum(msg, dst, num_segments=n_nodes)
        h = node_feats + agg
        h = jax.nn.relu(h @ W1.T + b1) @ W2.T + b2
        mean = jnp.mean(h, axis=0)
        var = jnp.var(h, axis=0)
        h = (h - mean) * jax.lax.rsqrt(var + BN_EPS) * gamma + beta
        return h

    def _L1_gnn_ref(x, src, dst, Wl1, Wr1, att1, b1, g1, be1, Wl2, Wr2, att2, b2, g2, be2):
        import jax, jax.numpy as jnp
        import numpy as np
        N = 20000
        E = 5000
        D = 128
        H = 4
        NEG_SLOPE = 0.2
        LN_EPS = 1e-05

        def gatv2_conv(x, src, dst, Wl, Wr, att, bias):
            n = x.shape[0]
            xl = (x @ Wl).reshape(n, H, D)
            xr = (x @ Wr).reshape(n, H, D)
            m = jax.nn.leaky_relu(xl[src] + xr[dst], NEG_SLOPE)
            e = jnp.einsum('ehd,hd->eh', m, att)
            e_max = jax.ops.segment_max(e, dst, num_segments=n)
            ex = jnp.exp(e - e_max[dst])
            denom = jax.ops.segment_sum(ex, dst, num_segments=n)
            alpha = ex / (denom[dst] + 1e-16)
            out = jax.ops.segment_sum(alpha[:, :, None] * xl[src], dst, num_segments=n)
            return out.mean(axis=1) + bias

        def layer_norm(x, g, b):
            mu = x.mean(axis=-1, keepdims=True)
            var = ((x - mu) ** 2).mean(axis=-1, keepdims=True)
            return (x - mu) * jax.lax.rsqrt(var + LN_EPS) * g + b
        n = x.shape[0]
        loops = jnp.arange(n, dtype=src.dtype)
        s = jnp.concatenate([src, loops])
        d = jnp.concatenate([dst, loops])
        h = gatv2_conv(x, s, d, Wl1, Wr1, att1, b1)
        h = layer_norm(h, g1, be1)
        h = jax.nn.relu(h + x)
        h2 = gatv2_conv(h, s, d, Wl2, Wr2, att2, b2)
        h2 = layer_norm(h2, g2, be2)
        return h2 + h

    def _L2_gnn_ref(node_embeddings, src, dst, W_n, a_src, a_dst, mlp_W1, mlp_b1, mlp_W2, mlp_b2):
        import jax, jax.numpy as jnp
        import numpy as np
        LEAKY_SLOPE = 0.2
        N_NODES = 50000
        N_EDGES = 12500
        IN_DIM = 128
        OUT_DIM = 64
        HEADS = 4
        MLP_HID = 256
        MLP_OUT = 128

        def _gat_forward(node_embeddings, src, dst, W_n, a_src, a_dst, mlp_W1, mlp_b1, mlp_W2, mlp_b2):
            N = node_embeddings.shape[0]
            h = jnp.einsum('nc,hcd->nhd', node_embeddings, W_n)
            s_src = jnp.einsum('nhd,hd->nh', h, a_src)
            s_dst = jnp.einsum('nhd,hd->nh', h, a_dst)
            e = jax.nn.leaky_relu(s_src[src] + s_dst[dst], negative_slope=LEAKY_SLOPE)
            e_max = jax.ops.segment_max(e, dst, num_segments=N)
            ex = jnp.exp(e - e_max[dst])
            den = jax.ops.segment_sum(ex, dst, num_segments=N)
            m = h[src]
            num = jax.ops.segment_sum(ex[:, :, None] * m, dst, num_segments=N)
            safe_den = jnp.where(den > 0, den, 1.0)
            head_out = jax.nn.relu(num / safe_den[:, :, None])
            concat = head_out.reshape(N, -1)
            hidden = jax.nn.relu(concat @ mlp_W1 + mlp_b1)
            return hidden @ mlp_W2 + mlp_b2
        return _gat_forward(node_embeddings, src, dst, W_n, a_src, a_dst, mlp_W1, mlp_b1, mlp_W2, mlp_b2)

    def _L3_gnn_ref(x, edge_index):
        import jax, jax.numpy as jnp
        import numpy as np
        N_NODES = 100000
        WEIGHT = 0.5
        src, dst = (edge_index[0], edge_index[1])
        n = x.shape[0]
        agg_sum = jax.ops.segment_sum(x[src], dst, num_segments=n)
        deg = jax.ops.segment_sum(jnp.ones_like(dst, dtype=x.dtype), dst, num_segments=n)
        agg_mean = agg_sum / jnp.maximum(deg, 1.0)[:, None]
        return x + WEIGHT * agg_mean
    edge_index = jnp.stack([src, dst])
    h = jnp.maximum(_layernorm(x, axis=-1), 0.0)
    x = x + _L0_gnn_ref(h, edge_attr_128, L0_gnn_W1, L0_gnn_b1, L0_gnn_W2, L0_gnn_b2, L0_gnn_gamma, L0_gnn_beta, src, dst)
    h = jnp.maximum(_layernorm(x, axis=-1), 0.0)
    x = x + _L1_gnn_ref(h, src, dst, L1_gnn_Wl1, L1_gnn_Wr1, L1_gnn_att1, L1_gnn_b1, L1_gnn_g1, L1_gnn_be1, L1_gnn_Wl2, L1_gnn_Wr2, L1_gnn_att2, L1_gnn_b2, L1_gnn_g2, L1_gnn_be2)
    h = jnp.maximum(_layernorm(x, axis=-1), 0.0)
    x = x + _L2_gnn_ref(h, src, dst, L2_gnn_W_n, L2_gnn_a_src, L2_gnn_a_dst, L2_gnn_mlp_W1, L2_gnn_mlp_b1, L2_gnn_mlp_W2, L2_gnn_mlp_b2)
    h = jnp.maximum(_layernorm(x, axis=-1), 0.0)
    x = x + _L3_gnn_ref(h, edge_index)
    return x

_drawn_inputs = setup_inputs


def setup_inputs(seed=0):
    import zlib

    import numpy as np

    out = dict(_drawn_inputs(seed))
    spreads = {'L0_gnn_gamma': (1.0, 0.2),
     'L0_gnn_beta': (0.0, 0.1),
     'L1_gnn_b1': (0.0, 0.1),
     'L1_gnn_g1': (1.0, 0.2),
     'L1_gnn_be1': (0.0, 0.1),
     'L1_gnn_b2': (0.0, 0.1),
     'L1_gnn_g2': (1.0, 0.2),
     'L1_gnn_be2': (0.0, 0.1),
     'L2_gnn_mlp_b1': (0.0, 0.317),
     'L2_gnn_mlp_b2': (0.0, 0.1)}
    factors = {'L0_gnn_b2': 8.0,
     'L1_gnn_Wr1': 8.0,
     'L1_gnn_att1': 4.225,
     'L1_gnn_Wr2': 8.0,
     'L1_gnn_att2': 6.621,
     'L2_gnn_a_src': 8.0,
     'L2_gnn_a_dst': 8.0}
    for name, (base, spread) in spreads.items():
        noise = np.random.default_rng([zlib.crc32(name.encode()), seed]).standard_normal(out[name].shape)
        drawn = base * np.exp(spread * noise) if base else spread * noise
        out[name] = jnp.asarray(drawn.astype(out[name].dtype))
    for name, factor in factors.items():
        out[name] = (out[name] * factor).astype(out[name].dtype)
    return out
```

```python
import numpy as np
from contextlib import ExitStack

import concourse.bass as bass
from concourse import mybir

F32 = mybir.dt.float32
I32 = mybir.dt.int32
ALU = mybir.AluOpType
ACT = mybir.ActivationFunctionType
AX = mybir.AxisListType

P = 128
D = 128
H = 4
SUB = 4
TILE = P * SUB
K = 7
EPS = 1e-5
SLOPE = 0.2
BEHIND = 3
BIG = 1e30
CH = P // H
HID = 256
HD = 64


def cdiv(a, b):
    return -(-a // b)


def padded(n):
    return cdiv(n + 1, TILE * K) * TILE * K


class Phase:

    def __init__(self, nc, name):
        self.nc, self.name, self.stack, self.used = nc, name, ExitStack(), []

    def __enter__(self):
        self.stack.__enter__()
        return self

    def __exit__(self, *error):
        if error[0] is None:
            with self.nc.Block() as block:
                @block.gpsimd
                def _(pool):
                    for s in self.used:
                        pool.sem_clear(s)
        return self.stack.__exit__(*error)

    def sb(self, name, shape, dt=F32):
        return self.stack.enter_context(self.nc.sbuf_tensor(self.name + name, shape, dt))

    def ps(self, name, shape, dt=F32):
        return self.stack.enter_context(self.nc.psum_tensor(self.name + name, shape, dt))

    def sem(self, name):
        s = self.stack.enter_context(self.nc.semaphore(self.name + name))
        self.used.append(s)
        return s

    def sbs(self, name, shape, dt=F32, n=K):
        return [self.sb(f"{name}{k}", shape, dt) for k in range(n)]

    def sems(self, name, n=K):
        return [self.sem(f"{name}{k}") for k in range(n)]


def node_rows(table, n):
    return table[bass.ds(n * TILE, TILE), :].rearrange("(p a) d -> p a d", p=P)


def edge_rows(table, n):
    return table[bass.ds(n * TILE, TILE), :].rearrange("(s p) d -> p s d", p=P)


def edge_span(row, n, parts):
    return row[:, bass.ds(n * TILE, TILE)].to_broadcast([parts, TILE])


def mean_and_variance(dve, stats, mv, stats_done, value, own_wait):
    dve.wait_ge(stats_done, value)
    dve.sem_inc(own_wait, 1)
    for a in range(SUB):
        last = dve.bn_aggr(out=mv[:, a, :], in_=stats[:, a, :])
    return last


def row_stats(dve, x, stats):
    for a in range(SUB):
        last = dve.bn_stats(out=stats[:, a, :], in_=x[:, a, :])
    return last


def prepare_indices(nc, g):
    nt, flat = g.NTE, g.EP // P
    with Phase(nc, "prepare_indices_") as m:
        idx = m.sb("idx", [P, nt, 20], I32)
        nxt = m.sb("nxt", [P, nt, SUB], I32)
        eid = m.sb("eid", [P, nt, SUB], I32)
        dstf, nxtf, same, dump = (m.sb(n, [P, nt, SUB]) for n in ("dstf", "nxtf", "same", "dump"))
        lastf, addf = m.sb("lastf", [P, nt, SUB]), m.sb("addf", [P, nt, SUB])
        rowi = m.sb("rowi", [P, 3, flat], I32)
        rowf = m.sb("rowf", [P, 3, flat])
        keep = m.sb("keep", [P, 2, flat])
        none = m.sb("none", [P, g.NP // P], I32)
        loaded, loaded_rows, ids_made, steps = m.sem("loaded"), m.sem("loaded_rows"), m.sem("ids_made"), m.sem("steps")
        idx_made, keep_made, stored, none_made = m.sem("idx_made"), m.sem("keep_made"), m.sem("stored"), m.sem("none_made")
        with nc.Block() as block:
            @block.sync
            def _(sp):
                tiles = lambda x: x.rearrange("t p s -> p t s")
                with nc.allow_non_contiguous_dma("four indices a run"):
                    sp.dma_start(idx[:, :, 0:4], tiles(g.src_t)).then_inc(loaded, 16)
                    sp.dma_start(idx[:, :, 4:8], tiles(g.dst_t)).then_inc(loaded, 16)
                    sp.dma_start(nxt[:, :, :], tiles(g.nxt_t)).then_inc(loaded, 16)
                for j, row in enumerate((g.dst_r, g.prev_r, g.next_r)):
                    sp.dma_start(rowi[:, j, :], row.rearrange("o (p j) -> (o p) j", p=P)).then_inc(loaded_rows, 16)
                sp.wait_ge(none_made, 1)
                sp.dma_start(g.LAST.rearrange("(p j) o -> p (j o)", p=P), none[:, :]).then_inc(stored, 16)
                sp.wait_ge(keep_made, 1)
                sp.dma_start(g.KEEP.rearrange("o (p j) -> (o p) j", p=P), keep[:, 0, :]).then_inc(stored, 16)
                sp.dma_start(g.KEEPN.rearrange("o (p j) -> (o p) j", p=P), keep[:, 1, :]).then_inc(stored, 16)
                sp.wait_ge(idx_made, 1)
                sp.dma_start(g.IDX.rearrange("t p s -> p t s"), idx[:, :, :]).then_inc(stored, 16)
                sp.wait_ge(stored, 4 * 16)

            @block.gpsimd
            def _(pool):
                pool.iota(eid[:, :, :], pattern=[[TILE, nt], [P, SUB]], base=0, channel_multiplier=1).then_inc(ids_made, 1)
                pool.memset(none[:, :], g.EP).then_inc(none_made, 1)

            @block.vector
            def _(dve):
                count = [0]

                def step(instruction):
                    count[0] += 1
                    instruction.then_inc(steps, 1)
                    dve.wait_ge(steps, count[0])

                dve.wait_ge(loaded_rows, 3 * 16)
                step(dve.tensor_copy(rowf[:, :, :], rowi[:, :, :]))
                dve.tensor_tensor(keep[:, 0, :], rowf[:, 0, :], rowf[:, 1, :], ALU.is_equal)
                dve.tensor_tensor(keep[:, 1, :], rowf[:, 0, :], rowf[:, 2, :], ALU.is_equal).then_inc(keep_made, 1)
                dve.wait_ge(loaded, 3 * 16)
                dve.wait_ge(ids_made, 1)
                dve.tensor_copy(dstf[:, :, :], idx[:, :, 4:8])
                dve.tensor_copy(dump[:, :, :], eid[:, :, :])
                dve.tensor_copy(idx[:, :, 16:20], eid[:, :, :])
                step(dve.tensor_copy(nxtf[:, :, :], nxt[:, :, :]))
                step(dve.tensor_tensor(same[:, :, :], dstf[:, :, :], nxtf[:, :, :], ALU.is_equal))
                dve.scalar_tensor_tensor(out=lastf[:, :, :], in0=same[:, :, :], scalar=float(g.NP), in1=dstf[:, :, :],
                                         op0=ALU.mult, op1=ALU.add)
                step(dve.scalar_tensor_tensor(out=dump[:, :, :], in0=dump[:, :, :], scalar=float(g.NP), in1=dstf[:, :, :],
                                              op0=ALU.add, op1=ALU.subtract))
                step(dve.tensor_tensor(addf[:, :, :], dump[:, :, :], same[:, :, :], ALU.mult))
                step(dve.tensor_tensor(addf[:, :, :], addf[:, :, :], dstf[:, :, :], ALU.add))
                dve.tensor_copy(idx[:, :, 8:12], lastf[:, :, :])
                dve.tensor_copy(idx[:, :, 12:16], addf[:, :, :]).then_inc(idx_made, 1)


def first_norm(nc, g):
    nb = g.NTN // K
    with Phase(nc, "first_norm_") as m:
        x, h = m.sbs("x", [P, SUB, D]), m.sbs("h", [P, SUB, D])
        stats, mv = m.sbs("stats", [P, SUB, 6]), m.sbs("mv", [P, SUB, 2])
        std, rstd, shift = m.sbs("std", [P, SUB]), m.sbs("rstd", [P, SUB]), m.sbs("shift", [P, SUB])
        eps, zero = m.sb("eps", [P, 1]), m.sb("zero", [P, K * TILE])
        x_in, h_out, h_made = m.sems("x_in"), m.sems("h_out"), m.sems("h_made")
        eps_set, zero_set = m.sem("eps_set"), m.sem("zero_set")
        zeros_out = g.zeros_out
        stats_done, own, mv_done, std_done, rstd_done, shift_done = (
            m.sem(n) for n in ("stats_done", "own", "mv_done", "std_done", "rstd_done", "shift_done"))
        with nc.Block() as block:
            @block.sync
            def _(sp):
                for k in range(K):
                    sp.dma_start(x[k][:, :, :], node_rows(g.x, k)).then_inc(x_in[k], 16)
                with sp.Fori(1, nb) as i:
                    for k in range(K):
                        sp.wait_ge(h_made[k], i)
                        sp.dma_start(node_rows(g.H, (i - 1) * K + k), h[k][:, :, :]).then_inc(h_out[k], 16)
                        sp.dma_start(x[k][:, :, :], node_rows(g.x, i * K + k)).then_inc(x_in[k], 16)
                for k in range(K):
                    sp.wait_ge(h_made[k], nb)
                    sp.dma_start(node_rows(g.H, (nb - 1) * K + k), h[k][:, :, :]).then_inc(h_out[k], 16)
                for k in range(K):
                    sp.wait_ge(h_out[k], 16 * nb)

            @block.gpsimd
            def _(pool):
                pool.memset(zero[:, :], 0.0).then_inc(zero_set, 1)
                pool.wait_ge(zero_set, 1)
                with pool.Fori(0, nb) as i:
                    pool.dma_start(g.AGG[bass.ds(i * (K * TILE), K * TILE), :].rearrange("(p a) d -> p (a d)", p=P),
                                   zero[:, :]).then_inc(zeros_out, 16)
                for i in range(g.NTE // K):
                    pool.dma_start(g.out[g.NP + i * K * TILE:g.NP + (i + 1) * K * TILE, :].rearrange("(p a) d -> p (a d)", p=P),
                                   zero[:, :]).then_inc(zeros_out, 16)
                pool.wait_ge(zeros_out, 16 * (nb + g.NTE // K))

            @block.vector
            def _(dve):
                dve.memset(eps[:, :], EPS).then_inc(eps_set, 1)
                with dve.Fori(0, nb) as i:
                    def scales(k):
                        dve.wait_ge(std_done, i * K + k + 1)
                        dve.reciprocal(rstd[k][:, :], std[k][:, :]).then_inc(rstd_done, 1)
                        dve.wait_ge(rstd_done, i * K + k + 1)
                        dve.scalar_tensor_tensor(out=shift[k][:, :], in0=mv[k][:, :, 0], scalar=-1.0, in1=rstd[k][:, :],
                                                 op0=ALU.mult, op1=ALU.mult).then_inc(shift_done, 1)

                    for k in range(K):
                        dve.wait_ge(x_in[k], (i + 1) * 16)
                        row_stats(dve, x[k], stats[k]).then_inc(stats_done, 1)
                        if k:
                            scales(k - 1)
                        mean_and_variance(dve, stats[k], mv[k], stats_done, i * K + k + 1, own).then_inc(mv_done, 1)
                    scales(K - 1)

            @block.scalar
            def _(act):
                act.wait_ge(eps_set, 1)
                with act.Fori(0, nb) as i:
                    def normalize(k):
                        act.wait_ge(shift_done, i * K + k + 1)
                        act.wait_ge(h_out[k], i * 16)
                        for a in range(SUB):
                            last = act.activation(h[k][:, a, :], x[k][:, a, :], ACT.Relu,
                                                  bias=shift[k][:, a:a + 1], scale=rstd[k][:, a:a + 1])
                        last.then_inc(h_made[k], 1)

                    for k in range(K):
                        act.wait_ge(mv_done, i * K + k + 1)
                        act.activation(std[k][:, :], mv[k][:, :, 1], ACT.Sqrt, bias=eps[:, :]).then_inc(std_done, 1)
                        if k:
                            normalize(k - 1)
                    normalize(K - 1)


def wait_alone(eng, sem, value, own):
    eng.wait_ge(sem, value)
    eng.sem_inc(own, 1)


def gather(pool, out, table, index):
    return pool.indirect_dma_start(out=out, out_offset=None, in_=table,
                                   in_offset=bass.IndirectOffsetOnAxis(ap=index, axis=0))


def scatter_last(pool, table, index, rows, bound):
    return pool.indirect_dma_start(out=table, out_offset=bass.IndirectOffsetOnAxis(ap=index, axis=0),
                                   in_=rows, in_offset=None, bounds_check=bound, oob_is_err=False)


def make_identity(pool, ident, made, cleared):
    pool.memset(ident[:, :], 0.0).then_inc(cleared, 1)
    pool.wait_ge(cleared, 1)
    pool.affine_select(out=ident[:, :], in_=ident[:, :], compare_op=ALU.not_equal, fill=1.0, base=0,
                       pattern=[[-1, P]], channel_multiplier=1).then_inc(made, 1)


def gine_edges(nc, g):
    nb = g.NTE // K
    with Phase(nc, "gine_edges_") as m:
        ident = m.sb("ident", [P, P])
        idx = m.sbs("idx", [P, 20], I32)
        hs, ea, msg = m.sbs("hs", [P, SUB, D]), m.sbs("ea", [P, SUB, D]), m.sbs("msg", [P, SUB, D])
        keep, msgT, sumT, rows = (m.sbs(n, [P, TILE]) for n in ("keep", "msgT", "sumT", "rows"))
        turned = [m.ps(f"turned{j}", [P, TILE]) for j in range(2)]
        back = [m.ps(f"back{j}", [P, TILE]) for j in range(2)]
        idx_in, tile_in, own = m.sems("idx_in"), m.sems("tile_in"), m.sem("own")
        hs_in, agg_out = g.gathered, g.scattered
        hs0, agg0 = g.start(hs_in, nb * 64), g.start(agg_out, nb * 64)
        cleared, ident_made, tail_set = m.sem("cleared"), m.sem("ident_made"), m.sem("tail_set")
        msg_made, msgT_psum, msgT_made, scanned, back_psum, rows_made = (
            m.sem(n) for n in ("msg_made", "msgT_psum", "msgT_made", "scanned", "back_psum", "rows_made"))
        with nc.Block() as block:
            @block.sync
            def _(sp):
                def load(k, i):
                    sp.dma_start(idx[k][:, :], g.IDX[bass.ds(i * K + k, 1), :, :].rearrange("t p s -> (t p) s")).then_inc(idx_in[k], 16)
                    sp.dma_start(ea[k][:, :, :], edge_rows(g.ea, i * K + k)).then_inc(tile_in[k], 16)
                    sp.dma_start(keep[k][:, :], edge_span(g.KEEP, i * K + k, P)).then_inc(tile_in[k], 16)

                for k in range(K):
                    load(k, 0)
                if nb > 1:
                    with sp.Fori(1, nb) as i:
                        for k in range(K):
                            sp.wait_ge(agg_out[k], i * 64 + agg0)
                            load(k, i)

            @block.gpsimd
            def _(pool):
                make_identity(pool, ident, ident_made, cleared)

                def gather_tile(k, i):
                    wait_alone(pool, idx_in[k], (i + 1) * 16, own)
                    for s in range(SUB):
                        gather(pool, hs[k][:, s, :], g.H[:, :], idx[k][:, s:s + 1]).then_inc(hs_in[k], 16)

                def body(i, more):
                    for k in range(K):
                        wait_alone(pool, rows_made, i * K + k + 1, own)
                        for s in range(SUB):
                            scatter_last(pool, g.AGG[:, :], idx[k][:, 8 + s:9 + s], rows[k][:, s * P:(s + 1) * P],
                                         g.NP - 1).then_inc(agg_out[k], 16)
                        if more and k >= BEHIND:
                            gather_tile(k - BEHIND, i + 1)
                    if more:
                        for k in range(K - BEHIND, K):
                            gather_tile(k, i + 1)

                for k in range(K):
                    gather_tile(k, 0)
                if nb > 1:
                    with pool.Fori(0, nb - 1) as i:
                        body(i, True)
                body(nb - 1, False)
                for k in range(K):
                    pool.wait_ge(agg_out[k], nb * 64 + agg0)

            @block.vector
            def _(dve):
                dve.memset(sumT[K - 1][:, TILE - 1:TILE], 0.0).then_inc(tail_set, 1)
                dve.wait_ge(tail_set, 1)
                with dve.Fori(0, nb) as i:
                    def add(k):
                        dve.wait_ge(hs_in[k], i * 64 + (64 + hs0))
                        dve.wait_ge(tile_in[k], (i + 1) * 32)
                        dve.tensor_tensor(msg[k][:, :, :], hs[k][:, :, :], ea[k][:, :, :], ALU.add).then_inc(msg_made, 1)

                    def scan(k):
                        dve.wait_ge(msgT_made, i * K + k + 1)
                        dve.wait_ge(scanned, i * K + k)
                        dve.tensor_tensor_scan(sumT[k][:, :], keep[k][:, :], msgT[k][:, :],
                                               sumT[k - 1][:, TILE - 1:TILE], ALU.mult, ALU.add).then_inc(scanned, 1)

                    for k in range(K):
                        add(k)
                        if k:
                            scan(k - 1)
                    scan(K - 1)

            @block.tensor
            def _(pe):
                pe.wait_ge(ident_made, 1)
                with pe.Fori(0, nb) as i:
                    def turn(k):
                        pe.wait_ge(msg_made, i * K + k + 1)
                        if k >= 2:
                            pe.wait_ge(msgT_made, i * K + k - 1)
                        else:
                            pe.wait_ge(msgT_made, i * K)
                        for s in range(SUB):
                            last = pe.transpose(turned[k % 2][:, s * P:(s + 1) * P], msg[k][:, s, :], ident[:, :])
                        last.then_inc(msgT_psum, 1)

                    def turn_back(k):
                        pe.wait_ge(scanned, i * K + k + 1)
                        if k >= 2:
                            pe.wait_ge(rows_made, i * K + k - 1)
                        else:
                            pe.wait_ge(rows_made, i * K)
                        for s in range(SUB):
                            last = pe.transpose(back[k % 2][:, s * P:(s + 1) * P], sumT[k][:, s * P:(s + 1) * P], ident[:, :])
                        last.then_inc(back_psum, 1)

                    for k in range(K):
                        turn(k)
                        if k:
                            turn_back(k - 1)
                    turn_back(K - 1)

            @block.scalar
            def _(act):
                with act.Fori(0, nb) as i:
                    def copy_back(k):
                        act.wait_ge(back_psum, i * K + k + 1)
                        act.wait_ge(agg_out[k], i * 64 + agg0)
                        act.activation(rows[k][:, :], back[k % 2][:, :], ACT.Copy).then_inc(rows_made, 1)

                    for k in range(K):
                        act.wait_ge(msgT_psum, i * K + k + 1)
                        act.activation(msgT[k][:, :], turned[k % 2][:, :], ACT.Relu).then_inc(msgT_made, 1)
                        if k:
                            copy_back(k - 1)
                    copy_back(K - 1)


class Norm:

    def __init__(self, m, name):
        self.stats, self.mv = m.sbs(f"{name}_stats", [P, SUB, 6]), m.sbs(f"{name}_mv", [P, SUB, 2])
        self.std, self.rstd = m.sbs(f"{name}_std", [P, SUB]), m.sbs(f"{name}_rstd", [P, SUB])
        self.shift = m.sbs(f"{name}_shift", [P, SUB])
        self.stats_done, self.own, self.mv_done = (m.sem(f"{name}_{n}") for n in ("stats_done", "own", "mv_done"))
        self.std_done, self.rstd_done, self.shift_done = (m.sem(f"{name}_{n}") for n in ("std_done", "rstd_done", "shift_done"))

    def take_stats(self, dve, x, k):
        for a in range(SUB):
            last = dve.bn_stats(out=self.stats[k][:, a, :], in_=x[:, a, :])
        last.then_inc(self.stats_done, 1)

    def moments(self, dve, k, done):
        dve.wait_ge(self.stats_done, done)
        dve.sem_inc(self.own, 1)
        for a in range(SUB):
            last = dve.bn_aggr(out=self.mv[k][:, a, :], in_=self.stats[k][:, a, :])
        last.then_inc(self.mv_done, 1)

    def root(self, act, k, done, eps):
        act.wait_ge(self.mv_done, done)
        act.activation(self.std[k][:, :], self.mv[k][:, :, 1], ACT.Sqrt, bias=eps[:, :]).then_inc(self.std_done, 1)

    def scales(self, dve, k, done):
        dve.wait_ge(self.std_done, done)
        dve.reciprocal(self.rstd[k][:, :], self.std[k][:, :]).then_inc(self.rstd_done, 1)
        dve.wait_ge(self.rstd_done, done)
        dve.scalar_tensor_tensor(out=self.shift[k][:, :], in0=self.mv[k][:, :, 0], scalar=-1.0, in1=self.rstd[k][:, :],
                                 op0=ALU.mult, op1=ALU.mult).then_inc(self.shift_done, 1)

    def apply(self, act, out, x, k, func):
        for a in range(SUB):
            last = act.activation(out[:, a, :], x[:, a, :], func,
                                  bias=self.shift[k][:, a:a + 1], scale=self.rstd[k][:, a:a + 1])
        return last


def slot_tiles(slot):
    return (K + 1 - slot) // 2


def run_bodies(eng, nb, body):
    with eng.Fori(0, nb) as i:
        body(i)


def stream(sp, nb, load, store, free):
    for k in range(K):
        load(k, 0)
    if nb > 1:
        with sp.Fori(1, nb) as i:
            for k in range(K):
                free(k, i)
                store(k, i - 1)
                load(k, i)
    for k in range(K):
        free(k, nb)
        store(k, nb - 1)


def gine_mlp(nc, g):
    nb = g.NTN // K
    with Phase(nc, "gine_mlp_") as m:
        ident = m.sb("ident", [P, P])
        w1, w2, b1, b2 = m.sb("w1", [D, D]), m.sb("w2", [D, D]), m.sb("b1", [D, 1]), m.sb("b2", [D, 1])
        gamma, beta, eps = m.sb("gamma", [D, 1]), m.sb("beta", [D, 1]), m.sb("eps", [P, 1])
        h, agg, s = m.sbs("h", [P, SUB, D]), m.sbs("agg", [P, SUB, D]), m.sbs("s", [P, SUB, D])
        sT, hidT, yT = m.sbs("sT", [P, TILE]), m.sbs("hidT", [P, TILE]), m.sbs("yT", [P, TILE])
        y_stats, y_mv, y_std = m.sb("y_stats", [P, g.NTN, 6]), m.sb("y_mv", [P, 2]), m.sb("y_std", [P, 1])
        turned, hid, y = ([m.ps(f"{n}{j}", [P, TILE]) for j in range(2)] for n in ("turned", "hid", "y"))
        tile_in, y_out = m.sems("tile_in"), m.sems("y_out")
        cleared, ident_made, weights_in, eps_set = (m.sem(n) for n in ("cleared", "ident_made", "weights_in", "eps_set"))
        s_made, turned_done, sT_made, hid_done, hidT_made, y_done, yT_made, y_measured = (
            m.sem(n) for n in ("s_made", "turned_done", "sT_made", "hid_done", "hidT_made", "y_done", "yT_made", "y_measured"))
        idx, ids_in, last_out = m.sbs("idx", [P, 20], I32), g.gathered, g.scattered
        ids0, last0 = g.start(ids_in, g.NTE // K * 16), g.start(last_out, g.NTE // K * 64)
        pool_own = m.sem("pool_own")
        own, steps, y_root, mv_ready = m.sem("own"), m.sem("steps"), m.sem("y_root"), m.sem("mv_ready")
        with nc.Block() as block:
            @block.sync
            def _(sp):
                for dst, src in ((w1, g.w1T), (w2, g.w2T), (b1, g.b1), (b2, g.b2), (gamma, g.gamma), (beta, g.beta)):
                    sp.dma_start(dst[:, :], src).then_inc(weights_in, 16)

                def load(k, i):
                    sp.dma_start(h[k][:, :, :], node_rows(g.H, i * K + k)).then_inc(tile_in[k], 16)
                    sp.dma_start(agg[k][:, :, :], node_rows(g.AGG, i * K + k)).then_inc(tile_in[k], 16)

                def store(k, i):
                    sp.dma_start(g.YT[bass.ds(i * K + k, 1), :, :].rearrange("t p j -> (t p) j"), yT[k][:, :]).then_inc(y_out[k], 16)

                stream(sp, nb, load, store, lambda k, i: sp.wait_ge(yT_made, (i - 1) * K + k + 1))
                for k in range(K):
                    sp.wait_ge(y_out[k], 16 * nb)

            @block.gpsimd
            def _(pool):
                make_identity(pool, ident, ident_made, cleared)

                def body(i):
                    for k in range(K):
                        pool.wait_ge(last_out[k], i * 64 + last0)
                        pool.dma_start(idx[k][:, :], g.IDX[bass.ds(i * K + k, 1), :, :].rearrange("t p s -> (t p) s")).then_inc(ids_in[k], 16)
                    for k in range(K):
                        wait_alone(pool, ids_in[k], i * 16 + (16 + ids0), pool_own)
                        for s in range(SUB):
                            scatter_last(pool, g.LAST[:, :], idx[k][:, 8 + s:9 + s], idx[k][:, 16 + s:17 + s], g.NP - 1).then_inc(last_out[k], 16)

                run_bodies(pool, g.NTE // K, body)
                for k in range(K):
                    pool.wait_ge(last_out[k], g.NTE // K * 64 + last0)

            @block.vector
            def _(dve):
                dve.memset(eps[:, :], EPS).then_inc(eps_set, 1)

                def body(i):
                    def measure(k):
                        dve.wait_ge(yT_made, i * K + k + 1)
                        dve.bn_stats(out=y_stats[:, bass.ds(i * K + k, 1), :].rearrange("p t c -> p (t c)"), in_=yT[k][:, :]).then_inc(y_measured, 1)

                    for k in range(K):
                        dve.wait_ge(tile_in[k], (i + 1) * 32)
                        dve.tensor_tensor(s[k][:, :, :], h[k][:, :, :], agg[k][:, :, :], ALU.add).then_inc(s_made, 1)
                        if k >= 3:
                            measure(k - 3)
                    for k in range(K - 3, K):
                        measure(k)

                run_bodies(dve, nb, body)
                dve.wait_ge(y_measured, g.NTN)
                used = g.NTN
                for k in range(K):
                    t = g.NTN - K + k
                    real = min(max(g.N - t * TILE, 0), TILE) // SUB
                    if real == 0:
                        used = min(used, t)
                    elif real < P:
                        dve.bn_stats(out=y_stats[:, t, :], in_=yT[k][:, :].rearrange("p (a j) -> p a j", a=SUB)[:, :, 0:real]).then_inc(own, 1)
                        dve.wait_ge(own, 1)
                dve.bn_aggr(out=y_mv[:, :], in_=y_stats[:, 0:used, :].rearrange("p t c -> p (t c)")).then_inc(mv_ready, 1)
                dve.wait_ge(y_root, 1)
                dve.wait_ge(weights_in, 6 * 16)
                dve.reciprocal(y_std[:, :], y_std[:, :]).then_inc(steps, 1)
                dve.wait_ge(steps, 1)
                dve.tensor_tensor(g.bn_scale[:, :], y_std[:, :], gamma[:, :], ALU.mult).then_inc(steps, 1)
                dve.wait_ge(steps, 2)
                dve.tensor_tensor(g.bn_shift[:, :], y_mv[:, 0:1], g.bn_scale[:, :], ALU.mult).then_inc(steps, 1)
                dve.wait_ge(steps, 3)
                dve.tensor_tensor(g.bn_shift[:, :], beta[:, :], g.bn_shift[:, :], ALU.subtract)

            @block.tensor
            def _(pe):
                pe.wait_ge(ident_made, 1)
                pe.wait_ge(weights_in, 6 * 16)

                def body(i):
                    def turn(k):
                        pe.wait_ge(s_made, i * K + k + 1)
                        pe.wait_ge(sT_made, i * K + max(k - 1, 0))
                        for a in range(SUB):
                            last = pe.transpose(turned[k % 2][:, a * P:(a + 1) * P], s[k][:, a, :], ident[:, :])
                        last.then_inc(turned_done, 1)

                    def first(k):
                        pe.wait_ge(sT_made, i * K + k + 1)
                        pe.wait_ge(hidT_made, i * K + max(k - 1, 0))
                        pe.matmul(hid[k % 2][:, :], w1[:, :], sT[k][:, :], start=True, stop=True).then_inc(hid_done, 1)

                    def second(k):
                        pe.wait_ge(hidT_made, i * K + k + 1)
                        pe.wait_ge(yT_made, i * K + max(k - 1, 0))
                        pe.matmul(y[k % 2][:, :], w2[:, :], hidT[k][:, :], start=True, stop=True).then_inc(y_done, 1)

                    for k in range(K + 2):
                        if k < K:
                            turn(k)
                        if 1 <= k <= K:
                            first(k - 1)
                        if k >= 2:
                            second(k - 2)

                run_bodies(pe, nb, body)

            @block.scalar
            def _(act):
                act.wait_ge(weights_in, 6 * 16)

                def body(i):
                    for k in range(K + 2):
                        if k < K:
                            act.wait_ge(turned_done, i * K + k + 1)
                            act.activation(sT[k][:, :], turned[k % 2][:, :], ACT.Copy).then_inc(sT_made, 1)
                        if 1 <= k <= K:
                            act.wait_ge(hid_done, i * K + k)
                            act.activation(hidT[k - 1][:, :], hid[(k - 1) % 2][:, :], ACT.Relu, bias=b1[:, :]).then_inc(hidT_made, 1)
                        if k >= 2:
                            act.wait_ge(y_done, i * K + k - 1)
                            act.wait_ge(y_out[k - 2], i * 16)
                            act.wait_ge(y_measured, i * K)
                            act.activation(yT[k - 2][:, :], y[(k - 2) % 2][:, :], ACT.Identity, bias=b2[:, :]).then_inc(yT_made, 1)

                run_bodies(act, nb, body)
                act.wait_ge(eps_set, 1)
                act.wait_ge(mv_ready, 1)
                act.activation(y_std[:, :], y_mv[:, 1:2], ACT.Sqrt, bias=eps[:, :]).then_inc(y_root, 1)


def gine_finish(nc, g):
    nb = g.NTN // K
    with Phase(nc, "gine_finish_") as m:
        ident, eps = m.sb("ident", [P, P]), m.sb("eps", [P, 1])
        x, yT, bT = m.sbs("x", [P, SUB, D]), m.sbs("yT", [P, TILE]), m.sbs("bT", [P, TILE])
        x1, h1 = m.sbs("x1", [P, SUB, D]), m.sbs("h1", [P, SUB, D])
        rows = [m.ps(f"rows{j}", [P, SUB, D]) for j in range(3)]
        norm = Norm(m, "norm")
        tile_in, out = m.sems("tile_in"), m.sems("out")
        cleared, ident_made, eps_set = (m.sem(n) for n in ("cleared", "ident_made", "eps_set"))
        bT_made, rows_done, x1_made, h1_made = (m.sem(n) for n in ("bT_made", "rows_done", "x1_made", "h1_made"))
        with nc.Block() as block:
            @block.sync
            def _(sp):
                def load(k, i):
                    sp.dma_start(x[k][:, :, :], node_rows(g.x, i * K + k)).then_inc(tile_in[k], 16)
                    sp.dma_start(yT[k][:, :], g.YT[bass.ds(i * K + k, 1), :, :].rearrange("t p j -> (t p) j")).then_inc(tile_in[k], 16)

                def store(k, i):
                    sp.dma_start(node_rows(g.X, i * K + k), x1[k][:, :, :]).then_inc(out[k], 16)
                    sp.dma_start(node_rows(g.H, i * K + k), h1[k][:, :, :]).then_inc(out[k], 16)

                stream(sp, nb, load, store, lambda k, i: sp.wait_ge(h1_made, (i - 1) * K + k + 1))
                for k in range(K):
                    sp.wait_ge(out[k], 32 * nb)

            @block.gpsimd
            def _(pool):
                make_identity(pool, ident, ident_made, cleared)

            @block.tensor
            def _(pe):
                pe.wait_ge(ident_made, 1)

                def body(i):
                    for k in range(K):
                        pe.wait_ge(bT_made, i * K + k + 1)
                        pe.wait_ge(x1_made, i * K + max(k - 2, 0))
                        for a in range(SUB):
                            last = pe.transpose(rows[k % 3][:, a, :], bT[k][:, a * P:(a + 1) * P], ident[:, :])
                        last.then_inc(rows_done, 1)

                run_bodies(pe, nb, body)

            @block.vector
            def _(dve):
                dve.memset(eps[:, :], EPS).then_inc(eps_set, 1)

                def body(i):
                    for k in range(K + 2):
                        if k < K:
                            dve.wait_ge(rows_done, i * K + k + 1)
                            dve.wait_ge(out[k], i * 32)
                            dve.tensor_tensor(x1[k][:, :, :], rows[k % 3][:, :, :], x[k][:, :, :], ALU.add).then_inc(x1_made, 1)
                        if 1 <= k <= K:
                            norm.moments(dve, k - 1, i * K + k)
                        if k >= 2:
                            norm.scales(dve, k - 2, i * K + k - 1)
                        if k < K:
                            dve.wait_ge(x1_made, i * K + k + 1)
                            norm.take_stats(dve, x1[k], k)

                run_bodies(dve, nb, body)

            @block.scalar
            def _(act):
                act.wait_ge(eps_set, 1)

                def body(i):
                    for k in range(K + 3):
                        if k < K:
                            act.wait_ge(tile_in[k], (i + 1) * 32)
                            act.activation(bT[k][:, :], yT[k][:, :], ACT.Identity, bias=g.bn_shift[:, :], scale=g.bn_scale[:, :]).then_inc(bT_made, 1)
                        if 1 <= k <= K:
                            norm.root(act, k - 1, i * K + k, eps)
                        if k >= 3:
                            act.wait_ge(norm.shift_done, i * K + k - 2)
                            act.wait_ge(out[k - 3], i * 32)
                            norm.apply(act, h1[k - 3], x1[k - 3], k - 3, ACT.Relu).then_inc(h1_made, 1)

                run_bodies(act, nb, body)


def conv_logits(nc, g, layer):
    nb = g.NTE // K
    with Phase(nc, f"conv_logits{layer}_") as m:
        ident, wr, att = m.sb("ident", [P, P]), m.sb("wr", [D, H * D]), m.sb("att", [D, H, 32])
        idx = m.sbs("idx", [P, 20], I32)
        hs, hd, hdT = m.sbs("hs", [P, SUB, D]), m.sbs("hd", [P, SUB, D]), m.sbs("hdT", [P, TILE], n=2)
        sloped, leaky = m.sbs("sloped", [P, TILE], n=2 * H), m.sbs("leaky", [P, TILE], n=2 * H)
        logit = [m.sbs(f"logit{j}_", [P, TILE], n=2) for j in range(2)]
        hsT_ps, hdT_ps = m.ps("hsT_ps", [P, TILE]), m.ps("hdT_ps", [P, TILE])
        z = [m.ps(f"z{h}", [P, TILE]) for h in range(H)]
        dots = [m.ps(f"dots{j}", [P, TILE]) for j in range(2)]
        idx_in, rows_in, own = m.sems("idx_in"), g.gathered, m.sem("own")
        rows0 = g.start(rows_in, nb * 128)
        logit_out = [m.sems(f"logit_out{j}_", 2) for j in range(2)]
        cleared, ident_made, weights_in, att_set, weights_made = (
            m.sem(n) for n in ("cleared", "ident_made", "weights_in", "att_set", "weights_made"))
        turned_done, hdT_made, diff_made, mean_step = (m.sem(n) for n in ("turned_done", "hdT_made", "diff_made", "mean_step"))
        z_done, sloped_made = ([m.sem(f"{n}{j}") for j in range(2)] for n in ("z_done", "sloped_made"))
        leaky_made, dots_done, logit_made = ([m.sem(f"{n}{j}") for j in range(2)] for n in ("leaky_made", "dots_done", "logit_made"))
        with nc.Block() as block:
            @block.sync
            def _(sp):
                wl_in, wr_in, att_in = g.conv_weights[layer]
                sp.dma_start(g.wl[:, :], wl_in).then_inc(weights_in, 16)
                sp.dma_start(wr[:, :], wr_in).then_inc(weights_in, 16)
                sp.wait_ge(att_set, 1)
                with nc.allow_non_contiguous_dma("a column of each head"):
                    sp.dma_start(att[:, :, 0:1], att_in.rearrange("d (h o) -> d h o", o=1)).then_inc(weights_in, 16)

                def load(k, i):
                    sp.dma_start(idx[k][:, :], g.IDX[bass.ds(i * K + k, 1), :, :].rearrange("t p s -> (t p) s")).then_inc(idx_in[k], 16)

                def store(j, k, i, slot):
                    sp.wait_ge(logit_made[j], i * K + k + 1)
                    sp.dma_start(g.LOGIT[j][:, bass.ds((i * K + k) * TILE, TILE)], logit[j][slot][0:P:32, :]).then_inc(logit_out[j][slot], 16)

                def body(i, more):
                    for k in range(K):
                        store(0, k, i, k % 2)
                        store(1, k, i, k % 2)
                        if more:
                            load(k, i + 1)

                for k in range(K):
                    load(k, 0)
                if nb > 1:
                    with sp.Fori(0, nb - 1) as i:
                        body(i, True)
                body(nb - 1, False)
                for j in range(2):
                    for slot in range(2):
                        sp.wait_ge(logit_out[j][slot], 16 * nb * slot_tiles(slot))

            @block.gpsimd
            def _(pool):
                make_identity(pool, ident, ident_made, cleared)

                def gather_tile(k, i):
                    wait_alone(pool, idx_in[k], (i + 1) * 16, own)
                    for s in range(SUB):
                        gather(pool, hd[k][:, s, :], g.H[:, :], idx[k][:, 4 + s:5 + s]).then_inc(rows_in[k], 16)
                        gather(pool, hs[k][:, s, :], g.H[:, :], idx[k][:, s:s + 1]).then_inc(rows_in[k], 16)

                for k in range(K):
                    gather_tile(k, 0)
                if nb > 1:
                    with pool.Fori(1, nb) as i:
                        for k in range(K):
                            pool.wait_ge(turned_done, (i - 1) * K + k + 1)
                            gather_tile(k, i)

            @block.tensor
            def _(pe):
                pe.wait_ge(ident_made, 1)
                pe.wait_ge(weights_made, 1)

                def body(i):
                    n = i * K

                    def turn(k):
                        pe.wait_ge(rows_in[k], i * 128 + (128 + rows0))
                        pe.wait_ge(diff_made, n + k)
                        for s in range(SUB):
                            pe.transpose(hdT_ps[:, s * P:(s + 1) * P], hd[k][:, s, :], ident[:, :])
                        for s in range(SUB):
                            last = pe.transpose(hsT_ps[:, s * P:(s + 1) * P], hs[k][:, s, :], ident[:, :])
                        last.then_inc(turned_done, 1)

                    def dot(j, k):
                        pe.wait_ge(leaky_made[j], H * n + H * (k + 1))
                        pe.wait_ge(logit_made[j], n + k)
                        for h in range(H):
                            last = pe.matmul(dots[j][32 * h:32 * h + 32, :], att[:, h, :], leaky[H * j + h][:, :],
                                             start=True, stop=True, tile_position=(0, 32 * h))
                        last.then_inc(dots_done[j], 1)

                    turn(0)
                    for k in range(K):
                        pe.wait_ge(hdT_made, n + k + 1)
                        pe.wait_ge(leaky_made[1], H * n + H * k)
                        for h in range(H):
                            pe.matmul(z[h][:, :], g.wsum[:, h * D:(h + 1) * D], hdT[k % 2][:, :],
                                      start=True, stop=True).then_inc(z_done[0], 1)
                        if k:
                            dot(1, k - 1)
                        if k + 1 < K:
                            turn(k + 1)
                        pe.wait_ge(diff_made, n + k + 1)
                        for h in range(H):
                            pe.wait_ge(leaky_made[0], H * n + H * k + h + 1)
                            pe.matmul(z[h][:, :], g.wl[:, h * D:(h + 1) * D], g.diffT[:, bass.ds((n + k) * TILE, TILE)],
                                      start=False, stop=True, skip_group_check=True).then_inc(z_done[1], 1)
                        dot(0, k)
                    dot(1, K - 1)

                run_bodies(pe, nb, body)

            @block.scalar
            def _(act):
                def body(i):
                    n = i * K

                    def copy_dst(k):
                        act.wait_ge(turned_done, n + k + 1)
                        act.activation(hdT[k % 2][:, :], hdT_ps[:, :], ACT.Copy).then_inc(hdT_made, 1)

                    def slope(j, k):
                        for h in range(H):
                            act.wait_ge(z_done[j], H * n + H * k + h + 1)
                            act.activation(sloped[H * j + h][:, :], z[h][:, :], ACT.Copy, scale=SLOPE).then_inc(sloped_made[j], 1)

                    def copy_dots(j, k):
                        act.wait_ge(dots_done[j], n + k + 1)
                        slot = k % 2
                        act.wait_ge(logit_out[j][slot], i * (16 * slot_tiles(slot)) + 16 * (k // 2))
                        act.activation(logit[j][slot][:, :], dots[j][:, :], ACT.Copy).then_inc(logit_made[j], 1)

                    copy_dst(0)
                    for k in range(K):
                        slope(0, k)
                        if k:
                            copy_dots(1, k - 1)
                        if k + 1 < K:
                            copy_dst(k + 1)
                        slope(1, k)
                        copy_dots(0, k)
                    copy_dots(1, K - 1)

                run_bodies(act, nb, body)

            @block.vector
            def _(dve):
                dve.memset(att[:, :, :], 0.0).then_inc(att_set, 1)
                dve.wait_ge(weights_in, 48)
                dve.tensor_tensor(g.wmean[:, :], g.wl[:, 0:D], g.wl[:, D:2 * D], ALU.add).then_inc(mean_step, 1)
                for h in range(2, H):
                    dve.wait_ge(mean_step, h - 1)
                    dve.tensor_tensor(g.wmean[:, :], g.wmean[:, :], g.wl[:, h * D:(h + 1) * D], ALU.add).then_inc(mean_step, 1)
                dve.wait_ge(mean_step, H - 1)
                dve.tensor_scalar(g.wmean[:, :], g.wmean[:, :], 1.0 / H, None, ALU.mult)
                dve.tensor_tensor(g.wsum[:, :], g.wl[:, :], wr[:, :], ALU.add).then_inc(weights_made, 1)

                def body(i):
                    n = i * K

                    def diff(k):
                        dve.wait_ge(hdT_made, n + k + 1)
                        dve.tensor_tensor(g.diffT[:, bass.ds((n + k) * TILE, TILE)], hsT_ps[:, :], hdT[k % 2][:, :],
                                          ALU.subtract).then_inc(diff_made, 1)

                    def leak(j, k):
                        for h in range(H):
                            dve.wait_ge(sloped_made[j], H * n + H * k + h + 1)
                            if h == 0:
                                dve.wait_ge(dots_done[j], n + k)
                            dve.tensor_tensor(leaky[H * j + h][:, :], z[h][:, :], sloped[H * j + h][:, :],
                                              ALU.max).then_inc(leaky_made[j], 1)

                    diff(0)
                    for k in range(K):
                        leak(0, k)
                        if k + 1 < K:
                            diff(k + 1)
                        leak(1, k)

                run_bodies(dve, nb, body)


def edge_softmax(nc, g, layer, self_loops, share):
    J = g.EP // CH
    with Phase(nc, f"edge_softmax{layer}_") as m:
        ident, zero = m.sb("ident", [P, P]), m.sb("zero", [P, J])
        e, es, ex, exs, top, run, total, weight = (m.sb(n, [P, J]) for n in ("e", "es", "ex", "exs", "top", "run", "total", "weight"))
        keep = [m.sb(f"keep{b}", [P, J]) for b in range(2)]
        cut = [m.sb(f"cut{b}", [P, J]) for b in range(2)]
        lead = [m.sb(f"lead{b}", [P, J]) for b in range(2)]
        leadcut = [m.sb(f"leadcut{b}", [P, J]) for b in range(2)]
        whole, wholecut = m.sb("whole", [1, 2, P]), m.sb("wholecut", [1, 2, P])
        ends, carry = m.sb("ends", [1, P + 2]), m.sb("carry", [P, 1])
        row, col = m.ps("row", [1, P]), m.ps("col", [P, 1])
        loaded, cleared, ident_made, steps, turn_done, diff_done, exp_done, asked, alpha_made, alpha_out = (
            m.sem(n) for n in ("loaded", "cleared", "ident_made", "steps", "turn_done", "diff_done", "exp_done", "asked", "alpha_made", "alpha_out"))
        n_loads = 8 + 1 + self_loops
        flat = lambda table: table.rearrange("h (c j) -> (h c) j", j=J)
        end = lambda b: 0 if b else J - 1
        with nc.Block() as block:
            @block.sync
            def _(sp):
                for b, table in enumerate((g.KEEP, g.KEEPN)):
                    for h in range(H):
                        sp.dma_start(keep[b][CH * h:CH * (h + 1), :], table.rearrange("o (c j) -> (o c) j", j=J)).then_inc(loaded, 16)
                sp.dma_start(e[:, :], flat(g.LOGIT[1])).then_inc(loaded, 16)
                if self_loops:
                    sp.dma_start(es[:, :], flat(g.LOGIT[0])).then_inc(loaded, 16)
                sp.wait_ge(alpha_made, 1)
                sp.dma_start(flat(g.ALPHA), weight[:, :]).then_inc(alpha_out, 16)
                sp.wait_ge(alpha_out, 16)

            @block.gpsimd
            def _(pool):
                make_identity(pool, ident, ident_made, cleared)

            @block.vector
            def _(dve):
                count, turned = [0], [0]

                def step(instruction):
                    count[0] += 1
                    instruction.then_inc(steps, 1)
                    dve.wait_ge(steps, count[0])

                def turn():
                    dve.sem_inc(asked, 1)
                    turned[0] += 1
                    dve.wait_ge(turn_done, turned[0])

                order = lambda x, b: x[:, ::-1] if b else x[:, :]
                def join(b, local, op_carry, op_in, out):
                    turn()
                    inner = ends[:, 1:P + 1]
                    data0 = wholecut[:, b, :] if op_carry == ALU.add else whole[:, b, :]
                    step(dve.tensor_tensor_scan(inner[:, ::-1] if b else inner, data0[:, ::-1] if b else data0,
                                                row[:, ::-1] if b else row[:, :], -BIG if op_carry == ALU.add else 0.0, op_carry, op_in))
                    turn()
                    step(dve.tensor_copy(carry[:, :], col[:, :]))
                    step(dve.scalar_tensor_tensor(out=out[:, :], in0=(leadcut if op_carry == ALU.add else lead)[b][:, :], scalar=carry[:, :],
                                                  in1=local[:, :], op0=op_carry, op1=op_in))

                step(dve.memset(zero[:, :], 0.0))
                step(dve.memset(ends[:, :], 0.0))
                dve.wait_ge(loaded, 16 * n_loads)
                for b in range(2):
                    dve.tensor_scalar(cut[b][:, :], keep[b][:, :], -1.0, BIG, ALU.add, ALU.mult)
                    step(dve.tensor_tensor_scan(order(lead[b], b), order(keep[b], b), zero[:, :], 1.0, ALU.mult, ALU.add))
                    dve.tensor_scalar(leadcut[b][:, :], lead[b][:, :], -1.0, BIG, ALU.add, ALU.mult)
                    turn()
                    step(dve.tensor_copy(whole[:, b, :], row[:, :]))
                    step(dve.tensor_scalar(wholecut[:, b, :], whole[:, b, :], -1.0, BIG, ALU.add, ALU.mult))
                if self_loops:
                    step(dve.tensor_tensor(top[:, :], e[:, :], es[:, :], ALU.max))
                    most = top
                else:
                    most = e
                step(dve.tensor_tensor_scan(run[:, :], cut[0][:, :], most[:, :], -BIG, ALU.add, ALU.max))
                join(0, run, ALU.add, ALU.max, total)
                step(dve.tensor_tensor_scan(order(run, 1), order(cut[1], 1), order(total, 1), -BIG, ALU.add, ALU.max))
                join(1, run, ALU.add, ALU.max, top)
                if self_loops:
                    dve.tensor_tensor(es[:, :], es[:, :], top[:, :], ALU.subtract)
                dve.tensor_tensor(e[:, :], e[:, :], top[:, :], ALU.subtract).then_inc(diff_done, 1)
                dve.wait_ge(exp_done, 1 + self_loops)
                step(dve.tensor_tensor_scan(run[:, :], keep[0][:, :], ex[:, :], 0.0, ALU.mult, ALU.add))
                join(0, run, ALU.mult, ALU.add, total)
                step(dve.scalar_tensor_tensor(out=total[:, :], in0=keep[1][:, :], scalar=-1.0, in1=total[:, :],
                                              op0=ALU.add, op1=ALU.mult))
                step(dve.tensor_tensor_scan(order(run, 1), order(keep[1], 1), order(total, 1), 0.0, ALU.mult, ALU.add))
                join(1, run, ALU.mult, ALU.add, total)
                if self_loops:
                    step(dve.tensor_tensor(total[:, :], exs[:, :], total[:, :], ALU.subtract))
                else:
                    step(dve.tensor_scalar(total[:, :], total[:, :], -1.0, None, ALU.mult))
                step(dve.reciprocal(total[:, :], total[:, :]))
                dve.scalar_tensor_tensor(out=weight[:, :], in0=ex[:, :], scalar=share, in1=total[:, :],
                                         op0=ALU.mult, op1=ALU.mult).then_inc(alpha_made, 1)

            @block.scalar
            def _(act):
                act.wait_ge(diff_done, 1)
                act.activation(ex[:, :], e[:, :], ACT.Exp).then_inc(exp_done, 1)
                if self_loops:
                    act.activation(exs[:, :], es[:, :], ACT.Exp).then_inc(exp_done, 1)

            @block.tensor
            def _(pe):
                pe.wait_ge(ident_made, 1)
                count = [0]

                def column(source, b):
                    count[0] += 1
                    pe.wait_ge(asked, count[0])
                    pe.matmul(row[:, :], source[:, end(b):end(b) + 1], ident[:, :], start=True, stop=True).then_inc(turn_done, 1)

                def carries(b):
                    count[0] += 1
                    pe.wait_ge(asked, count[0])
                    pe.matmul(col[:, :], ends[:, 2 * b:2 * b + P], ident[0:1, 0:1], start=True, stop=True).then_inc(turn_done, 1)

                for b in range(2):
                    column(lead[b], b)
                for _ in ("maximum", "sum"):
                    for b in range(2):
                        column(run, b)
                        carries(b)


def conv_aggregate(nc, g, layer):
    nb = g.NTE // K
    with Phase(nc, f"conv_aggregate{layer}_") as m:
        ident = m.sb("ident", [P, P])
        idx = m.sbs("idx", [P, 20], I32)
        alphaT, keep = m.sbs("alphaT", [H, TILE]), m.sbs("keep", [P, TILE])
        alpha, diff = m.sbs("alpha", [P, SUB * H], n=2), m.sbs("diff", [P, TILE], n=2)
        part, sumT, rows = m.sbs("part", [P, SUB, D], n=2), m.sbs("sumT", [P, TILE], n=2), m.sbs("rows", [P, TILE])
        y = [m.ps(f"y{s}", [P, H * D]) for s in range(SUB)]
        alpha_ps, partT, back = m.ps("alpha_ps", [P, SUB * H]), m.ps("partT", [P, TILE]), m.ps("back", [P, TILE])
        tile_in, agg_out, own = m.sems("tile_in"), g.scattered, m.sem("own")
        agg0 = g.start(agg_out, nb * 64)
        cleared, ident_made, tail_set = (m.sem(n) for n in ("cleared", "ident_made", "tail_set"))
        alpha_turned, alpha_made, diff_copied, y_done, part_step, part_made = (
            m.sem(n) for n in ("alpha_turned", "alpha_made", "diff_copied", "y_done", "part_step", "part_made"))
        partT_done, scanned, back_done, rows_made = (m.sem(n) for n in ("partT_done", "scanned", "back_done", "rows_made"))
        with nc.Block() as block:
            @block.sync
            def _(sp):
                def load(k, i):
                    n = i * K + k
                    sp.dma_start(idx[k][:, :], g.IDX[bass.ds(n, 1), :, :].rearrange("t p s -> (t p) s")).then_inc(tile_in[k], 16)
                    sp.dma_start(alphaT[k][:, :], g.ALPHA[:, bass.ds(n * TILE, TILE)]).then_inc(tile_in[k], 16)
                    sp.dma_start(keep[k][:, :], edge_span(g.KEEP, n, P)).then_inc(tile_in[k], 16)

                for k in range(K):
                    load(k, 0)
                if nb > 1:
                    with sp.Fori(1, nb) as i:
                        for k in range(K):
                            sp.wait_ge(agg_out[k], i * 64 + agg0)
                            load(k, i)

            @block.gpsimd
            def _(pool):
                make_identity(pool, ident, ident_made, cleared)

                def body(i):
                    for k in range(K):
                        wait_alone(pool, rows_made, i * K + k + 1, own)
                        for s in range(SUB):
                            scatter_last(pool, g.AGG[:, :], idx[k][:, 8 + s:9 + s], rows[k][:, s * P:(s + 1) * P],
                                         g.NP - 1).then_inc(agg_out[k], 16)

                run_bodies(pool, nb, body)
                for k in range(K):
                    pool.wait_ge(agg_out[k], nb * 64 + agg0)

            @block.tensor
            def _(pe):
                pe.wait_ge(ident_made, 1)

                def body(i):
                    n = i * K

                    def turn_alpha(k):
                        pe.wait_ge(tile_in[k], (i + 1) * 48)
                        pe.wait_ge(alpha_made, n + k)
                        for s in range(SUB):
                            last = pe.matmul(alpha_ps[:, s * H:(s + 1) * H], alphaT[k][:, s * P:(s + 1) * P], ident[0:H, 0:H],
                                             start=True, stop=True)
                        last.then_inc(alpha_turned, 1)

                    def project(k):
                        pe.wait_ge(diff_copied, n + k + 1)
                        pe.wait_ge(part_made, n + k)
                        for s in range(SUB):
                            last = pe.matmul(y[s][:, :], diff[k % 2][:, s * P:(s + 1) * P], g.wl[:, :], start=True, stop=True)
                            last.then_inc(y_done, 1)

                    def turn(k):
                        pe.wait_ge(part_made, n + k + 1)
                        pe.wait_ge(scanned, n + k)
                        for s in range(SUB):
                            last = pe.transpose(partT[:, s * P:(s + 1) * P], part[k % 2][:, s, :], ident[:, :])
                        last.then_inc(partT_done, 1)

                    def turn_back(k):
                        pe.wait_ge(scanned, n + k + 1)
                        pe.wait_ge(rows_made, n + k)
                        for s in range(SUB):
                            last = pe.transpose(back[:, s * P:(s + 1) * P], sumT[k % 2][:, s * P:(s + 1) * P], ident[:, :])
                        last.then_inc(back_done, 1)

                    turn_alpha(0)
                    for k in range(K + 2):
                        if k < K:
                            project(k)
                        if k + 1 < K:
                            turn_alpha(k + 1)
                        if 1 <= k <= K:
                            turn(k - 1)
                        if k >= 2:
                            turn_back(k - 2)

                run_bodies(pe, nb, body)

            @block.scalar
            def _(act):
                def body(i):
                    n = i * K

                    def copy_alpha(k):
                        act.wait_ge(alpha_turned, n + k + 1)
                        act.wait_ge(part_made, n + max(k - 1, 0))
                        if k == 0:
                            act.wait_ge(part_made, n)
                        act.activation(alpha[k % 2][:, :], alpha_ps[:, :], ACT.Copy).then_inc(alpha_made, 1)

                    def copy_diff(k):
                        act.wait_ge(y_done, SUB * n + SUB * max(k - 1, 0))
                        act.activation(diff[k % 2][:, :], g.diffT[:, bass.ds((n + k) * TILE, TILE)], ACT.Copy).then_inc(diff_copied, 1)

                    copy_diff(0)
                    copy_alpha(0)
                    for k in range(K + 2):
                        if k + 1 < K:
                            copy_diff(k + 1)
                            copy_alpha(k + 1)
                        if k >= 2:
                            act.wait_ge(back_done, n + k - 1)
                            act.wait_ge(agg_out[k - 2], i * 64 + agg0)
                            act.activation(rows[k - 2][:, :], back[:, :], ACT.Copy).then_inc(rows_made, 1)

                run_bodies(act, nb, body)

            @block.vector
            def _(dve):
                for j in range(2):
                    dve.memset(sumT[j][:, TILE - 1:TILE], 0.0).then_inc(tail_set, 1)
                dve.wait_ge(tail_set, 2)

                def body(i):
                    n = i * K

                    def weigh(k):
                        dve.wait_ge(alpha_made, n + k + 1)
                        dve.wait_ge(partT_done, n + max(k - 1, 0))
                        for h in range(H):
                            if h:
                                dve.wait_ge(part_step, (H - 1) * n + (H - 1) * k + h)
                            for s in range(SUB):
                                if h == 0:
                                    dve.wait_ge(y_done, SUB * n + SUB * k + s + 1)
                                a = alpha[k % 2][:, s * H + h:s * H + h + 1]
                                yh, out = y[s][:, h * D:(h + 1) * D], part[k % 2][:, s, :]
                                if h == 0:
                                    last = dve.tensor_scalar(out, yh, a, None, ALU.mult)
                                else:
                                    last = dve.scalar_tensor_tensor(out=out, in0=yh, scalar=a, in1=out, op0=ALU.mult, op1=ALU.add)
                            last.then_inc(part_made if h == H - 1 else part_step, 1)

                    def scan(k):
                        dve.wait_ge(partT_done, n + k + 1)
                        dve.wait_ge(scanned, n + k)
                        dve.wait_ge(back_done, n + max(k - 1, 0))
                        before = sumT[(k - 1) % 2 if k else (K - 1) % 2]
                        dve.tensor_tensor_scan(sumT[k % 2][:, :], keep[k][:, :], partT[:, :], before[:, TILE - 1:TILE],
                                               ALU.mult, ALU.add).then_inc(scanned, 1)

                    for k in range(K + 1):
                        if k < K:
                            weigh(k)
                        if k:
                            scan(k - 1)

                run_bodies(dve, nb, body)


def broadcast_rows(sp, dst, src, done):
    sp.dma_start(dst, src.to_broadcast([P, dst.shape[1]])).then_inc(done, 16)


def conv_nodes(nc, g, layer, final):
    nb = g.NTN // K
    bias_in, gamma_in, beta_in = g.conv_norms[layer]
    with Phase(nc, f"conv_nodes{layer}_") as m:
        ident, eps, ones = m.sb("ident", [P, P]), m.sb("eps", [P, 1]), m.sb("ones", [1, P])
        gamma, beta, bias = m.sb("gamma", [P, TILE]), m.sb("beta", [P, TILE]), m.sb("bias", [1, TILE])
        h, agg = m.sbs("h", [P, SUB, D]), m.sbs("agg", [P, SUB, D])
        x = m.sbs("x", [P, SUB, D]) if final else None
        hT = m.sbs("hT", [P, TILE], n=2)
        base, o, scaled, res = (m.sbs(n, [P, SUB, D], n=K) for n in ("base", "o", "scaled", "res"))
        h_out = m.sbs("h_out", [P, SUB, D]) if final else res
        turned = [m.ps(f"turned{j}", [P, TILE]) for j in range(2)]
        o_ps = [m.ps(f"o_ps{j}", [P, SUB, D]) for j in range(3)]
        norm = Norm(m, "norm")
        last_norm = Norm(m, "last_norm") if final else None
        tile_in, out = m.sems("tile_in"), m.sems("out")
        cleared, ident_made, set_once, weights_in = (m.sem(n) for n in ("cleared", "ident_made", "set_once", "weights_in"))
        turned_done, hT_made, o_done, o_made, base_made, half_base = (
            m.sem(n) for n in ("turned_done", "hT_made", "o_done", "o_made", "base_made", "half_base"))
        normed, scaled_made, sum_made, all_made = (m.sem(n) for n in ("normed", "scaled_made", "sum_made", "all_made"))
        own = m.sem("own")
        n_in = 48 if final else 32
        lag = 5 if final else 3
        with nc.Block() as block:
            @block.sync
            def _(sp):
                for a in range(SUB):
                    broadcast_rows(sp, gamma[:, a * D:(a + 1) * D], gamma_in, weights_in)
                    broadcast_rows(sp, beta[:, a * D:(a + 1) * D], beta_in, weights_in)
                    sp.dma_start(bias[:, a * D:(a + 1) * D], bias_in).then_inc(weights_in, 16)

                def load(k, i):
                    sp.dma_start(h[k][:, :, :], node_rows(g.H, i * K + k)).then_inc(tile_in[k], 16)
                    sp.dma_start(agg[k][:, :, :], node_rows(g.AGG, i * K + k)).then_inc(tile_in[k], 16)
                    if final:
                        sp.dma_start(x[k][:, :, :], node_rows(g.X, i * K + k)).then_inc(tile_in[k], 16)

                def store(k, i):
                    sp.dma_start(node_rows(g.H, i * K + k), h_out[k][:, :, :]).then_inc(out[k], 16)
                    if final:
                        sp.dma_start(node_rows(g.X, i * K + k), res[k][:, :, :]).then_inc(out[k], 16)

                stream(sp, nb, load, store, lambda k, i: sp.wait_ge(all_made, (i - 1) * K + k + 1))
                for k in range(K):
                    sp.wait_ge(out[k], (32 if final else 16) * nb)

            @block.gpsimd
            def _(pool):
                make_identity(pool, ident, ident_made, cleared)
                pool.wait_ge(weights_in, 16 * 12)

                def body(i):
                    for k in range(K):
                        wait_alone(pool, tile_in[k], (i + 1) * n_in, own)
                        flat = lambda t: t[:, :, :].rearrange("p a d -> p (a d)")
                        first = pool.tensor_tensor(flat(base[k]), flat(h[k]), beta[:, :], ALU.add)
                        if final:
                            first.then_inc(half_base, 1)
                            pool.wait_ge(half_base, i * K + k + 1)
                            pool.tensor_tensor(flat(base[k]), flat(base[k]), flat(x[k]), ALU.add).then_inc(base_made, 1)
                        else:
                            first.then_inc(base_made, 1)

                run_bodies(pool, nb, body)

            @block.tensor
            def _(pe):
                pe.wait_ge(ident_made, 1)
                pe.wait_ge(set_once, 2)
                pe.wait_ge(weights_in, 16 * 12)

                def body(i):
                    n = i * K
                    for k in range(K + 1):
                        if k < K:
                            pe.wait_ge(tile_in[k], (i + 1) * n_in)
                            pe.wait_ge(hT_made, n + max(k - 1, 0))
                            for a in range(SUB):
                                last = pe.transpose(turned[k % 2][:, a * P:(a + 1) * P], h[k][:, a, :], ident[:, :])
                            last.then_inc(turned_done, 1)
                        if k:
                            j = k - 1
                            pe.wait_ge(o_made, n + max(j - 2, 0))
                            whole = o_ps[j % 3][:, :, :].rearrange("p a d -> p (a d)")
                            pe.matmul(whole, ones[:, :], bias[:, :], start=True, stop=True)
                            pe.wait_ge(hT_made, n + j + 1)
                            for a in range(SUB):
                                last = pe.matmul(o_ps[j % 3][:, a, :], hT[j % 2][:, a * P:(a + 1) * P], g.wmean[:, :],
                                                 start=False, stop=True, skip_group_check=True)
                            last.then_inc(o_done, 1)

                run_bodies(pe, nb, body)

            @block.vector
            def _(dve):
                dve.memset(eps[:, :], EPS).then_inc(set_once, 1)
                dve.memset(ones[:, :], 1.0).then_inc(set_once, 1)
                dve.wait_ge(weights_in, 16 * 12)

                def body(i):
                    n = i * K

                    def start(k):
                        dve.wait_ge(o_done, n + k + 1)
                        dve.tensor_tensor(o[k][:, :, :], o_ps[k % 3][:, :, :], agg[k][:, :, :], ALU.add).then_inc(o_made, 1)

                    def finish(k):
                        flat = lambda t: t[:, :, :].rearrange("p a d -> p (a d)")
                        dve.wait_ge(normed, n + k + 1)
                        dve.tensor_tensor(flat(o[k]), flat(scaled[k]), gamma[:, :], ALU.mult).then_inc(scaled_made, 1)
                        dve.wait_ge(base_made, n + k + 1)
                        dve.wait_ge(scaled_made, n + k + 1)
                        if final:
                            dve.wait_ge(out[k], i * 32)
                        dve.tensor_tensor(flat(res[k]) if final else flat(scaled[k]), flat(o[k]), flat(base[k]), ALU.add).then_inc(sum_made, 1)

                    for k in range(K + lag):
                        if k < K:
                            start(k)
                        if 1 <= k <= K:
                            norm.moments(dve, k - 1, n + k)
                        if k < K:
                            dve.wait_ge(o_made, n + k + 1)
                            norm.take_stats(dve, o[k], k)
                        if 2 <= k < K + 2:
                            norm.scales(dve, k - 2, n + k - 1)
                        if 3 <= k < K + 3:
                            finish(k - 3)
                        if final and 4 <= k < K + 4:
                            dve.wait_ge(sum_made, n + k - 3)
                            last_norm.take_stats(dve, res[k - 4], k - 4)
                            last_norm.moments(dve, k - 4, n + k - 3)
                        if final and 5 <= k:
                            last_norm.scales(dve, k - 5, n + k - 4)

                run_bodies(dve, nb, body)

            @block.scalar
            def _(act):
                act.wait_ge(set_once, 2)

                def body(i):
                    n = i * K
                    for k in range(K + lag + 1):
                        if k < K:
                            act.wait_ge(turned_done, n + k + 1)
                            act.wait_ge(o_done, n + max(k - 1, 0))
                            act.activation(hT[k % 2][:, :], turned[k % 2][:, :], ACT.Copy).then_inc(hT_made, 1)
                        if 1 <= k <= K:
                            norm.root(act, k - 1, n + k, eps)
                        if 2 <= k < K + 2:
                            act.wait_ge(norm.shift_done, n + k - 1)
                            if not final:
                                act.wait_ge(all_made, n)
                            norm.apply(act, scaled[k - 2], o[k - 2], k - 2, ACT.Identity).then_inc(normed, 1)
                        if not final and 4 <= k:
                            act.wait_ge(sum_made, n + k - 3)
                            act.wait_ge(out[k - 4], i * 16)
                            act.activation(res[k - 4][:, :, :], scaled[k - 4][:, :, :], ACT.Relu).then_inc(all_made, 1)
                        if final and 4 <= k < K + 4:
                            last_norm.root(act, k - 4, n + k - 3, eps)
                        if final and 6 <= k:
                            act.wait_ge(last_norm.shift_done, n + k - 5)
                            act.wait_ge(out[k - 6], i * 32)
                            last_norm.apply(act, h_out[k - 6], res[k - 6], k - 6, ACT.Relu).then_inc(all_made, 1)

                run_bodies(act, nb, body)


def gat_logits(nc, g):
    nb = g.NTE // K
    with Phase(nc, "gat_logits_") as m:
        ident = m.sb("ident", [P, P])
        a_rows, product, wa = m.sb("a_rows", [P, 2, HID]), m.sb("product", [D, 2, HID]), m.sb("wa", [D, 2, H])
        idx = m.sbs("idx", [P, 20], I32)
        hs, hd, hdT = m.sbs("hs", [P, SUB, D]), m.sbs("hd", [P, SUB, D]), m.sbs("hdT", [P, TILE], n=2)
        sloped, logit = m.sbs("sloped", [H, TILE], n=2), m.sbs("logit", [H, TILE], n=2)
        hsT_ps, hdT_ps = ([m.ps(f"{n}{j}", [P, TILE]) for j in range(2)] for n in ("hsT_ps", "hdT_ps"))
        e_ps = [m.ps(f"e_ps{j}", [H, TILE]) for j in range(2)]
        idx_in, rows_in, logit_out, own = m.sems("idx_in"), g.gathered, m.sems("logit_out", 2), m.sem("own")
        rows0 = g.start(rows_in, nb * 128)
        cleared, ident_made, weights_in, product_made, weights_made = (
            m.sem(n) for n in ("cleared", "ident_made", "weights_in", "product_made", "weights_made"))
        turned_done, hdT_made, hsT_made, e_done, sloped_made, logit_made = (
            m.sem(n) for n in ("turned_done", "hdT_made", "hsT_made", "e_done", "sloped_made", "logit_made"))
        with nc.Block() as block:
            @block.sync
            def _(sp):
                sp.dma_start(g.wn[:, :], g.wnT).then_inc(weights_in, 16)
                broadcast_rows(sp, a_rows[:, 0, :], g.a_src, weights_in)
                broadcast_rows(sp, a_rows[:, 1, :], g.a_dst, weights_in)

                def load(k, i):
                    sp.dma_start(idx[k][:, :], g.IDX[bass.ds(i * K + k, 1), :, :].rearrange("t p s -> (t p) s")).then_inc(idx_in[k], 16)

                def body(i, more):
                    for k in range(K):
                        sp.wait_ge(logit_made, i * K + k + 1)
                        sp.dma_start(g.LOGIT[1][:, bass.ds((i * K + k) * TILE, TILE)], logit[k % 2][:, :]).then_inc(logit_out[k % 2], 16)
                        if more:
                            load(k, i + 1)

                for k in range(K):
                    load(k, 0)
                if nb > 1:
                    with sp.Fori(0, nb - 1) as i:
                        body(i, True)
                body(nb - 1, False)
                for slot in range(2):
                    sp.wait_ge(logit_out[slot], 16 * nb * slot_tiles(slot))

            @block.gpsimd
            def _(pool):
                make_identity(pool, ident, ident_made, cleared)

                def gather_tile(k, i):
                    wait_alone(pool, idx_in[k], (i + 1) * 16, own)
                    for s in range(SUB):
                        gather(pool, hd[k][:, s, :], g.H[:, :], idx[k][:, 4 + s:5 + s]).then_inc(rows_in[k], 16)
                        gather(pool, hs[k][:, s, :], g.H[:, :], idx[k][:, s:s + 1]).then_inc(rows_in[k], 16)

                for k in range(K):
                    gather_tile(k, 0)
                if nb > 1:
                    with pool.Fori(1, nb) as i:
                        for k in range(K):
                            pool.wait_ge(turned_done, (i - 1) * K + k + 1)
                            gather_tile(k, i)

            @block.tensor
            def _(pe):
                pe.wait_ge(ident_made, 1)
                pe.wait_ge(weights_made, 1)

                def body(i):
                    n = i * K
                    for k in range(K + 1):
                        if k < K:
                            pe.wait_ge(rows_in[k], i * 128 + (128 + rows0))
                            pe.wait_ge(hdT_made, n + max(k - 1, 0))
                            pe.wait_ge(hsT_made, n + max(k - 1, 0))
                            for s in range(SUB):
                                pe.transpose(hdT_ps[k % 2][:, s * P:(s + 1) * P], hd[k][:, s, :], ident[:, :])
                            for s in range(SUB):
                                last = pe.transpose(hsT_ps[k % 2][:, s * P:(s + 1) * P], hs[k][:, s, :], ident[:, :])
                            last.then_inc(turned_done, 1)
                        if k:
                            j = k - 1
                            pe.wait_ge(hdT_made, n + j + 1)
                            pe.wait_ge(logit_made, n + max(j - 1, 0))
                            pe.matmul(e_ps[j % 2][:, :], wa[:, 1, :], hdT[j % 2][:, :], start=True, stop=False)
                            pe.wait_ge(hsT_made, n + j + 1)
                            pe.matmul(e_ps[j % 2][:, :], wa[:, 0, :], g.srcT[:, bass.ds((n + j) * TILE, TILE)],
                                      start=False, stop=True).then_inc(e_done, 1)

                run_bodies(pe, nb, body)

            @block.scalar
            def _(act):
                def body(i):
                    n = i * K
                    for k in range(K + 1):
                        if k < K:
                            act.wait_ge(turned_done, n + k + 1)
                            act.wait_ge(e_done, n + max(k - 1, 0))
                            act.activation(hdT[k % 2][:, :], hdT_ps[k % 2][:, :], ACT.Copy).then_inc(hdT_made, 1)
                        if k:
                            j = k - 1
                            act.wait_ge(e_done, n + j + 1)
                            act.wait_ge(logit_made, n + max(j - 1, 0))
                            act.activation(sloped[j % 2][:, :], e_ps[j % 2][:, :], ACT.Copy, scale=SLOPE).then_inc(sloped_made, 1)

                run_bodies(act, nb, body)

            @block.vector
            def _(dve):
                dve.wait_ge(weights_in, 48)
                for j in range(2):
                    dve.tensor_tensor(product[:, j, :], g.wn[:, :], a_rows[:, j, :], ALU.mult).then_inc(product_made, 1)
                dve.wait_ge(product_made, 2)
                dve.tensor_reduce(out=wa[:, :, :].rearrange("p j h -> p (j h)"),
                                  in_=product[:, :, :].rearrange("p j (h d) -> p (j h) d", h=H), axis=AX.X, op=ALU.add).then_inc(weights_made, 1)

                def body(i):
                    n = i * K
                    for k in range(K + 1):
                        if k < K:
                            dve.wait_ge(turned_done, n + k + 1)
                            dve.tensor_copy(g.srcT[:, bass.ds((n + k) * TILE, TILE)], hsT_ps[k % 2][:, :]).then_inc(hsT_made, 1)
                        if k:
                            j = k - 1
                            dve.wait_ge(sloped_made, n + j + 1)
                            dve.wait_ge(logit_out[j % 2], i * (16 * slot_tiles(j % 2)) + 16 * (j // 2))
                            dve.tensor_tensor(logit[j % 2][:, :], e_ps[j % 2][:, :], sloped[j % 2][:, :], ALU.max).then_inc(logit_made, 1)

                run_bodies(dve, nb, body)


def gat_aggregate(nc, g):
    nb = g.NTE // K
    with Phase(nc, "gat_aggregate_") as m:
        ident, none = m.sb("ident", [P, P]), m.sb("none", [1, HID])
        alphaT, keep = m.sbs("alphaT", [H, TILE]), m.sbs("keep", [P, TILE])
        alpha, src = m.sbs("alpha", [P, SUB * H], n=2), m.sbs("src", [P, TILE], n=2)
        part = m.sbs("part", [P, SUB, HID], n=2)
        sumT, rows = m.sbs("sumT", [P, 2, TILE], n=2), m.sbs("rows", [P, SUB, HID])
        y = [m.ps(f"y{j}", [P, 2, HID]) for j in range(2)]
        partT = [m.ps(f"partT{j}", [P, TILE]) for j in range(2)]
        back = [m.ps(f"back{j}", [P, 2, HID]) for j in range(2)]
        alpha_ps = m.ps("alpha_ps", [P, SUB * H])
        tile_in, rows_out, none_out = m.sems("tile_in"), m.sems("rows_out"), m.sem("none_out")
        cleared, ident_made, set_once, none_set = (m.sem(n) for n in ("cleared", "ident_made", "set_once", "none_set"))
        alpha_turned, alpha_made, src_copied, y_done, part_made = (
            m.sem(n) for n in ("alpha_turned", "alpha_made", "src_copied", "y_done", "part_made"))
        partT_done, scanned, back_done, rows_made = (m.sem(n) for n in ("partT_done", "scanned", "back_done", "rows_made"))
        with nc.Block() as block:
            @block.sync
            def _(sp):
                sp.wait_ge(none_set, 1)
                sp.dma_start(g.GAT[g.EP:g.EP + 1, :], none[:, :]).then_inc(none_out, 16)

                def load(k, i):
                    n = i * K + k
                    sp.dma_start(alphaT[k][:, :], g.ALPHA[:, bass.ds(n * TILE, TILE)]).then_inc(tile_in[k], 16)
                    sp.dma_start(keep[k][:, :], edge_span(g.KEEP, n, P)).then_inc(tile_in[k], 16)

                def store(k, i):
                    sp.dma_start(edge_rows(g.GAT, i * K + k), rows[k][:, :, :]).then_inc(rows_out[k], 16)

                stream(sp, nb, load, store, lambda k, i: sp.wait_ge(rows_made, (i - 1) * K + k + 1))
                for k in range(K):
                    sp.wait_ge(rows_out[k], 16 * nb)
                sp.wait_ge(none_out, 16)

            @block.gpsimd
            def _(pool):
                make_identity(pool, ident, ident_made, cleared)

            @block.tensor
            def _(pe):
                pe.wait_ge(ident_made, 1)

                def body(i):
                    n = i * K

                    def turn_alpha(k):
                        pe.wait_ge(tile_in[k], (i + 1) * 32)
                        pe.wait_ge(alpha_made, n + k)
                        for s in range(SUB):
                            last = pe.matmul(alpha_ps[:, s * H:(s + 1) * H], alphaT[k][:, s * P:(s + 1) * P], ident[0:H, 0:H],
                                             start=True, stop=True)
                        last.then_inc(alpha_turned, 1)

                    def project(k):
                        pe.wait_ge(src_copied, n + k + 1)
                        pe.wait_ge(part_made, 2 * n + 2 * k)
                        for s in range(SUB):
                            pe.matmul(y[s // 2][:, s % 2, :], src[k % 2][:, s * P:(s + 1) * P], g.wn[:, :],
                                      start=True, stop=True).then_inc(y_done, 1)

                    def turn(k):
                        pe.wait_ge(part_made, 2 * n + 2 * (k + 1))
                        pe.wait_ge(scanned, 2 * n + 2 * k)
                        for j in range(2):
                            for s in range(SUB):
                                last = pe.transpose(partT[j][:, s * P:(s + 1) * P], part[k % 2][:, s, j * P:(j + 1) * P], ident[:, :])
                        last.then_inc(partT_done, 1)

                    def turn_back(k):
                        pe.wait_ge(scanned, 2 * n + 2 * (k + 1))
                        pe.wait_ge(rows_made, n + k)
                        for s in range(SUB):
                            for j in range(2):
                                last = pe.transpose(back[s // 2][:, s % 2, j * P:(j + 1) * P], sumT[k % 2][:, j, s * P:(s + 1) * P], ident[:, :])
                        last.then_inc(back_done, 1)

                    turn_alpha(0)
                    for k in range(K + 2):
                        if k < K:
                            project(k)
                        if k + 1 < K:
                            turn_alpha(k + 1)
                        if 1 <= k <= K:
                            turn(k - 1)
                        if k >= 2:
                            turn_back(k - 2)

                run_bodies(pe, nb, body)

            @block.scalar
            def _(act):
                def body(i):
                    n = i * K

                    def copy_alpha(k):
                        act.wait_ge(alpha_turned, n + k + 1)
                        act.wait_ge(part_made, 2 * n + 2 * max(k - 1, 0))
                        act.activation(alpha[k % 2][:, :], alpha_ps[:, :], ACT.Copy).then_inc(alpha_made, 1)

                    def copy_src(k):
                        act.wait_ge(y_done, SUB * n + SUB * max(k - 1, 0))
                        act.activation(src[k % 2][:, :], g.srcT[:, bass.ds((n + k) * TILE, TILE)], ACT.Copy).then_inc(src_copied, 1)

                    copy_src(0)
                    copy_alpha(0)
                    for k in range(K + 2):
                        if k + 1 < K:
                            copy_src(k + 1)
                            copy_alpha(k + 1)
                        if k >= 2:
                            act.wait_ge(back_done, n + k - 1)
                            act.wait_ge(rows_out[k - 2], i * 16)
                            for j in range(2):
                                last = act.activation(rows[k - 2][:, 2 * j:2 * j + 2, :], back[j][:, :, :], ACT.Copy)
                            last.then_inc(rows_made, 1)

                run_bodies(act, nb, body)

            @block.vector
            def _(dve):
                dve.memset(none[:, :], 0.0).then_inc(none_set, 1)
                for slot in range(2):
                    dve.memset(sumT[slot][:, :, TILE - 1:TILE], 0.0).then_inc(set_once, 1)
                dve.wait_ge(set_once, 2)

                def body(i):
                    n = i * K

                    def weigh(k):
                        dve.wait_ge(alpha_made, n + k + 1)
                        dve.wait_ge(partT_done, n + max(k - 1, 0))
                        for j in range(2):
                            dve.wait_ge(y_done, SUB * n + SUB * k + 2 * (j + 1))
                            weights = alpha[k % 2][:, 2 * H * j:2 * H * (j + 1)].unsqueeze(2).to_broadcast([P, 2 * H, HD])
                            dve.tensor_tensor(part[k % 2][:, 2 * j:2 * j + 2, :].rearrange("p s (h d) -> p (s h) d", h=H),
                                              y[j][:, :, :].rearrange("p s (h d) -> p (s h) d", h=H), weights, ALU.mult).then_inc(part_made, 1)

                    def scan(k):
                        dve.wait_ge(partT_done, n + k + 1)
                        dve.wait_ge(scanned, 2 * n + 2 * k)
                        dve.wait_ge(back_done, n + max(k - 1, 0))
                        before = sumT[(k - 1) % 2 if k else (K - 1) % 2]
                        for j in range(2):
                            dve.tensor_tensor_scan(sumT[k % 2][:, j, :], keep[k][:, :], partT[j][:, :],
                                                   before[:, j, TILE - 1:TILE], ALU.mult, ALU.add).then_inc(scanned, 1)

                    for k in range(K + 1):
                        if k < K:
                            weigh(k)
                        if k:
                            scan(k - 1)

                run_bodies(dve, nb, body)


def gat_mlp(nc, g):
    nb = g.NTN // K
    with Phase(nc, "gat_mlp_") as m:
        ident, eps, ones = m.sb("ident", [P, P]), m.sb("eps", [P, 1]), m.sb("ones", [1, P])
        w1, w2, b1, b2 = m.sb("w1", [P, 2, HID]), m.sb("w2", [P, 2, D]), m.sb("b1", [P, 2]), m.sb("b2", [1, TILE])
        last_edge = m.sbs("last_edge", [P, SUB], I32)
        heads, x = m.sbs("heads", [P, SUB, HID]), m.sbs("x", [P, SUB, D])
        headsT, hidT = m.sbs("headsT", [P, 2, TILE], n=2), m.sbs("hidT", [P, 2, TILE], n=2)
        x3, h4, total = (m.sbs(n, [P, SUB, D]) for n in ("x3", "h4", "total"))
        turned, hid, o = ([m.ps(f"{n}{j}", [P, TILE]) for j in range(2)] for n in ("turned", "hid", "o"))
        norm = Norm(m, "norm")
        idx_in, x_in, heads_in, out, own = m.sems("idx_in"), m.sems("x_in"), g.gathered, m.sems("out"), m.sem("own")
        heads0 = g.start(heads_in, nb * 64)
        cleared, ident_made, set_once, weights_in = (m.sem(n) for n in ("cleared", "ident_made", "set_once", "weights_in"))
        turned_done, headsT_made, hid_done, hidT_made, o_done, x3_made, h4_made, total_made = (
            m.sem(n) for n in ("turned_done", "headsT_made", "hid_done", "hidT_made", "o_done", "x3_made", "h4_made", "total_made"))
        with nc.Block() as block:
            @block.sync
            def _(sp):
                sp.dma_start(w1[:, :, :], g.mw1.rearrange("(j p) n -> p j n", p=P)).then_inc(weights_in, 16)
                sp.dma_start(w2[:, :, :], g.mw2.rearrange("(j p) n -> p j n", p=P)).then_inc(weights_in, 16)
                with nc.allow_non_contiguous_dma("256 biases"):
                    sp.dma_start(b1[:, :], g.mb1.rearrange("o (j p) -> p (o j)", p=P)).then_inc(weights_in, 16)
                for a in range(SUB):
                    sp.dma_start(b2[:, a * D:(a + 1) * D], g.mb2).then_inc(weights_in, 16)

                def load(k, i):
                    n = i * K + k
                    sp.dma_start(last_edge[k][:, :], g.LAST[bass.ds(n * TILE, TILE), :].rearrange("(p a) o -> p (a o)", p=P)).then_inc(idx_in[k], 16)
                    sp.dma_start(x[k][:, :, :], node_rows(g.X, n)).then_inc(x_in[k], 16)

                def store(k, i):
                    sp.dma_start(node_rows(g.H, i * K + k), h4[k][:, :, :]).then_inc(out[k], 16)
                    sp.dma_start(node_rows(g.out, i * K + k), total[k][:, :, :]).then_inc(out[k], 16)

                stream(sp, nb, load, store, lambda k, i: sp.wait_ge(total_made, (i - 1) * K + k + 1))
                for k in range(K):
                    sp.wait_ge(out[k], 32 * nb)

            @block.gpsimd
            def _(pool):
                make_identity(pool, ident, ident_made, cleared)

                def gather_tile(k, i):
                    wait_alone(pool, idx_in[k], (i + 1) * 16, own)
                    for a in range(SUB):
                        gather(pool, heads[k][:, a, :], g.GAT[:, :], last_edge[k][:, a:a + 1]).then_inc(heads_in[k], 16)

                for k in range(K):
                    gather_tile(k, 0)
                if nb > 1:
                    with pool.Fori(1, nb) as i:
                        for k in range(K):
                            pool.wait_ge(turned_done, 2 * (i - 1) * K + 2 * (k + 1))
                            gather_tile(k, i)

            @block.tensor
            def _(pe):
                pe.wait_ge(ident_made, 1)
                pe.wait_ge(set_once, 2)
                pe.wait_ge(weights_in, 16 * 7)

                def body(i):
                    n = i * K

                    def turn(k):
                        pe.wait_ge(heads_in[k], i * 64 + (64 + heads0))
                        for j in range(2):
                            pe.wait_ge(headsT_made, 2 * n + 2 * k - (1 - j) if k else 2 * n)
                            for a in range(SUB):
                                last = pe.transpose(turned[j][:, a * P:(a + 1) * P], heads[k][:, a, j * P:(j + 1) * P], ident[:, :])
                            last.then_inc(turned_done, 1)

                    def first(k):
                        pe.wait_ge(headsT_made, 2 * n + 2 * (k + 1))
                        for j in range(2):
                            pe.wait_ge(hidT_made, 2 * n + 2 * k - (1 - j) if k else 2 * n)
                            for c in range(2):
                                last = pe.matmul(hid[j][:, :], w1[:, c, j * P:(j + 1) * P], headsT[k % 2][:, c, :],
                                                 start=(c == 0), stop=(c == 1))
                            last.then_inc(hid_done, 1)

                    def second(k):
                        pe.wait_ge(x3_made, n + max(k - 1, 0))
                        pe.matmul(o[k % 2][:, :], ones[:, :], b2[:, :], start=True, stop=True)
                        pe.wait_ge(hidT_made, 2 * n + 2 * (k + 1))
                        for a in range(SUB):
                            for c in range(2):
                                last = pe.matmul(o[k % 2][:, a * D:(a + 1) * D], hidT[k % 2][:, c, a * P:(a + 1) * P], w2[:, c, :],
                                                 start=False, stop=True, skip_group_check=True)
                        last.then_inc(o_done, 1)

                    for k in range(K + 2):
                        if k < K:
                            turn(k)
                        if 1 <= k <= K:
                            first(k - 1)
                        if k >= 2:
                            second(k - 2)

                run_bodies(pe, nb, body)

            @block.scalar
            def _(act):
                act.wait_ge(set_once, 2)
                act.wait_ge(weights_in, 16 * 7)

                def body(i):
                    n = i * K
                    for k in range(K + 5):
                        if k < K:
                            for j in range(2):
                                act.wait_ge(turned_done, 2 * n + 2 * k + j + 1)
                                act.wait_ge(hid_done, 2 * n + 2 * max(k - 1, 0))
                                act.activation(headsT[k % 2][:, j, :], turned[j][:, :], ACT.Relu).then_inc(headsT_made, 1)
                        if 1 <= k <= K:
                            for j in range(2):
                                act.wait_ge(hid_done, 2 * n + 2 * (k - 1) + j + 1)
                                act.wait_ge(o_done, n + max(k - 2, 0))
                                act.activation(hidT[(k - 1) % 2][:, j, :], hid[j][:, :], ACT.Relu, bias=b1[:, j:j + 1]).then_inc(hidT_made, 1)
                        if 3 <= k < K + 3:
                            norm.root(act, k - 3, n + k - 2, eps)
                        if 5 <= k:
                            act.wait_ge(norm.shift_done, n + k - 4)
                            act.wait_ge(out[k - 5], i * 32)
                            norm.apply(act, h4[k - 5], x3[k - 5], k - 5, ACT.Relu).then_inc(h4_made, 1)

                run_bodies(act, nb, body)

            @block.vector
            def _(dve):
                dve.memset(eps[:, :], EPS).then_inc(set_once, 1)
                dve.memset(ones[:, :], 1.0).then_inc(set_once, 1)

                def body(i):
                    n = i * K
                    for k in range(K + 3):
                        if k < K:
                            dve.wait_ge(o_done, n + k + 1)
                            dve.wait_ge(x_in[k], (i + 1) * 16)
                            dve.wait_ge(h4_made, n)
                            flat = x3[k][:, :, :].rearrange("p a d -> p (a d)")
                            dve.tensor_tensor(flat, o[k % 2][:, :], x[k][:, :, :].rearrange("p a d -> p (a d)"), ALU.add).then_inc(x3_made, 1)
                            dve.wait_ge(x3_made, n + k + 1)
                            norm.take_stats(dve, x3[k], k)
                            norm.moments(dve, k, n + k + 1)
                        if 1 <= k <= K:
                            norm.scales(dve, k - 1, n + k)
                        if 3 <= k:
                            dve.wait_ge(h4_made, n + k - 2)
                            dve.wait_ge(out[k - 3], i * 32)
                            dve.tensor_tensor(total[k - 3][:, :, :], x3[k - 3][:, :, :], h4[k - 3][:, :, :], ALU.add).then_inc(total_made, 1)

                run_bodies(dve, nb, body)


def mean_edges(nc, g):
    nb = g.NTE // K
    with Phase(nc, "mean_edges_") as m:
        ident = m.sb("ident", [P, P])
        idx = m.sbs("idx", [P, 20], I32)
        hs, keep, sumT, rows = m.sbs("hs", [P, SUB, D]), m.sbs("keep", [P, TILE]), m.sbs("sumT", [P, TILE]), m.sbs("rows", [P, SUB, D])
        two, counts, half = m.sb("two", [1, TILE]), m.sbs("counts", [1, TILE], n=2), m.sbs("half", [P, SUB], n=2)
        turned, back, counts_ps = ([m.ps(f"{n}{j}", [P, TILE]) for j in range(2)] for n in ("turned", "back", "counts_ps"))
        idx_in, keep_in, hs_in, added = m.sems("idx_in"), m.sems("keep_in"), g.gathered, g.scattered
        hs0, added0 = g.start(hs_in, nb * 64), g.start(added, nb * 64)
        cleared, ident_made, set_once, own = (m.sem(n) for n in ("cleared", "ident_made", "set_once", "own"))
        turned_done, scanned, counted, half_made, back_done, rows_made = (
            m.sem(n) for n in ("turned_done", "scanned", "counted", "half_made", "back_done", "rows_made"))
        with nc.Block() as block:
            @block.sync
            def _(sp):
                def load(k, i):
                    sp.dma_start(idx[k][:, :], g.IDX[bass.ds(i * K + k, 1), :, :].rearrange("t p s -> (t p) s")).then_inc(idx_in[k], 16)
                    sp.dma_start(keep[k][:, :], edge_span(g.KEEP, i * K + k, P)).then_inc(keep_in[k], 16)

                for k in range(K):
                    load(k, 0)
                if nb > 1:
                    with sp.Fori(1, nb) as i:
                        for k in range(K):
                            sp.wait_ge(added[k], i * 64 + added0)
                            load(k, i)

            @block.gpsimd
            def _(pool):
                make_identity(pool, ident, ident_made, cleared)

                def gather_tile(k, i):
                    wait_alone(pool, idx_in[k], (i + 1) * 16, own)
                    for s in range(SUB):
                        gather(pool, hs[k][:, s, :], g.H[:, :], idx[k][:, s:s + 1]).then_inc(hs_in[k], 16)

                def body(i, more):
                    for k in range(K):
                        wait_alone(pool, rows_made, i * K + k + 1, own)
                        for s in range(SUB):
                            pool.indirect_dma_start(out=g.out[:, :], out_offset=bass.IndirectOffsetOnAxis(ap=idx[k][:, 12 + s:13 + s], axis=0),
                                                    in_=rows[k][:, s, :], in_offset=None, compute_op=ALU.add).then_inc(added[k], 16)
                        if more and k >= BEHIND:
                            gather_tile(k - BEHIND, i + 1)
                    if more:
                        for k in range(K - BEHIND, K):
                            gather_tile(k, i + 1)

                for k in range(K):
                    gather_tile(k, 0)
                if nb > 1:
                    with pool.Fori(0, nb - 1) as i:
                        body(i, True)
                body(nb - 1, False)
                for k in range(K):
                    pool.wait_ge(added[k], nb * 64 + added0)

            @block.tensor
            def _(pe):
                pe.wait_ge(ident_made, 1)

                def body(i):
                    n = i * K
                    for k in range(K + 1):
                        if k < K:
                            pe.wait_ge(hs_in[k], i * 64 + (64 + hs0))
                            pe.wait_ge(scanned, 2 * n + 2 * max(k - 1, 0))
                            for s in range(SUB):
                                last = pe.transpose(turned[k % 2][:, s * P:(s + 1) * P], hs[k][:, s, :], ident[:, :])
                            last.then_inc(turned_done, 1)
                        if k:
                            j = k - 1
                            pe.wait_ge(scanned, 2 * n + 2 * (j + 1))
                            pe.wait_ge(half_made, n + max(j - 1, 0))
                            for s in range(SUB):
                                last = pe.matmul(counts_ps[j % 2][:, s:s + 1], counts[j % 2][:, s * P:(s + 1) * P], ident[0:1, 0:1],
                                                 start=True, stop=True)
                            last.then_inc(counted, 1)
                            pe.wait_ge(rows_made, n + max(j - 1, 0))
                            for s in range(SUB):
                                last = pe.transpose(back[j % 2][:, s * P:(s + 1) * P], sumT[j][:, s * P:(s + 1) * P], ident[:, :])
                            last.then_inc(back_done, 1)

                run_bodies(pe, nb, body)

            @block.vector
            def _(dve):
                dve.memset(sumT[K - 1][:, TILE - 1:TILE], 0.0).then_inc(set_once, 1)
                for j in range(2):
                    dve.memset(counts[j][:, TILE - 1:TILE], 0.0).then_inc(set_once, 1)
                dve.memset(two[:, :], 2.0).then_inc(set_once, 1)
                dve.wait_ge(set_once, 4)

                def body(i):
                    n = i * K
                    for k in range(K + 1):
                        if k < K:
                            dve.wait_ge(keep_in[k], (i + 1) * 16)
                            dve.wait_ge(turned_done, n + k + 1)
                            dve.wait_ge(scanned, 2 * n + 2 * k)
                            dve.wait_ge(back_done, n)
                            dve.tensor_tensor_scan(sumT[k][:, :], keep[k][:, :], turned[k % 2][:, :],
                                                   sumT[k - 1][:, TILE - 1:TILE], ALU.mult, ALU.add).then_inc(scanned, 1)
                            dve.wait_ge(counted, n + max(k - 1, 0))
                            before = counts[(k - 1) % 2 if k else (K - 1) % 2]
                            dve.tensor_tensor_scan(counts[k % 2][:, :], keep[k][0:1, :], two[:, :],
                                                   before[:, TILE - 1:TILE], ALU.mult, ALU.add).then_inc(scanned, 1)
                        if k:
                            dve.wait_ge(counted, n + k)
                            dve.wait_ge(rows_made, n + max(k - 2, 0))
                            dve.reciprocal(half[(k - 1) % 2][:, :], counts_ps[(k - 1) % 2][:, 0:SUB]).then_inc(half_made, 1)

                run_bodies(dve, nb, body)

            @block.scalar
            def _(act):
                def body(i):
                    n = i * K
                    for k in range(K):
                        act.wait_ge(half_made, n + k + 1)
                        act.wait_ge(back_done, n + k + 1)
                        act.wait_ge(added[k], i * 64 + added0)
                        for s in range(SUB):
                            last = act.activation(rows[k][:, s, :], back[k % 2][:, s * P:(s + 1) * P], ACT.Copy, scale=half[k % 2][:, s:s + 1])
                        last.then_inc(rows_made, 1)

                run_bodies(act, nb, body)


class Graph:

    def start(self, sems, count):
        before = self.counted.get(id(sems), 0)
        self.counted[id(sems)] = before + count
        return before


def build(nc, g, phases=99):
    g.NTN, g.NTE = g.NP // TILE, g.EP // TILE
    dram = lambda name, shape, dt=F32: nc.dram_tensor(name, shape, dt).ap()
    g.H, g.AGG = dram("H", (g.NP, D)), dram("AGG", (g.NP, D))
    g.LAST = dram("LAST", (g.NP, 1), I32)
    g.KEEP, g.KEEPN = dram("KEEP", (1, g.EP)), dram("KEEPN", (1, g.EP))
    g.IDX = dram("IDX", (g.NTE, P, 20), I32)
    g.YT, g.X = dram("YT", (g.NTN, P, TILE)), dram("X", (g.NP, D))
    g.LOGIT = [dram("LOGIT_SELF", (H, g.EP)), dram("LOGIT_EDGE", (H, g.EP))]
    g.GAT = dram("GAT", (g.EP + 1, HID))
    g.ALPHA = dram("ALPHA", (H, g.EP))
    with ExitStack() as kept:
        sems = lambda name, n: [kept.enter_context(nc.semaphore(f"{name}{k}")) for k in range(n)]
        g.gathered, g.scattered, g.zeros_out = sems("gathered", K), sems("scattered", K), sems("zeros_out", 1)[0]
        g.counted = {}
        keep = lambda name, shape: kept.enter_context(nc.sbuf_tensor(name, shape, F32))
        g.bn_scale, g.bn_shift = keep("bn_scale", [D, 1]), keep("bn_shift", [D, 1])
        g.wn = keep("wn", [D, HID])
        g.wl, g.wsum, g.wmean = keep("wl", [D, H * D]), keep("wsum", [D, H * D]), keep("wmean", [D, D])
        steps = [prepare_indices, first_norm, gine_edges, gine_mlp, gine_finish,
                 lambda nc, g: convolution(nc, g, 0), lambda nc, g: convolution(nc, g, 1),
                 attention, gat_mlp, mean_edges]
        for step in steps[:phases]:
            step(nc, g)


def attention(nc, g):
    with nc.sbuf_tensor("srcT", [D, g.EP], F32) as g.srcT:
        gat_logits(nc, g)
        edge_softmax(nc, g, 2, 0, 1.0)
        gat_aggregate(nc, g)


def convolution(nc, g, layer):
    with nc.sbuf_tensor(f"diffT{layer}", [D, g.EP], F32) as g.diffT:
        conv_logits(nc, g, layer)
        edge_softmax(nc, g, layer, 1, 1.0 / H)
        conv_aggregate(nc, g, layer)
    conv_nodes(nc, g, layer, layer == 1)


def as_column(a):
    return a.reshape(-1, 1)


def as_row(a):
    return a.reshape(1, -1)


_WEIGHTS = {
    "w1T": ("L0_gnn_W1", np.transpose), "w2T": ("L0_gnn_W2", np.transpose),
    "b1": ("L0_gnn_b1", as_column), "b2": ("L0_gnn_b2", as_column),
    "gamma": ("L0_gnn_gamma", as_column), "beta": ("L0_gnn_beta", as_column),
    "wnT": ("L2_gnn_W_n", lambda a: a.transpose(1, 0, 2).reshape(D, HID)),
    "a_src": ("L2_gnn_a_src", as_row), "a_dst": ("L2_gnn_a_dst", as_row),
    "mw1": ("L2_gnn_mlp_W1", np.asarray), "mb1": ("L2_gnn_mlp_b1", as_row),
    "mw2": ("L2_gnn_mlp_W2", np.asarray), "mb2": ("L2_gnn_mlp_b2", as_row),
    "wl1": ("L1_gnn_Wl1", np.asarray), "wr1": ("L1_gnn_Wr1", np.asarray), "att1T": ("L1_gnn_att1", np.transpose),
    "cb1": ("L1_gnn_b1", as_row), "cg1": ("L1_gnn_g1", as_row), "cbe1": ("L1_gnn_be1", as_row),
    "wl2": ("L1_gnn_Wl2", np.asarray), "wr2": ("L1_gnn_Wr2", np.asarray), "att2T": ("L1_gnn_att2", np.transpose),
    "cb2": ("L1_gnn_b2", as_row), "cg2": ("L1_gnn_g2", as_row), "cbe2": ("L1_gnn_be2", as_row),
}


def layout(inputs):
    x, src, dst, ea = (np.asarray(inputs[k]) for k in ("x", "src", "dst", "edge_attr_128"))
    n, e = len(x), len(src)
    npad, epad = padded(n), padded(e)

    def pad(a, rows, value=0):
        return np.concatenate([a, np.full((rows - len(a), *a.shape[1:]), value, a.dtype)])

    def tiles(a):
        return np.ascontiguousarray(a.reshape(-1, SUB, P).transpose(0, 2, 1))

    src, dst = pad(src, epad, n), pad(dst, epad, n)
    before, after = np.append(np.int32(-1), dst[:-1]), np.append(dst[1:], np.int32(-1))
    arrays = {
        "x": pad(x, npad), "ea": pad(ea, epad),
        "src_t": tiles(src), "dst_t": tiles(dst), "nxt_t": tiles(after),
        "dst_r": dst[None], "prev_r": before[None], "next_r": after[None],
    }
    for name, (source, turn) in _WEIGHTS.items():
        arrays[name] = np.ascontiguousarray(turn(np.asarray(inputs[source])))
    return arrays, (n, npad, epad)


def declare_and_build(nc, arrays, sizes, phases=99):
    g = Graph()
    g.N, g.NP, g.EP = sizes
    given = {name: nc.dram_tensor(name, a.shape, mybir.dt.from_np(a.dtype), kind="ExternalInput").ap()
             for name, a in arrays.items()}
    g.x, g.ea, g.src_t, g.dst_t, g.nxt_t, g.dst_r, g.prev_r, g.next_r = (
        given[n] for n in ("x", "ea", "src_t", "dst_t", "nxt_t", "dst_r", "prev_r", "next_r"))
    g.w1T, g.w2T, g.b1, g.b2, g.gamma, g.beta = (
        given[n] for n in ("w1T", "w2T", "b1", "b2", "gamma", "beta"))
    g.wnT, g.a_src, g.a_dst, g.mw1, g.mb1, g.mw2, g.mb2 = (
        given[n] for n in ("wnT", "a_src", "a_dst", "mw1", "mb1", "mw2", "mb2"))
    g.conv_weights = [tuple(given[f"{n}{j}{t}"] for n, t in (("wl", ""), ("wr", ""), ("att", "T"))) for j in (1, 2)]
    g.conv_norms = [tuple(given[f"{n}{j}"] for n in ("cb", "cg", "cbe")) for j in (1, 2)]
    g.out = nc.dram_tensor("out", (g.NP + g.EP, D), F32, kind="ExternalOutput").ap()
    build(nc, g, phases)


def kernel(**inputs):
    import concourse.bacc as bacc
    from concourse.bass_utils import run_bass_kernel_spmd

    arrays, sizes = layout(inputs)
    nc = bacc.Bacc("TRN2", target_bir_lowering=False, num_devices=1)
    declare_and_build(nc, arrays, sizes)
    result = run_bass_kernel_spmd(nc, [arrays], core_ids=[0])
    return result.results[0]["out"][:sizes[0]]
```

```python
import numpy as np
from contextlib import ExitStack

import concourse.bass as bass
from concourse import mybir

F32 = mybir.dt.float32
I32 = mybir.dt.int32
ALU = mybir.AluOpType
ACT = mybir.ActivationFunctionType
AX = mybir.AxisListType

P = 128
D = 128
H = 4
SUB = 4
TILE = P * SUB
K = 7
RING = 7
NB = 2 * RING
EPS = 1e-5
SLOPE = 0.2
BEHIND = 3
BIG = 1e30
CH = P // H
HID = 256
HD = 64


def cdiv(a, b):
    return -(-a // b)


def padded(n, tiles):
    return cdiv(n + 1, TILE * tiles) * TILE * tiles


class Phase:

    def __init__(self, nc, name):
        self.nc, self.name, self.stack, self.used = nc, name, ExitStack(), []

    def __enter__(self):
        self.stack.__enter__()
        return self

    def __exit__(self, *error):
        if error[0] is None:
            with self.nc.Block() as block:
                @block.gpsimd
                def _(pool):
                    for s in self.used:
                        pool.sem_clear(s)
        return self.stack.__exit__(*error)

    def sb(self, name, shape, dt=F32):
        return self.stack.enter_context(self.nc.sbuf_tensor(self.name + name, shape, dt))

    def ps(self, name, shape, dt=F32):
        return self.stack.enter_context(self.nc.psum_tensor(self.name + name, shape, dt))

    def sem(self, name):
        s = self.stack.enter_context(self.nc.semaphore(self.name + name))
        self.used.append(s)
        return s

    def sbs(self, name, shape, dt=F32, n=K):
        return [self.sb(f"{name}{k}", shape, dt) for k in range(n)]

    def sems(self, name, n=K):
        return [self.sem(f"{name}{k}") for k in range(n)]


def node_rows(table, n):
    return table[bass.ds(n * TILE, TILE), :].rearrange("(p a) d -> p a d", p=P)


def edge_rows(table, n):
    return table[bass.ds(n * TILE, TILE), :].rearrange("(s p) d -> p s d", p=P)


def edge_span(row, n, parts):
    return row[:, bass.ds(n * TILE, TILE)].to_broadcast([parts, TILE])


def mean_and_variance(dve, stats, mv, stats_done, value, own_wait):
    dve.wait_ge(stats_done, value)
    dve.sem_inc(own_wait, 1)
    for a in range(SUB):
        last = dve.bn_aggr(out=mv[:, a, :], in_=stats[:, a, :])
    return last


def row_stats(dve, x, stats):
    for a in range(SUB):
        last = dve.bn_stats(out=stats[:, a, :], in_=x[:, a, :])
    return last


def prepare_indices(nc, g):
    nt, flat = g.NTE, g.EP // P
    with Phase(nc, "prepare_indices_") as m:
        idx = m.sb("idx", [P, nt, 16], I32)
        nxt = m.sb("nxt", [P, nt, SUB], I32)
        eid = m.sb("eid", [P, nt, SUB], I32)
        dstf, nxtf, same, dump = (m.sb(n, [P, nt, SUB]) for n in ("dstf", "nxtf", "same", "dump"))
        lastf, addf = m.sb("lastf", [P, nt, SUB]), m.sb("addf", [P, nt, SUB])
        rowi = m.sb("rowi", [P, 3, flat], I32)
        rowf = m.sb("rowf", [P, 3, flat])
        keep = m.sb("keep", [P, 2, flat])
        loaded, loaded_rows, ids_made, steps = m.sem("loaded"), m.sem("loaded_rows"), m.sem("ids_made"), m.sem("steps")
        idx_made, keep_made, stored = m.sem("idx_made"), m.sem("keep_made"), m.sem("stored")
        with nc.Block() as block:
            @block.sync
            def _(sp):
                tiles = lambda x: x.rearrange("t p s -> p t s")
                with nc.allow_non_contiguous_dma("four indices a run"):
                    sp.dma_start(idx[:, :, 0:4], tiles(g.src_t)).then_inc(loaded, 16)
                    sp.dma_start(idx[:, :, 4:8], tiles(g.dst_t)).then_inc(loaded, 16)
                    sp.dma_start(nxt[:, :, :], tiles(g.nxt_t)).then_inc(loaded, 16)
                for j, row in enumerate((g.dst_r, g.prev_r, g.next_r)):
                    sp.dma_start(rowi[:, j, :], row.rearrange("o (p j) -> (o p) j", p=P)).then_inc(loaded_rows, 16)
                sp.wait_ge(keep_made, 1)
                sp.dma_start(g.KEEP.rearrange("o (p j) -> (o p) j", p=P), keep[:, 0, :]).then_inc(stored, 16)
                sp.dma_start(g.KEEPN.rearrange("o (p j) -> (o p) j", p=P), keep[:, 1, :]).then_inc(stored, 16)
                sp.wait_ge(idx_made, 1)
                sp.dma_start(g.IDX.rearrange("t p s -> p t s"), idx[:, :, :]).then_inc(stored, 16)
                sp.wait_ge(stored, 3 * 16)

            @block.gpsimd
            def _(pool):
                pool.iota(eid[:, :, :], pattern=[[TILE, nt], [P, SUB]], base=0, channel_multiplier=1).then_inc(ids_made, 1)

            @block.vector
            def _(dve):
                count = [0]

                def step(instruction):
                    count[0] += 1
                    instruction.then_inc(steps, 1)
                    dve.wait_ge(steps, count[0])

                dve.wait_ge(loaded_rows, 3 * 16)
                step(dve.tensor_copy(rowf[:, :, :], rowi[:, :, :]))
                dve.tensor_tensor(keep[:, 0, :], rowf[:, 0, :], rowf[:, 1, :], ALU.is_equal)
                dve.tensor_tensor(keep[:, 1, :], rowf[:, 0, :], rowf[:, 2, :], ALU.is_equal).then_inc(keep_made, 1)
                dve.wait_ge(loaded, 3 * 16)
                dve.wait_ge(ids_made, 1)
                dve.tensor_copy(dstf[:, :, :], idx[:, :, 4:8])
                dve.tensor_copy(dump[:, :, :], eid[:, :, :])
                step(dve.tensor_copy(nxtf[:, :, :], nxt[:, :, :]))
                step(dve.tensor_tensor(same[:, :, :], dstf[:, :, :], nxtf[:, :, :], ALU.is_equal))
                dve.scalar_tensor_tensor(out=lastf[:, :, :], in0=same[:, :, :], scalar=float(g.NP), in1=dstf[:, :, :],
                                         op0=ALU.mult, op1=ALU.add)
                step(dve.scalar_tensor_tensor(out=dump[:, :, :], in0=dump[:, :, :], scalar=float(g.NP), in1=dstf[:, :, :],
                                              op0=ALU.add, op1=ALU.subtract))
                step(dve.tensor_tensor(addf[:, :, :], dump[:, :, :], same[:, :, :], ALU.mult))
                step(dve.tensor_tensor(addf[:, :, :], addf[:, :, :], dstf[:, :, :], ALU.add))
                dve.tensor_copy(idx[:, :, 8:12], lastf[:, :, :])
                dve.tensor_copy(idx[:, :, 12:16], addf[:, :, :]).then_inc(idx_made, 1)


def first_norm(nc, g):
    nb = g.NTN // K
    with Phase(nc, "first_norm_") as m:
        x, h = m.sbs("x", [P, SUB, D]), m.sbs("h", [P, SUB, D])
        stats, mv = m.sbs("stats", [P, SUB, 6]), m.sbs("mv", [P, SUB, 2])
        std, rstd, shift = m.sbs("std", [P, SUB]), m.sbs("rstd", [P, SUB]), m.sbs("shift", [P, SUB])
        eps, zero = m.sb("eps", [P, 1]), m.sb("zero", [P, K * TILE])
        x_in, h_out, h_made = m.sems("x_in"), m.sems("h_out"), m.sems("h_made")
        eps_set, zero_set = m.sem("eps_set"), m.sem("zero_set")
        zeros_out = g.zeros_out
        stats_done, own, mv_done, std_done, rstd_done, shift_done = (
            m.sem(n) for n in ("stats_done", "own", "mv_done", "std_done", "rstd_done", "shift_done"))
        with nc.Block() as block:
            @block.sync
            def _(sp):
                for k in range(K):
                    sp.dma_start(x[k][:, :, :], node_rows(g.x, k)).then_inc(x_in[k], 16)
                with sp.Fori(1, nb) as i:
                    for k in range(K):
                        sp.wait_ge(h_made[k], i)
                        sp.dma_start(node_rows(g.H, (i - 1) * K + k), h[k][:, :, :]).then_inc(h_out[k], 16)
                        sp.dma_start(x[k][:, :, :], node_rows(g.x, i * K + k)).then_inc(x_in[k], 16)
                for k in range(K):
                    sp.wait_ge(h_made[k], nb)
                    sp.dma_start(node_rows(g.H, (nb - 1) * K + k), h[k][:, :, :]).then_inc(h_out[k], 16)
                for k in range(K):
                    sp.wait_ge(h_out[k], 16 * nb)

            @block.gpsimd
            def _(pool):
                pool.memset(zero[:, :], 0.0).then_inc(zero_set, 1)
                pool.wait_ge(zero_set, 1)
                with pool.Fori(0, nb) as i:
                    pool.dma_start(g.AGG[bass.ds(i * (K * TILE), K * TILE), :].rearrange("(p a) d -> p (a d)", p=P),
                                   zero[:, :]).then_inc(zeros_out, 16)
                for i in range(g.NTE // K):
                    pool.dma_start(g.out[g.NP + i * K * TILE:g.NP + (i + 1) * K * TILE, :].rearrange("(p a) d -> p (a d)", p=P),
                                   zero[:, :]).then_inc(zeros_out, 16)
                pool.wait_ge(zeros_out, 16 * (nb + g.NTE // K))

            @block.vector
            def _(dve):
                dve.memset(eps[:, :], EPS).then_inc(eps_set, 1)
                with dve.Fori(0, nb) as i:
                    def scales(k):
                        dve.wait_ge(std_done, i * K + k + 1)
                        dve.reciprocal(rstd[k][:, :], std[k][:, :]).then_inc(rstd_done, 1)
                        dve.wait_ge(rstd_done, i * K + k + 1)
                        dve.scalar_tensor_tensor(out=shift[k][:, :], in0=mv[k][:, :, 0], scalar=-1.0, in1=rstd[k][:, :],
                                                 op0=ALU.mult, op1=ALU.mult).then_inc(shift_done, 1)

                    for k in range(K):
                        dve.wait_ge(x_in[k], (i + 1) * 16)
                        row_stats(dve, x[k], stats[k]).then_inc(stats_done, 1)
                        if k:
                            scales(k - 1)
                        mean_and_variance(dve, stats[k], mv[k], stats_done, i * K + k + 1, own).then_inc(mv_done, 1)
                    scales(K - 1)

            @block.scalar
            def _(act):
                act.wait_ge(eps_set, 1)
                with act.Fori(0, nb) as i:
                    def normalize(k):
                        act.wait_ge(shift_done, i * K + k + 1)
                        act.wait_ge(h_out[k], i * 16)
                        for a in range(SUB):
                            last = act.activation(h[k][:, a, :], x[k][:, a, :], ACT.Relu,
                                                  bias=shift[k][:, a:a + 1], scale=rstd[k][:, a:a + 1])
                        last.then_inc(h_made[k], 1)

                    for k in range(K):
                        act.wait_ge(mv_done, i * K + k + 1)
                        act.activation(std[k][:, :], mv[k][:, :, 1], ACT.Sqrt, bias=eps[:, :]).then_inc(std_done, 1)
                        if k:
                            normalize(k - 1)
                    normalize(K - 1)


def wait_alone(eng, sem, value, own):
    eng.wait_ge(sem, value)
    eng.sem_inc(own, 1)


def gather(pool, out, table, index):
    return pool.indirect_dma_start(out=out, out_offset=None, in_=table,
                                   in_offset=bass.IndirectOffsetOnAxis(ap=index, axis=0))


def scatter_last(pool, table, index, rows, bound):
    return pool.indirect_dma_start(out=table, out_offset=bass.IndirectOffsetOnAxis(ap=index, axis=0),
                                   in_=rows, in_offset=None, bounds_check=bound, oob_is_err=False)


def make_identity(pool, ident, made, cleared):
    pool.memset(ident[:, :], 0.0).then_inc(cleared, 1)
    pool.wait_ge(cleared, 1)
    pool.affine_select(out=ident[:, :], in_=ident[:, :], compare_op=ALU.not_equal, fill=1.0, base=0,
                       pattern=[[-1, P]], channel_multiplier=1).then_inc(made, 1)


def gine_edges(nc, g):
    nb = g.NTE // K
    with Phase(nc, "gine_edges_") as m:
        ident = m.sb("ident", [P, P])
        idx = m.sbs("idx", [P, 16], I32)
        hs, ea, msg = m.sbs("hs", [P, SUB, D]), m.sbs("ea", [P, SUB, D]), m.sbs("msg", [P, SUB, D])
        keep, msgT, sumT, rows = (m.sbs(n, [P, TILE]) for n in ("keep", "msgT", "sumT", "rows"))
        turned = [m.ps(f"turned{j}", [P, TILE]) for j in range(2)]
        back = [m.ps(f"back{j}", [P, TILE]) for j in range(2)]
        idx_in, tile_in, own = m.sems("idx_in"), m.sems("tile_in"), m.sem("own")
        hs_in, agg_out = g.gathered, g.scattered
        hs0, agg0 = g.start(hs_in, nb * 64), g.start(agg_out, nb * 64)
        cleared, ident_made, tail_set = m.sem("cleared"), m.sem("ident_made"), m.sem("tail_set")
        msg_made, msgT_psum, msgT_made, scanned, back_psum, rows_made = (
            m.sem(n) for n in ("msg_made", "msgT_psum", "msgT_made", "scanned", "back_psum", "rows_made"))
        with nc.Block() as block:
            @block.sync
            def _(sp):
                def load(k, i):
                    sp.dma_start(idx[k][:, :], g.IDX[bass.ds(i * K + k, 1), :, :].rearrange("t p s -> (t p) s")).then_inc(idx_in[k], 16)
                    sp.dma_start(ea[k][:, :, :], edge_rows(g.ea, i * K + k)).then_inc(tile_in[k], 16)
                    sp.dma_start(keep[k][:, :], edge_span(g.KEEP, i * K + k, P)).then_inc(tile_in[k], 16)

                for k in range(K):
                    load(k, 0)
                if nb > 1:
                    with sp.Fori(1, nb) as i:
                        for k in range(K):
                            sp.wait_ge(agg_out[k], i * 64 + agg0)
                            load(k, i)

            @block.gpsimd
            def _(pool):
                make_identity(pool, ident, ident_made, cleared)

                def gather_tile(k, i):
                    wait_alone(pool, idx_in[k], (i + 1) * 16, own)
                    for s in range(SUB):
                        gather(pool, hs[k][:, s, :], g.H[:, :], idx[k][:, s:s + 1]).then_inc(hs_in[k], 16)

                def body(i, more):
                    for k in range(K):
                        wait_alone(pool, rows_made, i * K + k + 1, own)
                        for s in range(SUB):
                            scatter_last(pool, g.AGG[:, :], idx[k][:, 8 + s:9 + s], rows[k][:, s * P:(s + 1) * P],
                                         g.NP - 1).then_inc(agg_out[k], 16)
                        if more and k >= BEHIND:
                            gather_tile(k - BEHIND, i + 1)
                    if more:
                        for k in range(K - BEHIND, K):
                            gather_tile(k, i + 1)

                for k in range(K):
                    gather_tile(k, 0)
                if nb > 1:
                    with pool.Fori(0, nb - 1) as i:
                        body(i, True)
                body(nb - 1, False)
                for k in range(K):
                    pool.wait_ge(agg_out[k], nb * 64 + agg0)

            @block.vector
            def _(dve):
                dve.memset(sumT[K - 1][:, TILE - 1:TILE], 0.0).then_inc(tail_set, 1)
                dve.wait_ge(tail_set, 1)
                with dve.Fori(0, nb) as i:
                    def add(k):
                        dve.wait_ge(hs_in[k], i * 64 + (64 + hs0))
                        dve.wait_ge(tile_in[k], (i + 1) * 32)
                        dve.tensor_tensor(msg[k][:, :, :], hs[k][:, :, :], ea[k][:, :, :], ALU.add).then_inc(msg_made, 1)

                    def scan(k):
                        dve.wait_ge(msgT_made, i * K + k + 1)
                        dve.wait_ge(scanned, i * K + k)
                        dve.tensor_tensor_scan(sumT[k][:, :], keep[k][:, :], msgT[k][:, :],
                                               sumT[k - 1][:, TILE - 1:TILE], ALU.mult, ALU.add).then_inc(scanned, 1)

                    for k in range(K):
                        add(k)
                        if k:
                            scan(k - 1)
                    scan(K - 1)

            @block.tensor
            def _(pe):
                pe.wait_ge(ident_made, 1)
                with pe.Fori(0, nb) as i:
                    def turn(k):
                        pe.wait_ge(msg_made, i * K + k + 1)
                        if k >= 2:
                            pe.wait_ge(msgT_made, i * K + k - 1)
                        else:
                            pe.wait_ge(msgT_made, i * K)
                        for s in range(SUB):
                            last = pe.transpose(turned[k % 2][:, s * P:(s + 1) * P], msg[k][:, s, :], ident[:, :])
                        last.then_inc(msgT_psum, 1)

                    def turn_back(k):
                        pe.wait_ge(scanned, i * K + k + 1)
                        if k >= 2:
                            pe.wait_ge(rows_made, i * K + k - 1)
                        else:
                            pe.wait_ge(rows_made, i * K)
                        for s in range(SUB):
                            last = pe.transpose(back[k % 2][:, s * P:(s + 1) * P], sumT[k][:, s * P:(s + 1) * P], ident[:, :])
                        last.then_inc(back_psum, 1)

                    for k in range(K):
                        turn(k)
                        if k:
                            turn_back(k - 1)
                    turn_back(K - 1)

            @block.scalar
            def _(act):
                with act.Fori(0, nb) as i:
                    def copy_back(k):
                        act.wait_ge(back_psum, i * K + k + 1)
                        act.wait_ge(agg_out[k], i * 64 + agg0)
                        act.activation(rows[k][:, :], back[k % 2][:, :], ACT.Copy).then_inc(rows_made, 1)

                    for k in range(K):
                        act.wait_ge(msgT_psum, i * K + k + 1)
                        act.activation(msgT[k][:, :], turned[k % 2][:, :], ACT.Relu).then_inc(msgT_made, 1)
                        if k:
                            copy_back(k - 1)
                    copy_back(K - 1)


class Norm:

    def __init__(self, m, name):
        self.stats, self.mv = m.sbs(f"{name}_stats", [P, SUB, 6]), m.sbs(f"{name}_mv", [P, SUB, 2])
        self.std, self.rstd = m.sbs(f"{name}_std", [P, SUB]), m.sbs(f"{name}_rstd", [P, SUB])
        self.shift = m.sbs(f"{name}_shift", [P, SUB])
        self.stats_done, self.own, self.mv_done = (m.sem(f"{name}_{n}") for n in ("stats_done", "own", "mv_done"))
        self.std_done, self.rstd_done, self.shift_done = (m.sem(f"{name}_{n}") for n in ("std_done", "rstd_done", "shift_done"))

    def take_stats(self, dve, x, k):
        for a in range(SUB):
            last = dve.bn_stats(out=self.stats[k][:, a, :], in_=x[:, a, :])
        last.then_inc(self.stats_done, 1)

    def moments(self, dve, k, done):
        dve.wait_ge(self.stats_done, done)
        dve.sem_inc(self.own, 1)
        for a in range(SUB):
            last = dve.bn_aggr(out=self.mv[k][:, a, :], in_=self.stats[k][:, a, :])
        last.then_inc(self.mv_done, 1)

    def root(self, act, k, done, eps):
        act.wait_ge(self.mv_done, done)
        act.activation(self.std[k][:, :], self.mv[k][:, :, 1], ACT.Sqrt, bias=eps[:, :]).then_inc(self.std_done, 1)

    def scales(self, dve, k, done):
        dve.wait_ge(self.std_done, done)
        dve.reciprocal(self.rstd[k][:, :], self.std[k][:, :]).then_inc(self.rstd_done, 1)
        dve.wait_ge(self.rstd_done, done)
        dve.scalar_tensor_tensor(out=self.shift[k][:, :], in0=self.mv[k][:, :, 0], scalar=-1.0, in1=self.rstd[k][:, :],
                                 op0=ALU.mult, op1=ALU.mult).then_inc(self.shift_done, 1)

    def apply(self, act, out, x, k, func):
        for a in range(SUB):
            last = act.activation(out[:, a, :], x[:, a, :], func,
                                  bias=self.shift[k][:, a:a + 1], scale=self.rstd[k][:, a:a + 1])
        return last


def slot_tiles(slot):
    return (K + 1 - slot) // 2


def run_bodies(eng, nb, body):
    with eng.Fori(0, nb) as i:
        body(i)


def stream(sp, nb, load, store, free):
    for k in range(K):
        load(k, 0)
    if nb > 1:
        with sp.Fori(1, nb) as i:
            for k in range(K):
                free(k, i)
                store(k, i - 1)
                load(k, i)
    for k in range(K):
        free(k, nb)
        store(k, nb - 1)


def gine_mlp(nc, g):
    nb = g.NTN // K
    with Phase(nc, "gine_mlp_") as m:
        ident = m.sb("ident", [P, P])
        w1, w2, b1, b2 = m.sb("w1", [D, D]), m.sb("w2", [D, D]), m.sb("b1", [D, 1]), m.sb("b2", [D, 1])
        gamma, beta, eps = m.sb("gamma", [D, 1]), m.sb("beta", [D, 1]), m.sb("eps", [P, 1])
        h, agg, s = m.sbs("h", [P, SUB, D]), m.sbs("agg", [P, SUB, D]), m.sbs("s", [P, SUB, D])
        sT, hidT, yT = m.sbs("sT", [P, TILE]), m.sbs("hidT", [P, TILE]), m.sbs("yT", [P, TILE])
        y_stats, y_mv, y_std = m.sb("y_stats", [P, g.NTN, 6]), m.sb("y_mv", [P, 2]), m.sb("y_std", [P, 1])
        turned, hid, y = ([m.ps(f"{n}{j}", [P, TILE]) for j in range(2)] for n in ("turned", "hid", "y"))
        tile_in, y_out = m.sems("tile_in"), m.sems("y_out")
        cleared, ident_made, weights_in, eps_set = (m.sem(n) for n in ("cleared", "ident_made", "weights_in", "eps_set"))
        s_made, turned_done, sT_made, hid_done, hidT_made, y_done, yT_made, y_measured = (
            m.sem(n) for n in ("s_made", "turned_done", "sT_made", "hid_done", "hidT_made", "y_done", "yT_made", "y_measured"))
        own, steps, y_root, mv_ready = m.sem("own"), m.sem("steps"), m.sem("y_root"), m.sem("mv_ready")
        with nc.Block() as block:
            @block.sync
            def _(sp):
                for dst, src in ((w1, g.w1T), (w2, g.w2T), (b1, g.b1), (b2, g.b2), (gamma, g.gamma), (beta, g.beta)):
                    sp.dma_start(dst[:, :], src).then_inc(weights_in, 16)

                def load(k, i):
                    sp.dma_start(h[k][:, :, :], node_rows(g.H, i * K + k)).then_inc(tile_in[k], 16)
                    sp.dma_start(agg[k][:, :, :], node_rows(g.AGG, i * K + k)).then_inc(tile_in[k], 16)

                def store(k, i):
                    sp.dma_start(g.YT[bass.ds(i * K + k, 1), :, :].rearrange("t p j -> (t p) j"), yT[k][:, :]).then_inc(y_out[k], 16)

                stream(sp, nb, load, store, lambda k, i: sp.wait_ge(yT_made, (i - 1) * K + k + 1))
                for k in range(K):
                    sp.wait_ge(y_out[k], 16 * nb)

            @block.gpsimd
            def _(pool):
                make_identity(pool, ident, ident_made, cleared)

            @block.vector
            def _(dve):
                dve.memset(eps[:, :], EPS).then_inc(eps_set, 1)

                def body(i):
                    def measure(k):
                        dve.wait_ge(yT_made, i * K + k + 1)
                        dve.bn_stats(out=y_stats[:, bass.ds(i * K + k, 1), :].rearrange("p t c -> p (t c)"), in_=yT[k][:, :]).then_inc(y_measured, 1)

                    for k in range(K):
                        dve.wait_ge(tile_in[k], (i + 1) * 32)
                        dve.tensor_tensor(s[k][:, :, :], h[k][:, :, :], agg[k][:, :, :], ALU.add).then_inc(s_made, 1)
                        if k >= 3:
                            measure(k - 3)
                    for k in range(K - 3, K):
                        measure(k)

                run_bodies(dve, nb, body)
                dve.wait_ge(y_measured, g.NTN)
                used = g.NTN
                for k in range(K):
                    t = g.NTN - K + k
                    real = min(max(g.N - t * TILE, 0), TILE) // SUB
                    if real == 0:
                        used = min(used, t)
                    elif real < P:
                        dve.bn_stats(out=y_stats[:, t, :], in_=yT[k][:, :].rearrange("p (a j) -> p a j", a=SUB)[:, :, 0:real]).then_inc(own, 1)
                        dve.wait_ge(own, 1)
                dve.bn_aggr(out=y_mv[:, :], in_=y_stats[:, 0:used, :].rearrange("p t c -> p (t c)")).then_inc(mv_ready, 1)
                dve.wait_ge(y_root, 1)
                dve.wait_ge(weights_in, 6 * 16)
                dve.reciprocal(y_std[:, :], y_std[:, :]).then_inc(steps, 1)
                dve.wait_ge(steps, 1)
                dve.tensor_tensor(g.bn_scale[:, :], y_std[:, :], gamma[:, :], ALU.mult).then_inc(steps, 1)
                dve.wait_ge(steps, 2)
                dve.tensor_tensor(g.bn_shift[:, :], y_mv[:, 0:1], g.bn_scale[:, :], ALU.mult).then_inc(steps, 1)
                dve.wait_ge(steps, 3)
                dve.tensor_tensor(g.bn_shift[:, :], beta[:, :], g.bn_shift[:, :], ALU.subtract)

            @block.tensor
            def _(pe):
                pe.wait_ge(ident_made, 1)
                pe.wait_ge(weights_in, 6 * 16)

                def body(i):
                    def turn(k):
                        pe.wait_ge(s_made, i * K + k + 1)
                        pe.wait_ge(sT_made, i * K + max(k - 1, 0))
                        for a in range(SUB):
                            last = pe.transpose(turned[k % 2][:, a * P:(a + 1) * P], s[k][:, a, :], ident[:, :])
                        last.then_inc(turned_done, 1)

                    def first(k):
                        pe.wait_ge(sT_made, i * K + k + 1)
                        pe.wait_ge(hidT_made, i * K + max(k - 1, 0))
                        pe.matmul(hid[k % 2][:, :], w1[:, :], sT[k][:, :], start=True, stop=True).then_inc(hid_done, 1)

                    def second(k):
                        pe.wait_ge(hidT_made, i * K + k + 1)
                        pe.wait_ge(yT_made, i * K + max(k - 1, 0))
                        pe.matmul(y[k % 2][:, :], w2[:, :], hidT[k][:, :], start=True, stop=True).then_inc(y_done, 1)

                    for k in range(K + 2):
                        if k < K:
                            turn(k)
                        if 1 <= k <= K:
                            first(k - 1)
                        if k >= 2:
                            second(k - 2)

                run_bodies(pe, nb, body)

            @block.scalar
            def _(act):
                act.wait_ge(weights_in, 6 * 16)

                def body(i):
                    for k in range(K + 2):
                        if k < K:
                            act.wait_ge(turned_done, i * K + k + 1)
                            act.activation(sT[k][:, :], turned[k % 2][:, :], ACT.Copy).then_inc(sT_made, 1)
                        if 1 <= k <= K:
                            act.wait_ge(hid_done, i * K + k)
                            act.activation(hidT[k - 1][:, :], hid[(k - 1) % 2][:, :], ACT.Relu, bias=b1[:, :]).then_inc(hidT_made, 1)
                        if k >= 2:
                            act.wait_ge(y_done, i * K + k - 1)
                            act.wait_ge(y_out[k - 2], i * 16)
                            act.wait_ge(y_measured, i * K)
                            act.activation(yT[k - 2][:, :], y[(k - 2) % 2][:, :], ACT.Identity, bias=b2[:, :]).then_inc(yT_made, 1)

                run_bodies(act, nb, body)
                act.wait_ge(eps_set, 1)
                act.wait_ge(mv_ready, 1)
                act.activation(y_std[:, :], y_mv[:, 1:2], ACT.Sqrt, bias=eps[:, :]).then_inc(y_root, 1)


def past(eng, sem, value):
    if not isinstance(value, int) or value > 0:
        eng.wait_ge(sem, value)


def pipeline(eng, bodies, tiles, steps):
    def at(t, i, first, last):
        for lag, step in steps:
            k = t - lag
            if 0 <= k < tiles:
                step(k, i)
            elif k < 0 and not first:
                step(tiles + k, i - 1)

    for t in range(tiles):
        at(t, 0, True, bodies == 1)
    if bodies > 1:
        with eng.Fori(1, bodies) as i:
            for t in range(tiles):
                at(t, i, False, False)
    for t in range(tiles, tiles + max(lag for lag, _ in steps)):
        at(t, bodies - 1, True, True)


def turns(k, i):
    return i * (NB // RING) + k // RING


def node_stream(sp, nb, load, freed, store, lag):
    def load_next(k, i):
        if k < NB - RING or not isinstance(i, int) or i < nb - 1:
            freed(k, i)
            k, i = k + RING, i
            load(k % NB, i + k // NB)

    for k in range(RING):
        load(k, 0)
    for t in range(NB):
        load_next(t, 0)
        if t >= lag:
            store(t - lag, 0)
    if nb > 2:
        with sp.Fori(1, nb - 1) as i:
            for t in range(NB):
                load_next(t, i)
                store((t - lag) % NB, i + (t - lag) // NB)
    for t in range(0 if nb > 1 else NB, NB + lag):
        if t < NB - RING:
            load_next(t, nb - 1)
        store((t - lag) % NB, nb - 1 + (t - lag) // NB)


def gine_finish(nc, g):
    nb = g.NTN // NB
    with Phase(nc, "gine_finish_") as m:
        ident, eps = m.sb("ident", [P, P]), m.sb("eps", [P, 1])
        x, yT, bT = m.sbs("x", [P, SUB, D]), m.sbs("yT", [P, TILE]), m.sbs("bT", [P, TILE])
        x1, h1 = m.sbs("x1", [P, SUB, D]), m.sbs("h1", [P, SUB, D])
        rows = [m.ps(f"rows{j}", [P, SUB, D]) for j in range(RING)]
        norm = Norm(m, "norm")
        tile_in, out = m.sems("tile_in"), m.sems("out")
        cleared, ident_made, eps_set = (m.sem(n) for n in ("cleared", "ident_made", "eps_set"))
        bT_made, rows_done, x1_made, h1_made = (m.sem(n) for n in ("bT_made", "rows_done", "x1_made", "h1_made"))
        with nc.Block() as block:
            @block.sync
            def _(sp):
                def load(k, i):
                    r, n = k % RING, i * NB + k
                    sp.dma_start(x[r][:, :, :], node_rows(g.x, n)).then_inc(tile_in[r], 16)
                    sp.dma_start(yT[r][:, :], g.YT[bass.ds(n, 1), :, :].rearrange("t p j -> (t p) j")).then_inc(tile_in[r], 16)

                def freed(k, i):
                    sp.wait_ge(x1_made, i * NB + k + 1)

                def store(k, i):
                    r, n = k % RING, i * NB + k
                    sp.wait_ge(h1_made, n + 1)
                    sp.dma_start(node_rows(g.X, n), x1[r][:, :, :]).then_inc(out[r], 16)
                    sp.dma_start(node_rows(g.H, n), h1[r][:, :, :]).then_inc(out[r], 16)

                node_stream(sp, nb, load, freed, store, 4)
                for r in range(RING):
                    sp.wait_ge(out[r], 32 * turns(r, nb))

            @block.gpsimd
            def _(pool):
                make_identity(pool, ident, ident_made, cleared)

            @block.tensor
            def _(pe):
                pe.wait_ge(ident_made, 1)

                def turn(k, i):
                    r, n = k % RING, i * NB + k
                    pe.wait_ge(bT_made, n + 1)
                    past(pe, x1_made, n + 1 - RING)
                    for a in range(SUB):
                        last = pe.transpose(rows[r][:, a, :], bT[r][:, a * P:(a + 1) * P], ident[:, :])
                    last.then_inc(rows_done, 1)

                pipeline(pe, nb, NB, [(0, turn)])

            @block.vector
            def _(dve):
                dve.memset(eps[:, :], EPS).then_inc(eps_set, 1)

                def add(k, i):
                    r = k % RING
                    dve.wait_ge(rows_done, i * NB + k + 1)
                    past(dve, out[r], 32 * turns(k, i))
                    dve.tensor_tensor(x1[r][:, :, :], rows[r][:, :, :], x[r][:, :, :], ALU.add).then_inc(x1_made, 1)

                def take_stats(k, i):
                    dve.wait_ge(x1_made, i * NB + k + 1)
                    norm.take_stats(dve, x1[k % RING], k % RING)

                pipeline(dve, nb, NB, [
                    (0, add),
                    (1, lambda k, i: norm.moments(dve, k % RING, i * NB + k + 1)),
                    (3, lambda k, i: norm.scales(dve, k % RING, i * NB + k + 1)),
                    (0, take_stats)])

            @block.scalar
            def _(act):
                act.wait_ge(eps_set, 1)

                def batch_norm(k, i):
                    r, n = k % RING, i * NB + k
                    act.wait_ge(tile_in[r], 32 * (turns(k, i) + 1))
                    past(act, rows_done, n + 1 - RING)
                    act.activation(bT[r][:, :], yT[r][:, :], ACT.Identity, bias=g.bn_shift[:, :], scale=g.bn_scale[:, :]).then_inc(bT_made, 1)

                def normalize(k, i):
                    r = k % RING
                    act.wait_ge(norm.shift_done, i * NB + k + 1)
                    past(act, out[r], 32 * turns(k, i))
                    norm.apply(act, h1[r], x1[r], r, ACT.Relu).then_inc(h1_made, 1)

                pipeline(act, nb, NB, [
                    (0, batch_norm),
                    (3, lambda k, i: norm.root(act, k % RING, i * NB + k + 1, eps)),
                    (5, normalize)])


def conv_logits(nc, g, layer):
    nb = g.NTE // K
    with Phase(nc, f"conv_logits{layer}_") as m:
        ident, wr, att = m.sb("ident", [P, P]), m.sb("wr", [D, H * D]), m.sb("att", [D, H, 32])
        idx = m.sbs("idx", [P, 16], I32)
        hs, hd, hdT = m.sbs("hs", [P, SUB, D]), m.sbs("hd", [P, SUB, D]), m.sbs("hdT", [P, TILE], n=2)
        sloped, leaky = m.sbs("sloped", [P, TILE], n=2 * H), m.sbs("leaky", [P, TILE], n=2 * H)
        logit = [m.sbs(f"logit{j}_", [P, TILE], n=2) for j in range(2)]
        hsT_ps, hdT_ps = m.ps("hsT_ps", [P, TILE]), m.ps("hdT_ps", [P, TILE])
        z = [m.ps(f"z{h}", [P, TILE]) for h in range(H)]
        dots = [m.ps(f"dots{j}", [P, TILE]) for j in range(2)]
        idx_in, rows_in, own = m.sems("idx_in"), g.gathered, m.sem("own")
        rows0 = g.start(rows_in, nb * 128)
        logit_out = [m.sems(f"logit_out{j}_", 2) for j in range(2)]
        cleared, ident_made, weights_in, att_set, weights_made = (
            m.sem(n) for n in ("cleared", "ident_made", "weights_in", "att_set", "weights_made"))
        turned_done, hdT_made, diff_made, mean_step = (m.sem(n) for n in ("turned_done", "hdT_made", "diff_made", "mean_step"))
        z_done, sloped_made = ([m.sem(f"{n}{j}") for j in range(2)] for n in ("z_done", "sloped_made"))
        leaky_made, dots_done, logit_made = ([m.sem(f"{n}{j}") for j in range(2)] for n in ("leaky_made", "dots_done", "logit_made"))
        with nc.Block() as block:
            @block.sync
            def _(sp):
                wl_in, wr_in, att_in = g.conv_weights[layer]
                sp.dma_start(g.wl[:, :], wl_in).then_inc(weights_in, 16)
                sp.dma_start(wr[:, :], wr_in).then_inc(weights_in, 16)
                sp.wait_ge(att_set, 1)
                with nc.allow_non_contiguous_dma("a column of each head"):
                    sp.dma_start(att[:, :, 0:1], att_in.rearrange("d (h o) -> d h o", o=1)).then_inc(weights_in, 16)

                def load(k, i):
                    sp.dma_start(idx[k][:, :], g.IDX[bass.ds(i * K + k, 1), :, :].rearrange("t p s -> (t p) s")).then_inc(idx_in[k], 16)

                def store(j, k, i, slot):
                    sp.wait_ge(logit_made[j], i * K + k + 1)
                    sp.dma_start(g.LOGIT[j][:, bass.ds((i * K + k) * TILE, TILE)], logit[j][slot][0:P:32, :]).then_inc(logit_out[j][slot], 16)

                def body(i, more):
                    for k in range(K):
                        store(0, k, i, k % 2)
                        store(1, k, i, k % 2)
                        if more:
                            load(k, i + 1)

                for k in range(K):
                    load(k, 0)
                if nb > 1:
                    with sp.Fori(0, nb - 1) as i:
                        body(i, True)
                body(nb - 1, False)
                for j in range(2):
                    for slot in range(2):
                        sp.wait_ge(logit_out[j][slot], 16 * nb * slot_tiles(slot))

            @block.gpsimd
            def _(pool):
                make_identity(pool, ident, ident_made, cleared)

                def gather_tile(k, i):
                    wait_alone(pool, idx_in[k], (i + 1) * 16, own)
                    for s in range(SUB):
                        gather(pool, hd[k][:, s, :], g.H[:, :], idx[k][:, 4 + s:5 + s]).then_inc(rows_in[k], 16)
                        gather(pool, hs[k][:, s, :], g.H[:, :], idx[k][:, s:s + 1]).then_inc(rows_in[k], 16)

                for k in range(K):
                    gather_tile(k, 0)
                if nb > 1:
                    with pool.Fori(1, nb) as i:
                        for k in range(K):
                            pool.wait_ge(turned_done, (i - 1) * K + k + 1)
                            gather_tile(k, i)

            @block.tensor
            def _(pe):
                pe.wait_ge(ident_made, 1)
                pe.wait_ge(weights_made, 1)

                def body(i):
                    n = i * K

                    def turn(k):
                        pe.wait_ge(rows_in[k], i * 128 + (128 + rows0))
                        pe.wait_ge(diff_made, n + k)
                        for s in range(SUB):
                            pe.transpose(hdT_ps[:, s * P:(s + 1) * P], hd[k][:, s, :], ident[:, :])
                        for s in range(SUB):
                            last = pe.transpose(hsT_ps[:, s * P:(s + 1) * P], hs[k][:, s, :], ident[:, :])
                        last.then_inc(turned_done, 1)

                    def dot(j, k):
                        pe.wait_ge(leaky_made[j], H * n + H * (k + 1))
                        pe.wait_ge(logit_made[j], n + k)
                        for h in range(H):
                            last = pe.matmul(dots[j][32 * h:32 * h + 32, :], att[:, h, :], leaky[H * j + h][:, :],
                                             start=True, stop=True, tile_position=(0, 32 * h))
                        last.then_inc(dots_done[j], 1)

                    turn(0)
                    for k in range(K):
                        pe.wait_ge(hdT_made, n + k + 1)
                        pe.wait_ge(leaky_made[1], H * n + H * k)
                        for h in range(H):
                            pe.matmul(z[h][:, :], g.wsum[:, h * D:(h + 1) * D], hdT[k % 2][:, :],
                                      start=True, stop=True).then_inc(z_done[0], 1)
                        if k:
                            dot(1, k - 1)
                        if k + 1 < K:
                            turn(k + 1)
                        pe.wait_ge(diff_made, n + k + 1)
                        for h in range(H):
                            pe.wait_ge(leaky_made[0], H * n + H * k + h + 1)
                            pe.matmul(z[h][:, :], g.wl[:, h * D:(h + 1) * D], g.diffT[:, bass.ds((n + k) * TILE, TILE)],
                                      start=False, stop=True, skip_group_check=True).then_inc(z_done[1], 1)
                        dot(0, k)
                    dot(1, K - 1)

                run_bodies(pe, nb, body)

            @block.scalar
            def _(act):
                def body(i):
                    n = i * K

                    def copy_dst(k):
                        act.wait_ge(turned_done, n + k + 1)
                        act.activation(hdT[k % 2][:, :], hdT_ps[:, :], ACT.Copy).then_inc(hdT_made, 1)

                    def slope(j, k):
                        for h in range(H):
                            act.wait_ge(z_done[j], H * n + H * k + h + 1)
                            act.activation(sloped[H * j + h][:, :], z[h][:, :], ACT.Copy, scale=SLOPE).then_inc(sloped_made[j], 1)

                    def copy_dots(j, k):
                        act.wait_ge(dots_done[j], n + k + 1)
                        slot = k % 2
                        act.wait_ge(logit_out[j][slot], i * (16 * slot_tiles(slot)) + 16 * (k // 2))
                        act.activation(logit[j][slot][:, :], dots[j][:, :], ACT.Copy).then_inc(logit_made[j], 1)

                    copy_dst(0)
                    for k in range(K):
                        slope(0, k)
                        if k:
                            copy_dots(1, k - 1)
                        if k + 1 < K:
                            copy_dst(k + 1)
                        slope(1, k)
                        copy_dots(0, k)
                    copy_dots(1, K - 1)

                run_bodies(act, nb, body)

            @block.vector
            def _(dve):
                dve.memset(att[:, :, :], 0.0).then_inc(att_set, 1)
                dve.wait_ge(weights_in, 48)
                dve.tensor_tensor(g.wmean[:, :], g.wl[:, 0:D], g.wl[:, D:2 * D], ALU.add).then_inc(mean_step, 1)
                for h in range(2, H):
                    dve.wait_ge(mean_step, h - 1)
                    dve.tensor_tensor(g.wmean[:, :], g.wmean[:, :], g.wl[:, h * D:(h + 1) * D], ALU.add).then_inc(mean_step, 1)
                dve.wait_ge(mean_step, H - 1)
                dve.tensor_scalar(g.wmean[:, :], g.wmean[:, :], 1.0 / H, None, ALU.mult)
                dve.tensor_tensor(g.wsum[:, :], g.wl[:, :], wr[:, :], ALU.add).then_inc(weights_made, 1)

                def body(i):
                    n = i * K

                    def diff(k):
                        dve.wait_ge(hdT_made, n + k + 1)
                        dve.tensor_tensor(g.diffT[:, bass.ds((n + k) * TILE, TILE)], hsT_ps[:, :], hdT[k % 2][:, :],
                                          ALU.subtract).then_inc(diff_made, 1)

                    def leak(j, k):
                        for h in range(H):
                            dve.wait_ge(sloped_made[j], H * n + H * k + h + 1)
                            if h == 0:
                                dve.wait_ge(dots_done[j], n + k)
                            dve.tensor_tensor(leaky[H * j + h][:, :], z[h][:, :], sloped[H * j + h][:, :],
                                              ALU.max).then_inc(leaky_made[j], 1)

                    diff(0)
                    for k in range(K):
                        leak(0, k)
                        if k + 1 < K:
                            diff(k + 1)
                        leak(1, k)

                run_bodies(dve, nb, body)


def edge_softmax(nc, g, layer, self_loops, share):
    J = g.EP // CH
    with Phase(nc, f"edge_softmax{layer}_") as m:
        ident, zero = m.sb("ident", [P, P]), m.sb("zero", [P, J])
        e, es, ex, exs, top, run, total, weight = (m.sb(n, [P, J]) for n in ("e", "es", "ex", "exs", "top", "run", "total", "weight"))
        keep = [m.sb(f"keep{b}", [P, J]) for b in range(2)]
        cut = [m.sb(f"cut{b}", [P, J]) for b in range(2)]
        lead = [m.sb(f"lead{b}", [P, J]) for b in range(2)]
        leadcut = [m.sb(f"leadcut{b}", [P, J]) for b in range(2)]
        whole, wholecut = m.sb("whole", [1, 2, P]), m.sb("wholecut", [1, 2, P])
        ends, carry = m.sb("ends", [1, P + 2]), m.sb("carry", [P, 1])
        row, col = m.ps("row", [1, P]), m.ps("col", [P, 1])
        loaded, cleared, ident_made, steps, turn_done, diff_done, exp_done, asked, alpha_made, alpha_out = (
            m.sem(n) for n in ("loaded", "cleared", "ident_made", "steps", "turn_done", "diff_done", "exp_done", "asked", "alpha_made", "alpha_out"))
        n_loads = 8 + 1 + self_loops
        flat = lambda table: table.rearrange("h (c j) -> (h c) j", j=J)
        end = lambda b: 0 if b else J - 1
        with nc.Block() as block:
            @block.sync
            def _(sp):
                for b, table in enumerate((g.KEEP, g.KEEPN)):
                    for h in range(H):
                        sp.dma_start(keep[b][CH * h:CH * (h + 1), :], table.rearrange("o (c j) -> (o c) j", j=J)).then_inc(loaded, 16)
                sp.dma_start(e[:, :], flat(g.LOGIT[1])).then_inc(loaded, 16)
                if self_loops:
                    sp.dma_start(es[:, :], flat(g.LOGIT[0])).then_inc(loaded, 16)
                sp.wait_ge(alpha_made, 1)
                sp.dma_start(flat(g.ALPHA), weight[:, :]).then_inc(alpha_out, 16)
                sp.wait_ge(alpha_out, 16)

            @block.gpsimd
            def _(pool):
                make_identity(pool, ident, ident_made, cleared)

            @block.vector
            def _(dve):
                count, turned = [0], [0]

                def step(instruction):
                    count[0] += 1
                    instruction.then_inc(steps, 1)
                    dve.wait_ge(steps, count[0])

                def turn():
                    dve.sem_inc(asked, 1)
                    turned[0] += 1
                    dve.wait_ge(turn_done, turned[0])

                order = lambda x, b: x[:, ::-1] if b else x[:, :]
                def join(b, local, op_carry, op_in, out):
                    turn()
                    inner = ends[:, 1:P + 1]
                    data0 = wholecut[:, b, :] if op_carry == ALU.add else whole[:, b, :]
                    step(dve.tensor_tensor_scan(inner[:, ::-1] if b else inner, data0[:, ::-1] if b else data0,
                                                row[:, ::-1] if b else row[:, :], -BIG if op_carry == ALU.add else 0.0, op_carry, op_in))
                    turn()
                    step(dve.tensor_copy(carry[:, :], col[:, :]))
                    step(dve.scalar_tensor_tensor(out=out[:, :], in0=(leadcut if op_carry == ALU.add else lead)[b][:, :], scalar=carry[:, :],
                                                  in1=local[:, :], op0=op_carry, op1=op_in))

                step(dve.memset(zero[:, :], 0.0))
                step(dve.memset(ends[:, :], 0.0))
                dve.wait_ge(loaded, 16 * n_loads)
                for b in range(2):
                    dve.tensor_scalar(cut[b][:, :], keep[b][:, :], -1.0, BIG, ALU.add, ALU.mult)
                    step(dve.tensor_tensor_scan(order(lead[b], b), order(keep[b], b), zero[:, :], 1.0, ALU.mult, ALU.add))
                    dve.tensor_scalar(leadcut[b][:, :], lead[b][:, :], -1.0, BIG, ALU.add, ALU.mult)
                    turn()
                    step(dve.tensor_copy(whole[:, b, :], row[:, :]))
                    step(dve.tensor_scalar(wholecut[:, b, :], whole[:, b, :], -1.0, BIG, ALU.add, ALU.mult))
                if self_loops:
                    step(dve.tensor_tensor(top[:, :], e[:, :], es[:, :], ALU.max))
                    most = top
                else:
                    most = e
                step(dve.tensor_tensor_scan(run[:, :], cut[0][:, :], most[:, :], -BIG, ALU.add, ALU.max))
                join(0, run, ALU.add, ALU.max, total)
                step(dve.tensor_tensor_scan(order(run, 1), order(cut[1], 1), order(total, 1), -BIG, ALU.add, ALU.max))
                join(1, run, ALU.add, ALU.max, top)
                if self_loops:
                    dve.tensor_tensor(es[:, :], es[:, :], top[:, :], ALU.subtract)
                dve.tensor_tensor(e[:, :], e[:, :], top[:, :], ALU.subtract).then_inc(diff_done, 1)
                dve.wait_ge(exp_done, 1 + self_loops)
                step(dve.tensor_tensor_scan(run[:, :], keep[0][:, :], ex[:, :], 0.0, ALU.mult, ALU.add))
                join(0, run, ALU.mult, ALU.add, total)
                step(dve.scalar_tensor_tensor(out=total[:, :], in0=keep[1][:, :], scalar=-1.0, in1=total[:, :],
                                              op0=ALU.add, op1=ALU.mult))
                step(dve.tensor_tensor_scan(order(run, 1), order(keep[1], 1), order(total, 1), 0.0, ALU.mult, ALU.add))
                join(1, run, ALU.mult, ALU.add, total)
                if self_loops:
                    step(dve.tensor_tensor(total[:, :], exs[:, :], total[:, :], ALU.subtract))
                else:
                    step(dve.tensor_scalar(total[:, :], total[:, :], -1.0, None, ALU.mult))
                step(dve.reciprocal(total[:, :], total[:, :]))
                dve.scalar_tensor_tensor(out=weight[:, :], in0=ex[:, :], scalar=share, in1=total[:, :],
                                         op0=ALU.mult, op1=ALU.mult).then_inc(alpha_made, 1)

            @block.scalar
            def _(act):
                act.wait_ge(diff_done, 1)
                act.activation(ex[:, :], e[:, :], ACT.Exp).then_inc(exp_done, 1)
                if self_loops:
                    act.activation(exs[:, :], es[:, :], ACT.Exp).then_inc(exp_done, 1)

            @block.tensor
            def _(pe):
                pe.wait_ge(ident_made, 1)
                count = [0]

                def column(source, b):
                    count[0] += 1
                    pe.wait_ge(asked, count[0])
                    pe.matmul(row[:, :], source[:, end(b):end(b) + 1], ident[:, :], start=True, stop=True).then_inc(turn_done, 1)

                def carries(b):
                    count[0] += 1
                    pe.wait_ge(asked, count[0])
                    pe.matmul(col[:, :], ends[:, 2 * b:2 * b + P], ident[0:1, 0:1], start=True, stop=True).then_inc(turn_done, 1)

                for b in range(2):
                    column(lead[b], b)
                for _ in ("maximum", "sum"):
                    for b in range(2):
                        column(run, b)
                        carries(b)


def conv_aggregate(nc, g, layer):
    nb = g.NTE // K
    with Phase(nc, f"conv_aggregate{layer}_") as m:
        ident = m.sb("ident", [P, P])
        idx = m.sbs("idx", [P, 16], I32)
        alphaT, keep = m.sbs("alphaT", [H, TILE]), m.sbs("keep", [P, TILE])
        alpha, diff = m.sbs("alpha", [P, SUB * H], n=2), m.sbs("diff", [P, TILE], n=2)
        part, sumT, rows = m.sbs("part", [P, SUB, D], n=2), m.sbs("sumT", [P, TILE], n=2), m.sbs("rows", [P, TILE])
        y = [m.ps(f"y{s}", [P, H * D]) for s in range(SUB)]
        alpha_ps, partT, back = m.ps("alpha_ps", [P, SUB * H]), m.ps("partT", [P, TILE]), m.ps("back", [P, TILE])
        tile_in, agg_out, own = m.sems("tile_in"), g.scattered, m.sem("own")
        agg0 = g.start(agg_out, nb * 64)
        cleared, ident_made, tail_set = (m.sem(n) for n in ("cleared", "ident_made", "tail_set"))
        alpha_turned, alpha_made, diff_copied, y_done, part_step, part_made = (
            m.sem(n) for n in ("alpha_turned", "alpha_made", "diff_copied", "y_done", "part_step", "part_made"))
        partT_done, scanned, back_done, rows_made = (m.sem(n) for n in ("partT_done", "scanned", "back_done", "rows_made"))
        with nc.Block() as block:
            @block.sync
            def _(sp):
                def load(k, i):
                    n = i * K + k
                    sp.dma_start(idx[k][:, :], g.IDX[bass.ds(n, 1), :, :].rearrange("t p s -> (t p) s")).then_inc(tile_in[k], 16)
                    sp.dma_start(alphaT[k][:, :], g.ALPHA[:, bass.ds(n * TILE, TILE)]).then_inc(tile_in[k], 16)
                    sp.dma_start(keep[k][:, :], edge_span(g.KEEP, n, P)).then_inc(tile_in[k], 16)

                for k in range(K):
                    load(k, 0)
                if nb > 1:
                    with sp.Fori(1, nb) as i:
                        for k in range(K):
                            sp.wait_ge(agg_out[k], i * 64 + agg0)
                            load(k, i)

            @block.gpsimd
            def _(pool):
                make_identity(pool, ident, ident_made, cleared)

                def body(i):
                    for k in range(K):
                        wait_alone(pool, rows_made, i * K + k + 1, own)
                        for s in range(SUB):
                            scatter_last(pool, g.AGG[:, :], idx[k][:, 8 + s:9 + s], rows[k][:, s * P:(s + 1) * P],
                                         g.NP - 1).then_inc(agg_out[k], 16)

                run_bodies(pool, nb, body)
                for k in range(K):
                    pool.wait_ge(agg_out[k], nb * 64 + agg0)

            @block.tensor
            def _(pe):
                pe.wait_ge(ident_made, 1)

                def body(i):
                    n = i * K

                    def turn_alpha(k):
                        pe.wait_ge(tile_in[k], (i + 1) * 48)
                        pe.wait_ge(alpha_made, n + k)
                        for s in range(SUB):
                            last = pe.matmul(alpha_ps[:, s * H:(s + 1) * H], alphaT[k][:, s * P:(s + 1) * P], ident[0:H, 0:H],
                                             start=True, stop=True)
                        last.then_inc(alpha_turned, 1)

                    def project(k):
                        pe.wait_ge(diff_copied, n + k + 1)
                        pe.wait_ge(part_made, n + k)
                        for s in range(SUB):
                            last = pe.matmul(y[s][:, :], diff[k % 2][:, s * P:(s + 1) * P], g.wl[:, :], start=True, stop=True)
                            last.then_inc(y_done, 1)

                    def turn(k):
                        pe.wait_ge(part_made, n + k + 1)
                        pe.wait_ge(scanned, n + k)
                        for s in range(SUB):
                            last = pe.transpose(partT[:, s * P:(s + 1) * P], part[k % 2][:, s, :], ident[:, :])
                        last.then_inc(partT_done, 1)

                    def turn_back(k):
                        pe.wait_ge(scanned, n + k + 1)
                        pe.wait_ge(rows_made, n + k)
                        for s in range(SUB):
                            last = pe.transpose(back[:, s * P:(s + 1) * P], sumT[k % 2][:, s * P:(s + 1) * P], ident[:, :])
                        last.then_inc(back_done, 1)

                    turn_alpha(0)
                    for k in range(K + 2):
                        if k < K:
                            project(k)
                        if k + 1 < K:
                            turn_alpha(k + 1)
                        if 1 <= k <= K:
                            turn(k - 1)
                        if k >= 2:
                            turn_back(k - 2)

                run_bodies(pe, nb, body)

            @block.scalar
            def _(act):
                def body(i):
                    n = i * K

                    def copy_alpha(k):
                        act.wait_ge(alpha_turned, n + k + 1)
                        act.wait_ge(part_made, n + max(k - 1, 0))
                        if k == 0:
                            act.wait_ge(part_made, n)
                        act.activation(alpha[k % 2][:, :], alpha_ps[:, :], ACT.Copy).then_inc(alpha_made, 1)

                    def copy_diff(k):
                        act.wait_ge(y_done, SUB * n + SUB * max(k - 1, 0))
                        act.activation(diff[k % 2][:, :], g.diffT[:, bass.ds((n + k) * TILE, TILE)], ACT.Copy).then_inc(diff_copied, 1)

                    copy_diff(0)
                    copy_alpha(0)
                    for k in range(K + 2):
                        if k + 1 < K:
                            copy_diff(k + 1)
                            copy_alpha(k + 1)
                        if k >= 2:
                            act.wait_ge(back_done, n + k - 1)
                            act.wait_ge(agg_out[k - 2], i * 64 + agg0)
                            act.activation(rows[k - 2][:, :], back[:, :], ACT.Copy).then_inc(rows_made, 1)

                run_bodies(act, nb, body)

            @block.vector
            def _(dve):
                for j in range(2):
                    dve.memset(sumT[j][:, TILE - 1:TILE], 0.0).then_inc(tail_set, 1)
                dve.wait_ge(tail_set, 2)

                def body(i):
                    n = i * K

                    def weigh(k):
                        dve.wait_ge(alpha_made, n + k + 1)
                        dve.wait_ge(partT_done, n + max(k - 1, 0))
                        for h in range(H):
                            if h:
                                dve.wait_ge(part_step, (H - 1) * n + (H - 1) * k + h)
                            for s in range(SUB):
                                if h == 0:
                                    dve.wait_ge(y_done, SUB * n + SUB * k + s + 1)
                                a = alpha[k % 2][:, s * H + h:s * H + h + 1]
                                yh, out = y[s][:, h * D:(h + 1) * D], part[k % 2][:, s, :]
                                if h == 0:
                                    last = dve.tensor_scalar(out, yh, a, None, ALU.mult)
                                else:
                                    last = dve.scalar_tensor_tensor(out=out, in0=yh, scalar=a, in1=out, op0=ALU.mult, op1=ALU.add)
                            last.then_inc(part_made if h == H - 1 else part_step, 1)

                    def scan(k):
                        dve.wait_ge(partT_done, n + k + 1)
                        dve.wait_ge(scanned, n + k)
                        dve.wait_ge(back_done, n + max(k - 1, 0))
                        before = sumT[(k - 1) % 2 if k else (K - 1) % 2]
                        dve.tensor_tensor_scan(sumT[k % 2][:, :], keep[k][:, :], partT[:, :], before[:, TILE - 1:TILE],
                                               ALU.mult, ALU.add).then_inc(scanned, 1)

                    for k in range(K + 1):
                        if k < K:
                            weigh(k)
                        if k:
                            scan(k - 1)

                run_bodies(dve, nb, body)


def broadcast_rows(sp, dst, src, done):
    sp.dma_start(dst, src.to_broadcast([P, dst.shape[1]])).then_inc(done, 16)


def conv_nodes(nc, g, layer, final):
    nb = g.NTN // NB
    bias_in, gamma_in, beta_in = g.conv_norms[layer]
    flat = lambda t: t[:, :, :].rearrange("p a d -> p (a d)")
    with Phase(nc, f"conv_nodes{layer}_") as m:
        ident, eps = m.sb("ident", [P, P]), m.sb("eps", [P, 1])
        gamma, beta, bias = (m.sb(n, [P, TILE]) for n in ("gamma", "beta", "bias"))
        h, agg = m.sbs("h", [P, SUB, D]), m.sbs("agg", [P, SUB, D])
        x = m.sbs("x", [P, SUB, D]) if final else None
        hT = m.sbs("hT", [P, TILE], n=2)
        base, o, scaled, res = (m.sbs(n, [P, SUB, D]) for n in ("base", "o", "scaled", "res"))
        h_out = m.sbs("h_out", [P, SUB, D]) if final else res
        turned = [m.ps(f"turned{j}", [P, TILE]) for j in range(2)]
        o_ps = [m.ps(f"o_ps{j}", [P, SUB, D]) for j in range(2)]
        norm = Norm(m, "norm")
        last_norm = Norm(m, "last_norm") if final else None
        tile_in, out = m.sems("tile_in"), m.sems("out")
        cleared, ident_made, set_once, weights_in = (m.sem(n) for n in ("cleared", "ident_made", "set_once", "weights_in"))
        turned_done, hT_made, o_done, o_made, base_made, half_base, agg_made = (
            m.sem(n) for n in ("turned_done", "hT_made", "o_done", "o_made", "base_made", "half_base", "agg_made"))
        normed, scaled_made, sum_made, all_made = (m.sem(n) for n in ("normed", "scaled_made", "sum_made", "all_made"))
        own = m.sem("own")
        n_in, n_out = (48, 32) if final else (32, 16)
        with nc.Block() as block:
            @block.sync
            def _(sp):
                for a in range(SUB):
                    broadcast_rows(sp, gamma[:, a * D:(a + 1) * D], gamma_in, weights_in)
                    broadcast_rows(sp, beta[:, a * D:(a + 1) * D], beta_in, weights_in)
                    broadcast_rows(sp, bias[:, a * D:(a + 1) * D], bias_in, weights_in)

                def load(k, i):
                    r, n = k % RING, i * NB + k
                    sp.dma_start(h[r][:, :, :], node_rows(g.H, n)).then_inc(tile_in[r], 16)
                    sp.dma_start(agg[r][:, :, :], node_rows(g.AGG, n)).then_inc(tile_in[r], 16)
                    if final:
                        sp.dma_start(x[r][:, :, :], node_rows(g.X, n)).then_inc(tile_in[r], 16)

                def freed(k, i):
                    sp.wait_ge(base_made, i * NB + k + 1)
                    sp.wait_ge(o_made, i * NB + k + 1)

                def store(k, i):
                    r, n = k % RING, i * NB + k
                    sp.wait_ge(all_made, n + 1)
                    sp.dma_start(node_rows(g.H, n), h_out[r][:, :, :]).then_inc(out[r], 16)
                    if final:
                        sp.dma_start(node_rows(g.X, n), res[r][:, :, :]).then_inc(out[r], 16)

                node_stream(sp, nb, load, freed, store, 9 if final else 6)
                for r in range(RING):
                    sp.wait_ge(out[r], n_out * turns(r, nb))

            @block.gpsimd
            def _(pool):
                make_identity(pool, ident, ident_made, cleared)
                pool.wait_ge(weights_in, 16 * 12)

                def make_base(k, i):
                    r, n = k % RING, i * NB + k
                    past(pool, sum_made, n + 1 - RING)
                    wait_alone(pool, tile_in[r], n_in * (turns(k, i) + 1), own)
                    pool.tensor_tensor(flat(agg[r]), flat(agg[r]), bias[:, :], ALU.add).then_inc(agg_made, 1)
                    first = pool.tensor_tensor(flat(base[r]), flat(h[r]), beta[:, :], ALU.add)
                    if final:
                        first.then_inc(half_base, 1)
                        pool.wait_ge(half_base, n + 1)
                        pool.tensor_tensor(flat(base[r]), flat(base[r]), flat(x[r]), ALU.add).then_inc(base_made, 1)
                    else:
                        first.then_inc(base_made, 1)

                pipeline(pool, nb, NB, [(0, make_base)])

            @block.tensor
            def _(pe):
                pe.wait_ge(ident_made, 1)

                def turn(k, i):
                    r, n = k % RING, i * NB + k
                    pe.wait_ge(tile_in[r], n_in * (turns(k, i) + 1))
                    past(pe, hT_made, n - 1)
                    for a in range(SUB):
                        last = pe.transpose(turned[k % 2][:, a * P:(a + 1) * P], h[r][:, a, :], ident[:, :])
                    last.then_inc(turned_done, 1)

                def project(k, i):
                    n = i * NB + k
                    past(pe, o_made, n - 1)
                    pe.wait_ge(hT_made, n + 1)
                    for a in range(SUB):
                        last = pe.matmul(o_ps[k % 2][:, a, :], hT[k % 2][:, a * P:(a + 1) * P], g.wmean[:, :],
                                         start=True, stop=True)
                    last.then_inc(o_done, 1)

                pipeline(pe, nb, NB, [(0, turn), (1, project)])

            @block.vector
            def _(dve):
                dve.memset(eps[:, :], EPS).then_inc(set_once, 1)
                dve.wait_ge(weights_in, 16 * 12)

                def start(k, i):
                    r, n = k % RING, i * NB + k
                    dve.wait_ge(o_done, n + 1)
                    dve.wait_ge(agg_made, n + 1)
                    past(dve, normed, n + 1 - RING)
                    dve.tensor_tensor(o[r][:, :, :], o_ps[k % 2][:, :, :], agg[r][:, :, :], ALU.add).then_inc(o_made, 1)

                def take_stats(k, i):
                    dve.wait_ge(o_made, i * NB + k + 1)
                    norm.take_stats(dve, o[k % RING], k % RING)

                def finish(k, i):
                    r, n = k % RING, i * NB + k
                    dve.wait_ge(normed, n + 1)
                    dve.tensor_tensor(flat(o[r]), flat(scaled[r]), gamma[:, :], ALU.mult).then_inc(scaled_made, 1)
                    dve.wait_ge(base_made, n + 1)
                    dve.wait_ge(scaled_made, n + 1)
                    if final:
                        past(dve, out[r], n_out * turns(k, i))
                    dve.tensor_tensor(flat(res[r]) if final else flat(scaled[r]), flat(o[r]), flat(base[r]), ALU.add).then_inc(sum_made, 1)

                def last_stats(k, i):
                    dve.wait_ge(sum_made, i * NB + k + 1)
                    last_norm.take_stats(dve, res[k % RING], k % RING)

                steps = [
                    (0, start),
                    (1, lambda k, i: norm.moments(dve, k % RING, i * NB + k + 1)),
                    (0, take_stats),
                    (3, lambda k, i: norm.scales(dve, k % RING, i * NB + k + 1)),
                    (5, finish)]
                if final:
                    steps += [
                        (6, lambda k, i: last_norm.moments(dve, k % RING, i * NB + k + 1)),
                        (5, last_stats),
                        (8, lambda k, i: last_norm.scales(dve, k % RING, i * NB + k + 1))]
                pipeline(dve, nb, NB, steps)

            @block.scalar
            def _(act):
                act.wait_ge(set_once, 1)

                def copy_turned(k, i):
                    n = i * NB + k
                    act.wait_ge(turned_done, n + 1)
                    past(act, o_done, n - 1)
                    act.activation(hT[k % 2][:, :], turned[k % 2][:, :], ACT.Copy).then_inc(hT_made, 1)

                def normalize(k, i):
                    r, n = k % RING, i * NB + k
                    act.wait_ge(norm.shift_done, n + 1)
                    past(act, sum_made, n + 1 - RING)
                    norm.apply(act, scaled[r], o[r], r, ACT.Identity).then_inc(normed, 1)

                def relu(k, i):
                    r, n = k % RING, i * NB + k
                    act.wait_ge(sum_made, n + 1)
                    past(act, out[r], n_out * turns(k, i))
                    act.activation(res[r][:, :, :], scaled[r][:, :, :], ACT.Relu).then_inc(all_made, 1)

                def last_normalize(k, i):
                    r, n = k % RING, i * NB + k
                    act.wait_ge(last_norm.shift_done, n + 1)
                    past(act, out[r], n_out * turns(k, i))
                    last_norm.apply(act, h_out[r], res[r], r, ACT.Relu).then_inc(all_made, 1)

                steps = [
                    (0, copy_turned),
                    (3, lambda k, i: norm.root(act, k % RING, i * NB + k + 1, eps)),
                    (5, normalize)]
                if final:
                    steps += [
                        (8, lambda k, i: last_norm.root(act, k % RING, i * NB + k + 1, eps)),
                        (10, last_normalize)]
                else:
                    steps += [(7, relu)]
                pipeline(act, nb, NB, steps)




def gat_logits(nc, g):
    nb = g.NTE // K
    with Phase(nc, "gat_logits_") as m:
        ident = m.sb("ident", [P, P])
        a_rows, product, wa = m.sb("a_rows", [P, 2, HID]), m.sb("product", [D, 2, HID]), m.sb("wa", [D, 2, H])
        idx = m.sbs("idx", [P, 16], I32)
        hs, hd, hdT = m.sbs("hs", [P, SUB, D]), m.sbs("hd", [P, SUB, D]), m.sbs("hdT", [P, TILE], n=2)
        sloped, logit = m.sbs("sloped", [H, TILE], n=2), m.sbs("logit", [H, TILE], n=2)
        hsT_ps, hdT_ps = ([m.ps(f"{n}{j}", [P, TILE]) for j in range(2)] for n in ("hsT_ps", "hdT_ps"))
        e_ps = [m.ps(f"e_ps{j}", [H, TILE]) for j in range(2)]
        idx_in, rows_in, logit_out, own = m.sems("idx_in"), g.gathered, m.sems("logit_out", 2), m.sem("own")
        rows0 = g.start(rows_in, nb * 128)
        cleared, ident_made, weights_in, product_made, weights_made = (
            m.sem(n) for n in ("cleared", "ident_made", "weights_in", "product_made", "weights_made"))
        turned_done, hdT_made, hsT_made, e_done, sloped_made, logit_made = (
            m.sem(n) for n in ("turned_done", "hdT_made", "hsT_made", "e_done", "sloped_made", "logit_made"))
        with nc.Block() as block:
            @block.sync
            def _(sp):
                sp.dma_start(g.wn[:, :], g.wnT).then_inc(weights_in, 16)
                broadcast_rows(sp, a_rows[:, 0, :], g.a_src, weights_in)
                broadcast_rows(sp, a_rows[:, 1, :], g.a_dst, weights_in)

                def load(k, i):
                    sp.dma_start(idx[k][:, :], g.IDX[bass.ds(i * K + k, 1), :, :].rearrange("t p s -> (t p) s")).then_inc(idx_in[k], 16)

                def body(i, more):
                    for k in range(K):
                        sp.wait_ge(logit_made, i * K + k + 1)
                        sp.dma_start(g.LOGIT[1][:, bass.ds((i * K + k) * TILE, TILE)], logit[k % 2][:, :]).then_inc(logit_out[k % 2], 16)
                        if more:
                            load(k, i + 1)

                for k in range(K):
                    load(k, 0)
                if nb > 1:
                    with sp.Fori(0, nb - 1) as i:
                        body(i, True)
                body(nb - 1, False)
                for slot in range(2):
                    sp.wait_ge(logit_out[slot], 16 * nb * slot_tiles(slot))

            @block.gpsimd
            def _(pool):
                make_identity(pool, ident, ident_made, cleared)

                def gather_tile(k, i):
                    wait_alone(pool, idx_in[k], (i + 1) * 16, own)
                    for s in range(SUB):
                        gather(pool, hd[k][:, s, :], g.H[:, :], idx[k][:, 4 + s:5 + s]).then_inc(rows_in[k], 16)
                        gather(pool, hs[k][:, s, :], g.H[:, :], idx[k][:, s:s + 1]).then_inc(rows_in[k], 16)

                for k in range(K):
                    gather_tile(k, 0)
                if nb > 1:
                    with pool.Fori(1, nb) as i:
                        for k in range(K):
                            pool.wait_ge(turned_done, (i - 1) * K + k + 1)
                            gather_tile(k, i)

            @block.tensor
            def _(pe):
                pe.wait_ge(ident_made, 1)
                pe.wait_ge(weights_made, 1)

                def body(i):
                    n = i * K
                    for k in range(K + 1):
                        if k < K:
                            pe.wait_ge(rows_in[k], i * 128 + (128 + rows0))
                            pe.wait_ge(hdT_made, n + max(k - 1, 0))
                            pe.wait_ge(hsT_made, n + max(k - 1, 0))
                            for s in range(SUB):
                                pe.transpose(hdT_ps[k % 2][:, s * P:(s + 1) * P], hd[k][:, s, :], ident[:, :])
                            for s in range(SUB):
                                last = pe.transpose(hsT_ps[k % 2][:, s * P:(s + 1) * P], hs[k][:, s, :], ident[:, :])
                            last.then_inc(turned_done, 1)
                        if k:
                            j = k - 1
                            pe.wait_ge(hdT_made, n + j + 1)
                            pe.wait_ge(logit_made, n + max(j - 1, 0))
                            pe.matmul(e_ps[j % 2][:, :], wa[:, 1, :], hdT[j % 2][:, :], start=True, stop=False)
                            pe.wait_ge(hsT_made, n + j + 1)
                            pe.matmul(e_ps[j % 2][:, :], wa[:, 0, :], g.srcT[:, bass.ds((n + j) * TILE, TILE)],
                                      start=False, stop=True).then_inc(e_done, 1)

                run_bodies(pe, nb, body)

            @block.scalar
            def _(act):
                def body(i):
                    n = i * K
                    for k in range(K + 1):
                        if k < K:
                            act.wait_ge(turned_done, n + k + 1)
                            act.wait_ge(e_done, n + max(k - 1, 0))
                            act.activation(hdT[k % 2][:, :], hdT_ps[k % 2][:, :], ACT.Copy).then_inc(hdT_made, 1)
                        if k:
                            j = k - 1
                            act.wait_ge(e_done, n + j + 1)
                            act.wait_ge(logit_made, n + max(j - 1, 0))
                            act.activation(sloped[j % 2][:, :], e_ps[j % 2][:, :], ACT.Copy, scale=SLOPE).then_inc(sloped_made, 1)

                run_bodies(act, nb, body)

            @block.vector
            def _(dve):
                dve.wait_ge(weights_in, 48)
                for j in range(2):
                    dve.tensor_tensor(product[:, j, :], g.wn[:, :], a_rows[:, j, :], ALU.mult).then_inc(product_made, 1)
                dve.wait_ge(product_made, 2)
                dve.tensor_reduce(out=wa[:, :, :].rearrange("p j h -> p (j h)"),
                                  in_=product[:, :, :].rearrange("p j (h d) -> p (j h) d", h=H), axis=AX.X, op=ALU.add).then_inc(weights_made, 1)

                def body(i):
                    n = i * K
                    for k in range(K + 1):
                        if k < K:
                            dve.wait_ge(turned_done, n + k + 1)
                            dve.tensor_copy(g.srcT[:, bass.ds((n + k) * TILE, TILE)], hsT_ps[k % 2][:, :]).then_inc(hsT_made, 1)
                        if k:
                            j = k - 1
                            dve.wait_ge(sloped_made, n + j + 1)
                            dve.wait_ge(logit_out[j % 2], i * (16 * slot_tiles(j % 2)) + 16 * (j // 2))
                            dve.tensor_tensor(logit[j % 2][:, :], e_ps[j % 2][:, :], sloped[j % 2][:, :], ALU.max).then_inc(logit_made, 1)

                run_bodies(dve, nb, body)


def slot(k):
    return 2 if k == K - 1 else k % 2


def slot_before(k, i):
    earlier = [j for j in range(k) if slot(j) == slot(k)]
    if earlier:
        return earlier[-1], i
    return max(j for j in range(K) if slot(j) == slot(k)), i - 1


def rows_freed(eng, scattered, start, k, i):
    kb, ib = slot_before(k, i)
    if not isinstance(ib, int) or ib >= 0:
        eng.wait_ge(scattered[kb], (ib + 1) * 64 + start)


def gat_aggregate(nc, g):
    nb = g.NTE // K
    with Phase(nc, "gat_aggregate_") as m:
        ident = m.sb("ident", [P, P])
        w1, w2, b1 = m.sb("w1", [P, 2, HID]), m.sb("w2", [P, 2, D]), m.sb("b1", [P, 2])
        above, below = m.sb("above", [P, 2]), m.sb("below", [P, 2])
        idx, alphaT, keep = m.sbs("idx", [P, 16], I32), m.sbs("alphaT", [H, TILE]), m.sbs("keep", [P, TILE])
        alpha, src = m.sbs("alpha", [P, SUB * H], n=3), m.sbs("src", [P, TILE], n=3)
        part, sumT = m.sbs("part", [P, SUB, HID], n=3), m.sbs("sumT", [P, 2, TILE], n=3)
        headsT, hidT, rows = m.sbs("headsT", [P, 2, TILE], n=3), m.sb("hidT", [P, 2, TILE]), m.sbs("rows", [P, TILE], n=3)
        y = [m.ps(f"y{j}", [P, 2, HID]) for j in range(2)]
        partT, hid = ([m.ps(f"{n}{j}", [P, TILE]) for j in range(2)] for n in ("partT", "hid"))
        o, alpha_ps = m.ps("o", [P, TILE]), m.ps("alpha_ps", [P, SUB * H])
        tile_in, weights_in = m.sems("tile_in"), m.sem("weights_in")
        agg_out, own = g.scattered, m.sem("own")
        agg0 = g.start(agg_out, nb * 64)
        cleared, ident_made, tail_set, bias_ready = (m.sem(n) for n in ("cleared", "ident_made", "tail_set", "bias_ready"))
        alpha_turned, alpha_made, src_copied, y_done, part_made = (
            m.sem(n) for n in ("alpha_turned", "alpha_made", "src_copied", "y_done", "part_made"))
        partT_done, scanned, headsT_made, hid_done, hidT_made, o_done, rows_made = (
            m.sem(n) for n in ("partT_done", "scanned", "headsT_made", "hid_done", "hidT_made", "o_done", "rows_made"))
        with nc.Block() as block:
            @block.sync
            def _(sp):
                sp.dma_start(w1[:, :, :], g.mw1.rearrange("(j p) n -> p j n", p=P)).then_inc(weights_in, 16)
                sp.dma_start(w2[:, :, :], g.mw2.rearrange("(j p) n -> p j n", p=P)).then_inc(weights_in, 16)
                with nc.allow_non_contiguous_dma("256 biases"):
                    sp.dma_start(b1[:, :], g.mb1.rearrange("o (j p) -> p (o j)", p=P)).then_inc(weights_in, 16)

                def load(k, i):
                    n = i * K + k
                    sp.dma_start(idx[k][:, :], g.IDX[bass.ds(n, 1), :, :].rearrange("t p s -> (t p) s")).then_inc(tile_in[k], 16)
                    sp.dma_start(alphaT[k][:, :], g.ALPHA[:, bass.ds(n * TILE, TILE)]).then_inc(tile_in[k], 16)
                    sp.dma_start(keep[k][:, :], edge_span(g.KEEP, n, P)).then_inc(tile_in[k], 16)

                for k in range(K):
                    load(k, 0)
                if nb > 1:
                    with sp.Fori(1, nb) as i:
                        for k in range(K):
                            sp.wait_ge(agg_out[k], i * 64 + agg0)
                            load(k, i)

            @block.gpsimd
            def _(pool):
                make_identity(pool, ident, ident_made, cleared)

                def body(i):
                    for k in range(K):
                        wait_alone(pool, rows_made, i * K + k + 1, own)
                        for s in range(SUB):
                            scatter_last(pool, g.AGG[:, :], idx[k][:, 8 + s:9 + s], rows[slot(k)][:, s * P:(s + 1) * P],
                                         g.NP - 1).then_inc(agg_out[k], 16)

                run_bodies(pool, nb, body)
                for k in range(K):
                    pool.wait_ge(agg_out[k], nb * 64 + agg0)

            @block.tensor
            def _(pe):
                pe.wait_ge(ident_made, 1)
                pe.wait_ge(weights_in, 48)

                def turn_alpha(k, i):
                    n = i * K + k
                    pe.wait_ge(tile_in[k], (i + 1) * 48)
                    past(pe, alpha_made, n)
                    for s in range(SUB):
                        last = pe.matmul(alpha_ps[:, s * H:(s + 1) * H], alphaT[k][:, s * P:(s + 1) * P], ident[0:H, 0:H],
                                         start=True, stop=True)
                    last.then_inc(alpha_turned, 1)

                def project(k, i):
                    n = i * K + k
                    pe.wait_ge(src_copied, n + 1)
                    past(pe, part_made, 2 * n)
                    for s in range(SUB):
                        pe.matmul(y[s // 2][:, s % 2, :], src[slot(k)][:, s * P:(s + 1) * P], g.wn[:, :],
                                  start=True, stop=True).then_inc(y_done, 1)

                def turn(k, i):
                    n = i * K + k
                    pe.wait_ge(part_made, 2 * n + 2)
                    past(pe, scanned, 2 * n)
                    for j in range(2):
                        for s in range(SUB):
                            last = pe.transpose(partT[j][:, s * P:(s + 1) * P], part[slot(k)][:, s, j * P:(j + 1) * P], ident[:, :])
                    last.then_inc(partT_done, 1)

                def first(k, i):
                    n = i * K + k
                    pe.wait_ge(headsT_made, n + 1)
                    for j in range(2):
                        past(pe, hidT_made, 2 * n + j - 1)
                        for c in range(2):
                            last = pe.matmul(hid[j][:, :], w1[:, c, j * P:(j + 1) * P], headsT[slot(k)][:, c, :],
                                             start=(c == 0), stop=(c == 1))
                        last.then_inc(hid_done, 1)

                def second(k, i):
                    n = i * K + k
                    past(pe, rows_made, n)
                    pe.wait_ge(hidT_made, 2 * n + 2)
                    for s in range(SUB):
                        for c in range(2):
                            last = pe.matmul(o[:, s * D:(s + 1) * D], hidT[:, c, s * P:(s + 1) * P], w2[:, c, :],
                                             start=(c == 0), stop=(c == 1))
                    last.then_inc(o_done, 1)

                pipeline(pe, nb, K, [(0, turn_alpha), (1, project), (2, turn), (3, first), (4, second)])

            @block.scalar
            def _(act):
                def copy_alpha(k, i):
                    n = i * K + k
                    act.wait_ge(alpha_turned, n + 1)
                    past(act, part_made, 2 * (n - 1))
                    act.activation(alpha[slot(k)][:, :], alpha_ps[:, :], ACT.Copy).then_inc(alpha_made, 1)

                def copy_src(k, i):
                    n = i * K + k
                    past(act, y_done, SUB * (n - 1))
                    act.activation(src[slot(k)][:, :], g.srcT[:, bass.ds(n * TILE, TILE)], ACT.Copy).then_inc(src_copied, 1)

                def copy_rows(k, i):
                    act.wait_ge(o_done, i * K + k + 1)
                    rows_freed(act, agg_out, agg0, k, i)
                    act.activation(rows[slot(k)][:, :], o[:, :], ACT.Copy).then_inc(rows_made, 1)

                def relu_heads(k, i):
                    n = i * K + k
                    act.wait_ge(scanned, 2 * n + 2)
                    past(act, hid_done, 2 * (n - 1))
                    act.activation(headsT[slot(k)][:, :, :], sumT[slot(k)][:, :, :], ACT.Relu).then_inc(headsT_made, 1)

                pipeline(act, nb, K, [(0, copy_alpha), (0, copy_src), (5, copy_rows), (2, relu_heads)])

            @block.vector
            def _(dve):
                dve.wait_ge(weights_in, 48)
                dve.tensor_scalar(above[:, :], b1[:, :], 0.0, None, ALU.min).then_inc(bias_ready, 1)
                dve.tensor_scalar(below[:, :], b1[:, :], 0.0, -1.0, ALU.max, ALU.mult).then_inc(bias_ready, 1)
                for j in range(3):
                    dve.memset(sumT[j][:, :, TILE - 1:TILE], 0.0).then_inc(tail_set, 1)
                dve.wait_ge(tail_set, 3)
                dve.wait_ge(bias_ready, 2)

                def hidden(k, i):
                    n = i * K + k
                    for j in range(2):
                        dve.wait_ge(hid_done, 2 * n + j + 1)
                        if j == 0:
                            past(dve, o_done, n)
                        dve.tensor_scalar(hidT[:, j, :], hid[j][:, :], above[:, j:j + 1], below[:, j:j + 1],
                                          ALU.add, ALU.max).then_inc(hidT_made, 1)

                def weigh(k, i):
                    n = i * K + k
                    dve.wait_ge(alpha_made, n + 1)
                    past(dve, partT_done, n - 1)
                    for j in range(2):
                        dve.wait_ge(y_done, SUB * n + 2 * (j + 1))
                        weights = alpha[slot(k)][:, 2 * H * j:2 * H * (j + 1)].unsqueeze(2).to_broadcast([P, 2 * H, HD])
                        dve.tensor_tensor(part[slot(k)][:, 2 * j:2 * j + 2, :].rearrange("p s (h d) -> p (s h) d", h=H),
                                          y[j][:, :, :].rearrange("p s (h d) -> p (s h) d", h=H), weights, ALU.mult).then_inc(part_made, 1)

                def scan(k, i):
                    n = i * K + k
                    dve.wait_ge(partT_done, n + 1)
                    past(dve, scanned, 2 * n)
                    past(dve, headsT_made, n - 1)
                    before = sumT[slot(k - 1 if k else K - 1)]
                    for j in range(2):
                        dve.tensor_tensor_scan(sumT[slot(k)][:, j, :], keep[k][:, :], partT[j][:, :],
                                               before[:, j, TILE - 1:TILE], ALU.mult, ALU.add).then_inc(scanned, 1)

                pipeline(dve, nb, K, [(4, hidden), (1, weigh), (2, scan)])


def gat_nodes(nc, g):
    nb = g.NTN // NB
    flat = lambda t: t[:, :, :].rearrange("p a d -> p (a d)")
    with Phase(nc, "gat_nodes_") as m:
        eps, ones = m.sb("eps", [P, 1]), m.sb("ones", [P, P])
        b1, relu_b1, w2 = m.sb("b1", [P, 2]), m.sb("relu_b1", [P, 2, P]), m.sb("w2", [P, 2, D])
        b2, c = m.sb("b2", [P, D]), m.sb("c", [P, TILE])
        x, agg, base, x3, h4, total = (m.sbs(n, [P, SUB, D]) for n in ("x", "agg", "base", "x3", "h4", "total"))
        c_ps = m.ps("c_ps", [P, D])
        norm = Norm(m, "norm")
        tile_in, out, own = m.sems("tile_in"), m.sems("out"), m.sem("own")
        weights_in, ones_set, relu_made, c_done, c_made, eps_set = (
            m.sem(n) for n in ("weights_in", "ones_set", "relu_made", "c_done", "c_made", "eps_set"))
        base_made, x3_made, h4_made, total_made = (m.sem(n) for n in ("base_made", "x3_made", "h4_made", "total_made"))
        with nc.Block() as block:
            @block.sync
            def _(sp):
                sp.dma_start(w2[:, :, :], g.mw2.rearrange("(j p) n -> p j n", p=P)).then_inc(weights_in, 16)
                with nc.allow_non_contiguous_dma("256 biases"):
                    sp.dma_start(b1[:, :], g.mb1.rearrange("o (j p) -> p (o j)", p=P)).then_inc(weights_in, 16)
                broadcast_rows(sp, b2[:, :], g.mb2, weights_in)

                def load(k, i):
                    r, n = k % RING, i * NB + k
                    sp.dma_start(x[r][:, :, :], node_rows(g.X, n)).then_inc(tile_in[r], 16)
                    sp.dma_start(agg[r][:, :, :], node_rows(g.AGG, n)).then_inc(tile_in[r], 16)

                def freed(k, i):
                    sp.wait_ge(x3_made, i * NB + k + 1)

                def store(k, i):
                    r, n = k % RING, i * NB + k
                    sp.wait_ge(total_made, n + 1)
                    sp.dma_start(node_rows(g.H, n), h4[r][:, :, :]).then_inc(out[r], 16)
                    sp.dma_start(node_rows(g.out, n), total[r][:, :, :]).then_inc(out[r], 16)

                node_stream(sp, nb, load, freed, store, 5)
                for r in range(RING):
                    sp.wait_ge(out[r], 32 * turns(r, nb))

            @block.tensor
            def _(pe):
                pe.wait_ge(relu_made, 2)
                for j in range(2):
                    last = pe.matmul(c_ps[:, :], relu_b1[:, j, :], w2[:, j, :], start=(j == 0), stop=(j == 1))
                last.then_inc(c_done, 1)

            @block.gpsimd
            def _(pool):
                pool.wait_ge(c_made, SUB)

                def make_base(k, i):
                    r, n = k % RING, i * NB + k
                    past(pool, x3_made, n + 1 - RING)
                    wait_alone(pool, tile_in[r], 32 * (turns(k, i) + 1), own)
                    pool.tensor_tensor(flat(base[r]), flat(x[r]), c[:, :], ALU.add).then_inc(base_made, 1)

                pipeline(pool, nb, NB, [(0, make_base)])

            @block.vector
            def _(dve):
                dve.memset(eps[:, :], EPS).then_inc(eps_set, 1)
                dve.memset(ones[:, :], 1.0).then_inc(ones_set, 1)
                dve.wait_ge(ones_set, 1)
                dve.wait_ge(weights_in, 48)
                for j in range(2):
                    dve.tensor_scalar(relu_b1[:, j, :], ones[:, :], b1[:, j:j + 1], 0.0, ALU.mult, ALU.max).then_inc(relu_made, 1)
                dve.wait_ge(c_done, 1)
                for a in range(SUB):
                    dve.tensor_tensor(c[:, a * D:(a + 1) * D], c_ps[:, :], b2[:, :], ALU.add).then_inc(c_made, 1)

                def add(k, i):
                    r, n = k % RING, i * NB + k
                    dve.wait_ge(base_made, n + 1)
                    dve.tensor_tensor(flat(x3[r]), flat(base[r]), flat(agg[r]), ALU.add).then_inc(x3_made, 1)

                def take_stats(k, i):
                    dve.wait_ge(x3_made, i * NB + k + 1)
                    norm.take_stats(dve, x3[k % RING], k % RING)

                def add_h4(k, i):
                    r, n = k % RING, i * NB + k
                    dve.wait_ge(h4_made, n + 1)
                    past(dve, out[r], 32 * turns(k, i))
                    dve.tensor_tensor(flat(total[r]), flat(x3[r]), flat(h4[r]), ALU.add).then_inc(total_made, 1)

                pipeline(dve, nb, NB, [
                    (0, add),
                    (1, lambda k, i: norm.moments(dve, k % RING, i * NB + k + 1)),
                    (0, take_stats),
                    (3, lambda k, i: norm.scales(dve, k % RING, i * NB + k + 1)),
                    (5, add_h4)])

            @block.scalar
            def _(act):
                act.wait_ge(eps_set, 1)

                def normalize(k, i):
                    r = k % RING
                    act.wait_ge(norm.shift_done, i * NB + k + 1)
                    past(act, out[r], 32 * turns(k, i))
                    norm.apply(act, h4[r], x3[r], r, ACT.Relu).then_inc(h4_made, 1)

                pipeline(act, nb, NB, [
                    (0, lambda k, i: norm.root(act, k % RING, i * NB + k + 1, eps)),
                    (2, normalize)])


def mean_edges(nc, g):
    nb = g.NTE // K
    with Phase(nc, "mean_edges_") as m:
        ident = m.sb("ident", [P, P])
        idx = m.sbs("idx", [P, 16], I32)
        hs, keep, sumT, rows = m.sbs("hs", [P, SUB, D]), m.sbs("keep", [P, TILE]), m.sbs("sumT", [P, TILE]), m.sbs("rows", [P, SUB, D])
        two, counts, half = m.sb("two", [1, TILE]), m.sbs("counts", [1, TILE], n=2), m.sbs("half", [P, SUB], n=2)
        turned, back, counts_ps = ([m.ps(f"{n}{j}", [P, TILE]) for j in range(2)] for n in ("turned", "back", "counts_ps"))
        idx_in, keep_in, hs_in, added = m.sems("idx_in"), m.sems("keep_in"), g.gathered, g.scattered
        hs0, added0 = g.start(hs_in, nb * 64), g.start(added, nb * 64)
        cleared, ident_made, set_once, own = (m.sem(n) for n in ("cleared", "ident_made", "set_once", "own"))
        turned_done, scanned, counted, half_made, back_done, rows_made = (
            m.sem(n) for n in ("turned_done", "scanned", "counted", "half_made", "back_done", "rows_made"))
        with nc.Block() as block:
            @block.sync
            def _(sp):
                def load(k, i):
                    sp.dma_start(idx[k][:, :], g.IDX[bass.ds(i * K + k, 1), :, :].rearrange("t p s -> (t p) s")).then_inc(idx_in[k], 16)
                    sp.dma_start(keep[k][:, :], edge_span(g.KEEP, i * K + k, P)).then_inc(keep_in[k], 16)

                for k in range(K):
                    load(k, 0)
                if nb > 1:
                    with sp.Fori(1, nb) as i:
                        for k in range(K):
                            sp.wait_ge(added[k], i * 64 + added0)
                            load(k, i)

            @block.gpsimd
            def _(pool):
                make_identity(pool, ident, ident_made, cleared)

                def gather_tile(k, i):
                    wait_alone(pool, idx_in[k], (i + 1) * 16, own)
                    for s in range(SUB):
                        gather(pool, hs[k][:, s, :], g.H[:, :], idx[k][:, s:s + 1]).then_inc(hs_in[k], 16)

                def body(i, more):
                    for k in range(K):
                        wait_alone(pool, rows_made, i * K + k + 1, own)
                        for s in range(SUB):
                            pool.indirect_dma_start(out=g.out[:, :], out_offset=bass.IndirectOffsetOnAxis(ap=idx[k][:, 12 + s:13 + s], axis=0),
                                                    in_=rows[k][:, s, :], in_offset=None, compute_op=ALU.add).then_inc(added[k], 16)
                        if more and k >= BEHIND:
                            gather_tile(k - BEHIND, i + 1)
                    if more:
                        for k in range(K - BEHIND, K):
                            gather_tile(k, i + 1)

                for k in range(K):
                    gather_tile(k, 0)
                if nb > 1:
                    with pool.Fori(0, nb - 1) as i:
                        body(i, True)
                body(nb - 1, False)
                for k in range(K):
                    pool.wait_ge(added[k], nb * 64 + added0)

            @block.tensor
            def _(pe):
                pe.wait_ge(ident_made, 1)

                def body(i):
                    n = i * K
                    for k in range(K + 1):
                        if k < K:
                            pe.wait_ge(hs_in[k], i * 64 + (64 + hs0))
                            pe.wait_ge(scanned, 2 * n + 2 * max(k - 1, 0))
                            for s in range(SUB):
                                last = pe.transpose(turned[k % 2][:, s * P:(s + 1) * P], hs[k][:, s, :], ident[:, :])
                            last.then_inc(turned_done, 1)
                        if k:
                            j = k - 1
                            pe.wait_ge(scanned, 2 * n + 2 * (j + 1))
                            pe.wait_ge(half_made, n + max(j - 1, 0))
                            for s in range(SUB):
                                last = pe.matmul(counts_ps[j % 2][:, s:s + 1], counts[j % 2][:, s * P:(s + 1) * P], ident[0:1, 0:1],
                                                 start=True, stop=True)
                            last.then_inc(counted, 1)
                            pe.wait_ge(rows_made, n + max(j - 1, 0))
                            for s in range(SUB):
                                last = pe.transpose(back[j % 2][:, s * P:(s + 1) * P], sumT[j][:, s * P:(s + 1) * P], ident[:, :])
                            last.then_inc(back_done, 1)

                run_bodies(pe, nb, body)

            @block.vector
            def _(dve):
                dve.memset(sumT[K - 1][:, TILE - 1:TILE], 0.0).then_inc(set_once, 1)
                for j in range(2):
                    dve.memset(counts[j][:, TILE - 1:TILE], 0.0).then_inc(set_once, 1)
                dve.memset(two[:, :], 2.0).then_inc(set_once, 1)
                dve.wait_ge(set_once, 4)

                def body(i):
                    n = i * K
                    for k in range(K + 1):
                        if k < K:
                            dve.wait_ge(keep_in[k], (i + 1) * 16)
                            dve.wait_ge(turned_done, n + k + 1)
                            dve.wait_ge(scanned, 2 * n + 2 * k)
                            dve.wait_ge(back_done, n)
                            dve.tensor_tensor_scan(sumT[k][:, :], keep[k][:, :], turned[k % 2][:, :],
                                                   sumT[k - 1][:, TILE - 1:TILE], ALU.mult, ALU.add).then_inc(scanned, 1)
                            dve.wait_ge(counted, n + max(k - 1, 0))
                            before = counts[(k - 1) % 2 if k else (K - 1) % 2]
                            dve.tensor_tensor_scan(counts[k % 2][:, :], keep[k][0:1, :], two[:, :],
                                                   before[:, TILE - 1:TILE], ALU.mult, ALU.add).then_inc(scanned, 1)
                        if k:
                            dve.wait_ge(counted, n + k)
                            dve.wait_ge(rows_made, n + max(k - 2, 0))
                            dve.reciprocal(half[(k - 1) % 2][:, :], counts_ps[(k - 1) % 2][:, 0:SUB]).then_inc(half_made, 1)

                run_bodies(dve, nb, body)

            @block.scalar
            def _(act):
                def body(i):
                    n = i * K
                    for k in range(K):
                        act.wait_ge(half_made, n + k + 1)
                        act.wait_ge(back_done, n + k + 1)
                        act.wait_ge(added[k], i * 64 + added0)
                        for s in range(SUB):
                            last = act.activation(rows[k][:, s, :], back[k % 2][:, s * P:(s + 1) * P], ACT.Copy, scale=half[k % 2][:, s:s + 1])
                        last.then_inc(rows_made, 1)

                run_bodies(act, nb, body)


class Graph:

    def start(self, sems, count):
        before = self.counted.get(id(sems), 0)
        self.counted[id(sems)] = before + count
        return before


def build(nc, g, phases=99):
    g.NTN, g.NTE = g.NP // TILE, g.EP // TILE
    dram = lambda name, shape, dt=F32: nc.dram_tensor(name, shape, dt).ap()
    g.H, g.AGG = dram("H", (g.NP, D)), dram("AGG", (g.NP, D))
    g.KEEP, g.KEEPN = dram("KEEP", (1, g.EP)), dram("KEEPN", (1, g.EP))
    g.IDX = dram("IDX", (g.NTE, P, 16), I32)
    g.YT, g.X = dram("YT", (g.NTN, P, TILE)), dram("X", (g.NP, D))
    g.LOGIT = [dram("LOGIT_SELF", (H, g.EP)), dram("LOGIT_EDGE", (H, g.EP))]
    g.ALPHA = dram("ALPHA", (H, g.EP))
    with ExitStack() as kept:
        sems = lambda name, n: [kept.enter_context(nc.semaphore(f"{name}{k}")) for k in range(n)]
        g.gathered, g.scattered, g.zeros_out = sems("gathered", K), sems("scattered", K), sems("zeros_out", 1)[0]
        g.counted = {}
        keep = lambda name, shape: kept.enter_context(nc.sbuf_tensor(name, shape, F32))
        g.bn_scale, g.bn_shift = keep("bn_scale", [D, 1]), keep("bn_shift", [D, 1])
        g.wn = keep("wn", [D, HID])
        g.wl, g.wsum, g.wmean = keep("wl", [D, H * D]), keep("wsum", [D, H * D]), keep("wmean", [D, D])
        steps = [prepare_indices, first_norm, gine_edges, gine_mlp, gine_finish,
                 lambda nc, g: convolution(nc, g, 0), lambda nc, g: convolution(nc, g, 1),
                 attention, gat_nodes, mean_edges]
        for step in steps[:phases]:
            step(nc, g)


def attention(nc, g):
    with nc.sbuf_tensor("srcT", [D, g.EP], F32) as g.srcT:
        gat_logits(nc, g)
        edge_softmax(nc, g, 2, 0, 1.0)
        gat_aggregate(nc, g)


def convolution(nc, g, layer):
    with nc.sbuf_tensor(f"diffT{layer}", [D, g.EP], F32) as g.diffT:
        conv_logits(nc, g, layer)
        edge_softmax(nc, g, layer, 1, 1.0 / H)
        conv_aggregate(nc, g, layer)
    conv_nodes(nc, g, layer, layer == 1)


def as_column(a):
    return a.reshape(-1, 1)


def as_row(a):
    return a.reshape(1, -1)


_WEIGHTS = {
    "w1T": ("L0_gnn_W1", np.transpose), "w2T": ("L0_gnn_W2", np.transpose),
    "b1": ("L0_gnn_b1", as_column), "b2": ("L0_gnn_b2", as_column),
    "gamma": ("L0_gnn_gamma", as_column), "beta": ("L0_gnn_beta", as_column),
    "wnT": ("L2_gnn_W_n", lambda a: a.transpose(1, 0, 2).reshape(D, HID)),
    "a_src": ("L2_gnn_a_src", as_row), "a_dst": ("L2_gnn_a_dst", as_row),
    "mw1": ("L2_gnn_mlp_W1", np.asarray), "mb1": ("L2_gnn_mlp_b1", as_row),
    "mw2": ("L2_gnn_mlp_W2", np.asarray), "mb2": ("L2_gnn_mlp_b2", as_row),
    "wl1": ("L1_gnn_Wl1", np.asarray), "wr1": ("L1_gnn_Wr1", np.asarray), "att1T": ("L1_gnn_att1", np.transpose),
    "cb1": ("L1_gnn_b1", as_row), "cg1": ("L1_gnn_g1", as_row), "cbe1": ("L1_gnn_be1", as_row),
    "wl2": ("L1_gnn_Wl2", np.asarray), "wr2": ("L1_gnn_Wr2", np.asarray), "att2T": ("L1_gnn_att2", np.transpose),
    "cb2": ("L1_gnn_b2", as_row), "cg2": ("L1_gnn_g2", as_row), "cbe2": ("L1_gnn_be2", as_row),
}


def layout(inputs):
    x, src, dst, ea = (np.asarray(inputs[k]) for k in ("x", "src", "dst", "edge_attr_128"))
    n, e = len(x), len(src)
    npad, epad = padded(n, NB), padded(e, K)

    def pad(a, rows, value=0):
        return np.concatenate([a, np.full((rows - len(a), *a.shape[1:]), value, a.dtype)])

    def tiles(a):
        return np.ascontiguousarray(a.reshape(-1, SUB, P).transpose(0, 2, 1))

    src, dst = pad(src, epad, n), pad(dst, epad, n)
    before, after = np.append(np.int32(-1), dst[:-1]), np.append(dst[1:], np.int32(-1))
    arrays = {
        "x": pad(x, npad), "ea": pad(ea, epad),
        "src_t": tiles(src), "dst_t": tiles(dst), "nxt_t": tiles(after),
        "dst_r": dst[None], "prev_r": before[None], "next_r": after[None],
    }
    for name, (source, turn) in _WEIGHTS.items():
        arrays[name] = np.ascontiguousarray(turn(np.asarray(inputs[source])))
    return arrays, (n, npad, epad)


def declare_and_build(nc, arrays, sizes, phases=99):
    g = Graph()
    g.N, g.NP, g.EP = sizes
    given = {name: nc.dram_tensor(name, a.shape, mybir.dt.from_np(a.dtype), kind="ExternalInput").ap()
             for name, a in arrays.items()}
    g.x, g.ea, g.src_t, g.dst_t, g.nxt_t, g.dst_r, g.prev_r, g.next_r = (
        given[n] for n in ("x", "ea", "src_t", "dst_t", "nxt_t", "dst_r", "prev_r", "next_r"))
    g.w1T, g.w2T, g.b1, g.b2, g.gamma, g.beta = (
        given[n] for n in ("w1T", "w2T", "b1", "b2", "gamma", "beta"))
    g.wnT, g.a_src, g.a_dst, g.mw1, g.mb1, g.mw2, g.mb2 = (
        given[n] for n in ("wnT", "a_src", "a_dst", "mw1", "mb1", "mw2", "mb2"))
    g.conv_weights = [tuple(given[f"{n}{j}{t}"] for n, t in (("wl", ""), ("wr", ""), ("att", "T"))) for j in (1, 2)]
    g.conv_norms = [tuple(given[f"{n}{j}"] for n in ("cb", "cg", "cbe")) for j in (1, 2)]
    g.out = nc.dram_tensor("out", (g.NP + g.EP, D), F32, kind="ExternalOutput").ap()
    build(nc, g, phases)


def kernel(**inputs):
    import concourse.bacc as bacc
    from concourse.bass_utils import run_bass_kernel_spmd

    arrays, sizes = layout(inputs)
    nc = bacc.Bacc("TRN2", target_bir_lowering=False, num_devices=1)
    declare_and_build(nc, arrays, sizes)
    result = run_bass_kernel_spmd(nc, [arrays], core_ids=[0])
    return result.results[0]["out"][:sizes[0]]
```

```python
import numpy as np
from contextlib import ExitStack

import concourse.bass as bass
from concourse import mybir

F32 = mybir.dt.float32
I32 = mybir.dt.int32
ALU = mybir.AluOpType
ACT = mybir.ActivationFunctionType
AX = mybir.AxisListType

P = 128
D = 128
H = 4
SUB = 4
TILE = P * SUB
K = 7
RING = 7
NB = 2 * RING
EPS = 1e-5
SLOPE = 0.2
BEHIND = 3
BIG = 1e30
CH = P // H
HID = 256
HD = 64


def cdiv(a, b):
    return -(-a // b)


def padded(n, tiles):
    return cdiv(n + 1, TILE * tiles) * TILE * tiles


class Phase:

    def __init__(self, nc, name):
        self.nc, self.name, self.stack, self.used = nc, name, ExitStack(), []

    def __enter__(self):
        self.stack.__enter__()
        return self

    def __exit__(self, *error):
        if error[0] is None:
            with self.nc.Block() as block:
                @block.gpsimd
                def _(pool):
                    for s in self.used:
                        pool.sem_clear(s)
        return self.stack.__exit__(*error)

    def sb(self, name, shape, dt=F32):
        return self.stack.enter_context(self.nc.sbuf_tensor(self.name + name, shape, dt))

    def ps(self, name, shape, dt=F32):
        return self.stack.enter_context(self.nc.psum_tensor(self.name + name, shape, dt))

    def sem(self, name):
        s = self.stack.enter_context(self.nc.semaphore(self.name + name))
        self.used.append(s)
        return s

    def sbs(self, name, shape, dt=F32, n=K):
        return [self.sb(f"{name}{k}", shape, dt) for k in range(n)]

    def sems(self, name, n=K):
        return [self.sem(f"{name}{k}") for k in range(n)]


def node_rows(table, n):
    return table[bass.ds(n * TILE, TILE), :].rearrange("(p a) d -> p a d", p=P)


def edge_rows(table, n):
    return table[bass.ds(n * TILE, TILE), :].rearrange("(s p) d -> p s d", p=P)


def edge_span(row, n, parts):
    return row[:, bass.ds(n * TILE, TILE)].to_broadcast([parts, TILE])


def broadcast_rows(sp, dst, src, done):
    sp.dma_start(dst, src.to_broadcast([P, dst.shape[1]])).then_inc(done, 16)


def prepare_indices(nc, g):
    nt, flat = g.NTE, g.EP // P
    with Phase(nc, "prepare_indices_") as m:
        idx = m.sb("idx", [P, nt, 16], I32)
        nxt = m.sb("nxt", [P, nt, SUB], I32)
        eid = m.sb("eid", [P, nt, SUB], I32)
        dstf, nxtf, same, dump = (m.sb(n, [P, nt, SUB]) for n in ("dstf", "nxtf", "same", "dump"))
        lastf, addf = m.sb("lastf", [P, nt, SUB]), m.sb("addf", [P, nt, SUB])
        rowi = m.sb("rowi", [P, 3, flat], I32)
        rowf = m.sb("rowf", [P, 3, flat])
        keep = m.sb("keep", [P, 2, flat])
        loaded, loaded_rows, ids_made, steps = m.sem("loaded"), m.sem("loaded_rows"), m.sem("ids_made"), m.sem("steps")
        idx_made, keep_made, stored = m.sem("idx_made"), m.sem("keep_made"), m.sem("stored")
        with nc.Block() as block:
            @block.sync
            def _(sp):
                tiles = lambda x: x.rearrange("t p s -> p t s")
                with nc.allow_non_contiguous_dma("four indices a run"):
                    sp.dma_start(idx[:, :, 0:4], tiles(g.src_t)).then_inc(loaded, 16)
                    sp.dma_start(idx[:, :, 4:8], tiles(g.dst_t)).then_inc(loaded, 16)
                    sp.dma_start(nxt[:, :, :], tiles(g.nxt_t)).then_inc(loaded, 16)
                for j, row in enumerate((g.dst_r, g.prev_r, g.next_r)):
                    sp.dma_start(rowi[:, j, :], row.rearrange("o (p j) -> (o p) j", p=P)).then_inc(loaded_rows, 16)
                sp.wait_ge(keep_made, 1)
                sp.dma_start(g.KEEP.rearrange("o (p j) -> (o p) j", p=P), keep[:, 0, :]).then_inc(stored, 16)
                sp.dma_start(g.KEEPN.rearrange("o (p j) -> (o p) j", p=P), keep[:, 1, :]).then_inc(stored, 16)
                sp.wait_ge(idx_made, 1)
                sp.dma_start(g.IDX.rearrange("t p s -> p t s"), idx[:, :, :]).then_inc(stored, 16)
                sp.wait_ge(stored, 3 * 16)

            @block.gpsimd
            def _(pool):
                pool.iota(eid[:, :, :], pattern=[[TILE, nt], [P, SUB]], base=0, channel_multiplier=1).then_inc(ids_made, 1)

            @block.vector
            def _(dve):
                count = [0]

                def step(instruction):
                    count[0] += 1
                    instruction.then_inc(steps, 1)
                    dve.wait_ge(steps, count[0])

                dve.wait_ge(loaded_rows, 3 * 16)
                step(dve.tensor_copy(rowf[:, :, :], rowi[:, :, :]))
                dve.tensor_tensor(keep[:, 0, :], rowf[:, 0, :], rowf[:, 1, :], ALU.is_equal)
                dve.tensor_tensor(keep[:, 1, :], rowf[:, 0, :], rowf[:, 2, :], ALU.is_equal).then_inc(keep_made, 1)
                dve.wait_ge(loaded, 3 * 16)
                dve.wait_ge(ids_made, 1)
                dve.tensor_copy(dstf[:, :, :], idx[:, :, 4:8])
                dve.tensor_copy(dump[:, :, :], eid[:, :, :])
                step(dve.tensor_copy(nxtf[:, :, :], nxt[:, :, :]))
                step(dve.tensor_tensor(same[:, :, :], dstf[:, :, :], nxtf[:, :, :], ALU.is_equal))
                dve.scalar_tensor_tensor(out=lastf[:, :, :], in0=same[:, :, :], scalar=float(g.NP), in1=dstf[:, :, :],
                                         op0=ALU.mult, op1=ALU.add)
                step(dve.scalar_tensor_tensor(out=dump[:, :, :], in0=dump[:, :, :], scalar=float(g.NP), in1=dstf[:, :, :],
                                              op0=ALU.add, op1=ALU.subtract))
                step(dve.tensor_tensor(addf[:, :, :], dump[:, :, :], same[:, :, :], ALU.mult))
                step(dve.tensor_tensor(addf[:, :, :], addf[:, :, :], dstf[:, :, :], ALU.add))
                dve.tensor_copy(idx[:, :, 8:12], lastf[:, :, :])
                dve.tensor_copy(idx[:, :, 12:16], addf[:, :, :]).then_inc(idx_made, 1)


def wait_alone(eng, sem, value, own):
    eng.wait_ge(sem, value)
    eng.sem_inc(own, 1)


def gather(pool, out, table, index):
    return pool.indirect_dma_start(out=out, out_offset=None, in_=table,
                                   in_offset=bass.IndirectOffsetOnAxis(ap=index, axis=0))


def scatter_last(pool, table, index, rows, bound):
    return pool.indirect_dma_start(out=table, out_offset=bass.IndirectOffsetOnAxis(ap=index, axis=0),
                                   in_=rows, in_offset=None, bounds_check=bound, oob_is_err=False)


def make_identity(pool, ident, made, cleared):
    pool.memset(ident[:, :], 0.0).then_inc(cleared, 1)
    pool.wait_ge(cleared, 1)
    pool.affine_select(out=ident[:, :], in_=ident[:, :], compare_op=ALU.not_equal, fill=1.0, base=0,
                       pattern=[[-1, P]], channel_multiplier=1).then_inc(made, 1)


class Norm:

    def __init__(self, m, name):
        self.stats, self.mv = m.sbs(f"{name}_stats", [P, SUB, 6]), m.sbs(f"{name}_mv", [P, SUB, 2])
        self.std, self.rstd = m.sbs(f"{name}_std", [P, SUB]), m.sbs(f"{name}_rstd", [P, SUB])
        self.shift = m.sbs(f"{name}_shift", [P, SUB])
        self.stats_done, self.own, self.mv_done = (m.sem(f"{name}_{n}") for n in ("stats_done", "own", "mv_done"))
        self.std_done, self.rstd_done, self.shift_done = (m.sem(f"{name}_{n}") for n in ("std_done", "rstd_done", "shift_done"))

    def take_stats(self, dve, x, k):
        for a in range(SUB):
            last = dve.bn_stats(out=self.stats[k][:, a, :], in_=x[:, a, :])
        last.then_inc(self.stats_done, 1)

    def moments(self, dve, k, done):
        dve.wait_ge(self.stats_done, done)
        dve.sem_inc(self.own, 1)
        for a in range(SUB):
            last = dve.bn_aggr(out=self.mv[k][:, a, :], in_=self.stats[k][:, a, :])
        last.then_inc(self.mv_done, 1)

    def root(self, act, k, done, eps):
        act.wait_ge(self.mv_done, done)
        act.activation(self.std[k][:, :], self.mv[k][:, :, 1], ACT.Sqrt, bias=eps[:, :]).then_inc(self.std_done, 1)

    def scales(self, dve, k, done):
        self.invert(dve, k, done)
        self.shifts(dve, k, done)

    def invert(self, dve, k, done):
        dve.wait_ge(self.std_done, done)
        dve.reciprocal(self.rstd[k][:, :], self.std[k][:, :]).then_inc(self.rstd_done, 1)

    def shifts(self, dve, k, done):
        dve.wait_ge(self.rstd_done, done)
        dve.scalar_tensor_tensor(out=self.shift[k][:, :], in0=self.mv[k][:, :, 0], scalar=-1.0, in1=self.rstd[k][:, :],
                                 op0=ALU.mult, op1=ALU.mult).then_inc(self.shift_done, 1)

    def apply(self, act, out, x, k, func):
        for a in range(SUB):
            last = act.activation(out[:, a, :], x[:, a, :], func,
                                  bias=self.shift[k][:, a:a + 1], scale=self.rstd[k][:, a:a + 1])
        return last


def past(eng, sem, value):
    if not isinstance(value, int) or value > 0:
        eng.wait_ge(sem, value)


def pipeline(eng, bodies, tiles, steps):
    def at(t, i, first):
        for lag, step in steps:
            k = t - lag
            if 0 <= k < tiles:
                step(k, i)
            elif k < 0 and not first:
                step(tiles + k, i - 1)

    for t in range(tiles):
        at(t, 0, True)
    if bodies > 1:
        with eng.Fori(1, bodies) as i:
            for t in range(tiles):
                at(t, i, False)
    for t in range(tiles, tiles + max(lag for lag, _ in steps)):
        at(t, bodies - 1, True)


def slot(k):
    return 2 if k == K - 1 else k % 2


def slot_before(k, i):
    earlier = [j for j in range(k) if slot(j) == slot(k)]
    if earlier:
        return earlier[-1], i
    return max(j for j in range(K) if slot(j) == slot(k)), i - 1


def rows_freed(eng, scattered, start, k, i):
    kb, ib = slot_before(k, i)
    if not isinstance(ib, int) or ib >= 0:
        eng.wait_ge(scattered[kb], (ib + 1) * 64 + start)


def slot_uses(k, i):
    return i if slot(k) == 2 else i * (K // 2) + k // 2


def slot_tiles(slot):
    return (K + 1 - slot) // 2


def run_bodies(eng, nb, body):
    with eng.Fori(0, nb) as i:
        body(i)


def turns(k, i):
    return i * (NB // RING) + k // RING


def node_stream(sp, nb, load, freed, store, lag):
    def load_next(k, i):
        if k < NB - RING or not isinstance(i, int) or i < nb - 1:
            freed(k, i)
            load((k + RING) % NB, i + (k + RING) // NB)

    for k in range(RING):
        load(k, 0)
    for t in range(NB):
        load_next(t, 0)
        if t >= lag:
            store(t - lag, 0)
    if nb > 2:
        with sp.Fori(1, nb - 1) as i:
            for t in range(NB):
                load_next(t, i)
                store((t - lag) % NB, i + (t - lag) // NB)
    for t in range(0 if nb > 1 else NB, NB + lag):
        if t < NB - RING:
            load_next(t, nb - 1)
        store((t - lag) % NB, nb - 1 + (t - lag) // NB)


def gine_edges(nc, g):
    nb = g.NTE // K
    fills = g.NP // (TILE * K)
    with Phase(nc, "gine_edges_") as m:
        ident, eps, zero = m.sb("ident", [P, P]), m.sb("eps", [P, 1]), m.sb("zero", [P, K * TILE])
        idx = m.sbs("idx", [P, 16], I32)
        hs, ea, msg = m.sbs("hs", [P, SUB, D]), m.sbs("ea", [P, SUB, D]), m.sbs("msg", [P, SUB, D])
        keep, msgT, sumT, rows = (m.sbs(n, [P, TILE]) for n in ("keep", "msgT", "sumT", "rows"))
        turned = [m.ps(f"turned{j}", [P, TILE]) for j in range(2)]
        back = [m.ps(f"back{j}", [P, TILE]) for j in range(2)]
        norm = Norm(m, "norm")
        idx_in, tile_in, own = m.sems("idx_in"), m.sems("tile_in"), m.sem("own")
        hs_in, agg_out = g.gathered, g.scattered
        hs0, agg0 = g.start(hs_in, nb * 64), g.start(agg_out, nb * 64)
        cleared, ident_made, tail_set, eps_set, zero_set, zeros_out = (
            m.sem(n) for n in ("cleared", "ident_made", "tail_set", "eps_set", "zero_set", "zeros_out"))
        h_made, msg_made, msgT_psum, msgT_made, scanned, back_psum, rows_made = (
            m.sem(n) for n in ("h_made", "msg_made", "msgT_psum", "msgT_made", "scanned", "back_psum", "rows_made"))
        with nc.Block() as block:
            @block.sync
            def _(sp):
                def load(k, i):
                    sp.dma_start(idx[k][:, :], g.IDX[bass.ds(i * K + k, 1), :, :].rearrange("t p s -> (t p) s")).then_inc(idx_in[k], 16)
                    sp.dma_start(ea[k][:, :, :], edge_rows(g.ea, i * K + k)).then_inc(tile_in[k], 16)
                    sp.dma_start(keep[k][:, :], edge_span(g.KEEP, i * K + k, P)).then_inc(tile_in[k], 16)

                for k in range(K):
                    load(k, 0)
                sp.wait_ge(zero_set, 1)
                for f in range(fills):
                    sp.dma_start(g.AGG[f * K * TILE:(f + 1) * K * TILE, :].rearrange("(p a) d -> p (a d)", p=P), zero[:, :]).then_inc(zeros_out, 16)
                if nb > 1:
                    with sp.Fori(1, nb) as i:
                        for k in range(K):
                            sp.wait_ge(agg_out[k], i * 64 + agg0)
                            load(k, i)

            @block.gpsimd
            def _(pool):
                make_identity(pool, ident, ident_made, cleared)

                def gather_tile(k, i):
                    wait_alone(pool, idx_in[k], (i + 1) * 16, own)
                    for s in range(SUB):
                        gather(pool, hs[k][:, s, :], g.x[:, :], idx[k][:, s:s + 1]).then_inc(hs_in[k], 16)

                def body(i, more):
                    for k in range(K):
                        wait_alone(pool, rows_made, i * K + k + 1, own)
                        for s in range(SUB):
                            scatter_last(pool, g.AGG[:, :], idx[k][:, 8 + s:9 + s], rows[k][:, s * P:(s + 1) * P],
                                         g.NP - 1).then_inc(agg_out[k], 16)
                        if more and k >= BEHIND:
                            gather_tile(k - BEHIND, i + 1)
                    if more:
                        for k in range(K - BEHIND, K):
                            gather_tile(k, i + 1)

                for k in range(K):
                    gather_tile(k, 0)
                pool.wait_ge(zeros_out, 16 * fills)
                if nb > 1:
                    with pool.Fori(0, nb - 1) as i:
                        body(i, True)
                body(nb - 1, False)
                for k in range(K):
                    pool.wait_ge(agg_out[k], nb * 64 + agg0)

            @block.vector
            def _(dve):
                dve.memset(zero[:, :], 0.0).then_inc(zero_set, 1)
                dve.memset(eps[:, :], EPS).then_inc(eps_set, 1)
                dve.memset(sumT[K - 1][:, TILE - 1:TILE], 0.0).then_inc(tail_set, 1)
                dve.wait_ge(tail_set, 1)

                def moments(k, i):
                    dve.wait_ge(hs_in[k], i * 64 + (64 + hs0))
                    norm.take_stats(dve, hs[k], k)
                    norm.moments(dve, k, i * K + k + 1)

                def scan(k, i):
                    n = i * K + k
                    dve.wait_ge(msgT_made, n + 1)
                    past(dve, scanned, n)
                    dve.tensor_tensor_scan(sumT[k][:, :], keep[k][:, :], msgT[k][:, :],
                                           sumT[k - 1][:, TILE - 1:TILE], ALU.mult, ALU.add).then_inc(scanned, 1)

                def add(k, i):
                    norm.scales(dve, k, i * K + k + 1)
                    dve.wait_ge(h_made, i * K + k + 1)
                    dve.wait_ge(tile_in[k], (i + 1) * 32)
                    dve.tensor_tensor(msg[k][:, :, :], hs[k][:, :, :], ea[k][:, :, :], ALU.add).then_inc(msg_made, 1)

                pipeline(dve, nb, K, [(0, moments), (1, scan), (0, add)])

            @block.tensor
            def _(pe):
                pe.wait_ge(ident_made, 1)

                def turn(k, i):
                    n = i * K + k
                    pe.wait_ge(msg_made, n + 1)
                    past(pe, msgT_made, n - 1 if k else n)
                    for s in range(SUB):
                        last = pe.transpose(turned[k % 2][:, s * P:(s + 1) * P], msg[k][:, s, :], ident[:, :])
                    last.then_inc(msgT_psum, 1)

                def turn_back(k, i):
                    n = i * K + k
                    pe.wait_ge(scanned, n + 1)
                    past(pe, rows_made, n - 1 if k else n)
                    for s in range(SUB):
                        last = pe.transpose(back[k % 2][:, s * P:(s + 1) * P], sumT[k][:, s * P:(s + 1) * P], ident[:, :])
                    last.then_inc(back_psum, 1)

                pipeline(pe, nb, K, [(1, turn_back), (0, turn)])

            @block.scalar
            def _(act):
                act.wait_ge(eps_set, 1)

                def normalize(k, i):
                    act.wait_ge(norm.shift_done, i * K + k + 1)
                    norm.apply(act, hs[k], hs[k], k, ACT.Relu).then_inc(h_made, 1)

                def copy_turned(k, i):
                    act.wait_ge(msgT_psum, i * K + k + 1)
                    act.activation(msgT[k][:, :], turned[k % 2][:, :], ACT.Relu).then_inc(msgT_made, 1)

                def copy_back(k, i):
                    act.wait_ge(back_psum, i * K + k + 1)
                    past(act, agg_out[k], i * 64 + agg0)
                    act.activation(rows[k][:, :], back[k % 2][:, :], ACT.Copy).then_inc(rows_made, 1)

                pipeline(act, nb, K, [
                    (0, lambda k, i: norm.root(act, k, i * K + k + 1, eps)),
                    (1, copy_back), (0, normalize), (0, copy_turned)])


def gine_mlp(nc, g):
    nb = g.NTN // NB
    flat = lambda t: t[:, :, :].rearrange("p a d -> p (a d)")
    with Phase(nc, "gine_mlp_") as m:
        ident = m.sb("ident", [P, P])
        w1, w2, b1, b2 = m.sb("w1", [D, D]), m.sb("w2", [D, D]), m.sb("b1", [D, 1]), m.sb("b2", [D, 1])
        gamma, beta, eps = m.sb("gamma", [D, 1]), m.sb("beta", [D, 1]), m.sb("eps", [P, 1])
        x, agg, h, s = (m.sbs(n, [P, SUB, D]) for n in ("x", "agg", "h", "s"))
        sT, hidT, yT = m.sbs("sT", [P, TILE]), m.sbs("hidT", [P, TILE]), m.sbs("yT", [P, TILE])
        y_stats, y_mv, y_std = m.sb("y_stats", [P, g.NTN, 6]), m.sb("y_mv", [P, 2]), m.sb("y_std", [P, 1])
        turned, hid, y = ([m.ps(f"{n}{j}", [P, TILE]) for j in range(2)] for n in ("turned", "hid", "y"))
        norm = Norm(m, "norm")
        tile_in, y_out = m.sems("tile_in"), m.sems("y_out")
        cleared, ident_made, weights_in, eps_set = (m.sem(n) for n in ("cleared", "ident_made", "weights_in", "eps_set"))
        h_made, s_made, turned_done, sT_made, hid_done, hidT_made, y_done, yT_made, y_measured = (
            m.sem(n) for n in ("h_made", "s_made", "turned_done", "sT_made", "hid_done", "hidT_made", "y_done", "yT_made", "y_measured"))
        own, steps, y_root, mv_ready = m.sem("own"), m.sem("steps"), m.sem("y_root"), m.sem("mv_ready")
        with nc.Block() as block:
            @block.sync
            def _(sp):
                def load(k, i):
                    r, n = k % RING, i * NB + k
                    sp.dma_start(x[r][:, :, :], node_rows(g.x, n)).then_inc(tile_in[r], 16)
                    sp.dma_start(agg[r][:, :, :], node_rows(g.AGG, n)).then_inc(tile_in[r], 16)
                    if k == 0 and isinstance(i, int) and i == 0:
                        for dst, src in ((w1, g.w1T), (w2, g.w2T), (b1, g.b1), (b2, g.b2), (gamma, g.gamma), (beta, g.beta)):
                            sp.dma_start(dst[:, :], src).then_inc(weights_in, 16)

                def freed(k, i):
                    sp.wait_ge(s_made, i * NB + k + 1)

                def store(k, i):
                    r, n = k % RING, i * NB + k
                    sp.wait_ge(yT_made, n + 1)
                    sp.dma_start(g.YT[bass.ds(n, 1), :, :].rearrange("t p j -> (t p) j"), yT[r][:, :]).then_inc(y_out[r], 16)

                node_stream(sp, nb, load, freed, store, 5)
                for r in range(RING):
                    sp.wait_ge(y_out[r], 16 * turns(r, nb))

            @block.gpsimd
            def _(pool):
                make_identity(pool, ident, ident_made, cleared)

                def add(k, i):
                    r, n = k % RING, i * NB + k
                    past(pool, turned_done, n + 1 - RING)
                    pool.wait_ge(h_made, n + 1)
                    pool.tensor_tensor(flat(s[r]), flat(h[r]), flat(agg[r]), ALU.add).then_inc(s_made, 1)

                pipeline(pool, nb, NB, [(0, add)])

            @block.vector
            def _(dve):
                dve.memset(eps[:, :], EPS).then_inc(eps_set, 1)
                dve.wait_ge(weights_in, 6 * 16)

                def take_stats(k, i):
                    r = k % RING
                    dve.wait_ge(tile_in[r], 32 * (turns(k, i) + 1))
                    norm.take_stats(dve, x[r], r)

                def copy_y(k, i):
                    r, n = k % RING, i * NB + k
                    dve.wait_ge(y_done, n + 1)
                    past(dve, y_out[r], 16 * turns(k, i))
                    dve.tensor_scalar(yT[r][:, :], y[k % 2][:, :], b2[:, :], None, ALU.add).then_inc(yT_made, 1)

                def measure_y(k, i):
                    n = i * NB + k
                    dve.wait_ge(yT_made, n + 1)
                    dve.bn_stats(out=y_stats[:, bass.ds(n, 1), :].rearrange("p t c -> p (t c)"), in_=yT[k % RING][:, :]).then_inc(y_measured, 1)

                pipeline(dve, nb, NB, [
                    (0, take_stats),
                    (9, copy_y),
                    (1, lambda k, i: norm.moments(dve, k % RING, i * NB + k + 1)),
                    (3, lambda k, i: norm.scales(dve, k % RING, i * NB + k + 1)),
                    (9, measure_y)])
                dve.wait_ge(y_measured, g.NTN)
                used = g.NTN
                for r in range(RING):
                    t = g.NTN - RING + r
                    real = min(max(g.N - t * TILE, 0), TILE) // SUB
                    if real == 0:
                        used = min(used, t)
                    elif real < P:
                        dve.bn_stats(out=y_stats[:, t, :], in_=yT[r][:, :].rearrange("p (a j) -> p a j", a=SUB)[:, :, 0:real]).then_inc(own, 1)
                        dve.wait_ge(own, 1)
                dve.bn_aggr(out=y_mv[:, :], in_=y_stats[:, 0:used, :].rearrange("p t c -> p (t c)")).then_inc(mv_ready, 1)
                dve.wait_ge(y_root, 1)
                dve.reciprocal(y_std[:, :], y_std[:, :]).then_inc(steps, 1)
                dve.wait_ge(steps, 1)
                dve.tensor_tensor(g.bn_scale[:, :], y_std[:, :], gamma[:, :], ALU.mult).then_inc(steps, 1)
                dve.wait_ge(steps, 2)
                dve.tensor_tensor(g.bn_shift[:, :], y_mv[:, 0:1], g.bn_scale[:, :], ALU.mult).then_inc(steps, 1)
                dve.wait_ge(steps, 3)
                dve.tensor_tensor(g.bn_shift[:, :], beta[:, :], g.bn_shift[:, :], ALU.subtract)

            @block.tensor
            def _(pe):
                pe.wait_ge(ident_made, 1)
                pe.wait_ge(weights_in, 6 * 16)

                def turn(k, i):
                    r, n = k % RING, i * NB + k
                    pe.wait_ge(s_made, n + 1)
                    past(pe, sT_made, n - 1)
                    for a in range(SUB):
                        last = pe.transpose(turned[k % 2][:, a * P:(a + 1) * P], s[r][:, a, :], ident[:, :])
                    last.then_inc(turned_done, 1)

                def first(k, i):
                    n = i * NB + k
                    pe.wait_ge(sT_made, n + 1)
                    past(pe, hidT_made, n - 1)
                    pe.matmul(hid[k % 2][:, :], w1[:, :], sT[k % RING][:, :], start=True, stop=True).then_inc(hid_done, 1)

                def second(k, i):
                    n = i * NB + k
                    pe.wait_ge(hidT_made, n + 1)
                    past(pe, yT_made, n - 1)
                    pe.matmul(y[k % 2][:, :], w2[:, :], hidT[k % RING][:, :], start=True, stop=True).then_inc(y_done, 1)

                pipeline(pe, nb, NB, [(0, turn), (1, first), (2, second)])

            @block.scalar
            def _(act):
                act.wait_ge(eps_set, 1)
                act.wait_ge(weights_in, 6 * 16)

                def normalize(k, i):
                    r, n = k % RING, i * NB + k
                    act.wait_ge(norm.shift_done, n + 1)
                    past(act, s_made, n + 1 - RING)
                    norm.apply(act, h[r], x[r], r, ACT.Relu).then_inc(h_made, 1)

                def copy_turned(k, i):
                    n = i * NB + k
                    act.wait_ge(turned_done, n + 1)
                    past(act, hid_done, n + 1 - RING)
                    act.activation(sT[k % RING][:, :], turned[k % 2][:, :], ACT.Copy).then_inc(sT_made, 1)

                def hidden(k, i):
                    n = i * NB + k
                    act.wait_ge(hid_done, n + 1)
                    past(act, y_done, n + 1 - RING)
                    act.activation(hidT[k % RING][:, :], hid[k % 2][:, :], ACT.Relu, bias=b1[:, :]).then_inc(hidT_made, 1)

                pipeline(act, nb, NB, [
                    (0, lambda k, i: norm.root(act, k % RING, i * NB + k + 1, eps)),
                    (2, normalize), (4, copy_turned), (6, hidden)])
                act.wait_ge(mv_ready, 1)
                act.activation(y_std[:, :], y_mv[:, 1:2], ACT.Sqrt, bias=eps[:, :]).then_inc(y_root, 1)


def gine_finish(nc, g):
    nb = g.NTN // NB
    with Phase(nc, "gine_finish_") as m:
        ident, eps = m.sb("ident", [P, P]), m.sb("eps", [P, 1])
        x, yT, bT = m.sbs("x", [P, SUB, D]), m.sbs("yT", [P, TILE]), m.sbs("bT", [P, TILE])
        x1, h1, x1_beta = (m.sbs(n, [P, SUB, D]) for n in ("x1", "h1", "x1_beta"))
        beta, beta_in, shifted_made, own = m.sb("beta", [P, SUB, D]), m.sem("beta_in"), m.sem("shifted_made"), m.sem("own")
        rows = [m.ps(f"rows{j}", [P, SUB, D]) for j in range(RING)]
        norm = Norm(m, "norm")
        tile_in, out = m.sems("tile_in"), m.sems("out")
        cleared, ident_made, eps_set = (m.sem(n) for n in ("cleared", "ident_made", "eps_set"))
        bT_made, rows_done, x1_made, h1_made = (m.sem(n) for n in ("bT_made", "rows_done", "x1_made", "h1_made"))
        with nc.Block() as block:
            @block.sync
            def _(sp):
                for a in range(SUB):
                    broadcast_rows(sp, beta[:, a, :], g.conv_norms[1][2], beta_in)

                def load(k, i):
                    r, n = k % RING, i * NB + k
                    sp.dma_start(x[r][:, :, :], node_rows(g.x, n)).then_inc(tile_in[r], 16)
                    sp.dma_start(yT[r][:, :], g.YT[bass.ds(n, 1), :, :].rearrange("t p j -> (t p) j")).then_inc(tile_in[r], 16)

                def freed(k, i):
                    sp.wait_ge(x1_made, i * NB + k + 1)

                def store(k, i):
                    r, n = k % RING, i * NB + k
                    sp.wait_ge(h1_made, n + 1)
                    sp.wait_ge(shifted_made, n + 1)
                    sp.dma_start(node_rows(g.X, n), x1_beta[r][:, :, :]).then_inc(out[r], 16)
                    sp.dma_start(node_rows(g.H, n), h1[r][:, :, :]).then_inc(out[r], 16)

                node_stream(sp, nb, load, freed, store, 4)
                for r in range(RING):
                    sp.wait_ge(out[r], 32 * turns(r, nb))

            @block.gpsimd
            def _(pool):
                make_identity(pool, ident, ident_made, cleared)
                pool.wait_ge(beta_in, 16 * SUB)

                def add_beta(k, i):
                    r, n = k % RING, i * NB + k
                    wait_alone(pool, x1_made, n + 1, own)
                    past(pool, out[r], 32 * turns(k, i))
                    pool.tensor_tensor(x1_beta[r][:, :, :], x1[r][:, :, :], beta[:, :, :], ALU.add).then_inc(shifted_made, 1)

                pipeline(pool, nb, NB, [(0, add_beta)])

            @block.tensor
            def _(pe):
                pe.wait_ge(ident_made, 1)

                def turn(k, i):
                    r, n = k % RING, i * NB + k
                    pe.wait_ge(bT_made, n + 1)
                    past(pe, x1_made, n + 1 - RING)
                    for a in range(SUB):
                        last = pe.transpose(rows[r][:, a, :], bT[r][:, a * P:(a + 1) * P], ident[:, :])
                    last.then_inc(rows_done, 1)

                pipeline(pe, nb, NB, [(0, turn)])

            @block.vector
            def _(dve):
                dve.memset(eps[:, :], EPS).then_inc(eps_set, 1)

                def add(k, i):
                    r = k % RING
                    dve.wait_ge(rows_done, i * NB + k + 1)
                    past(dve, out[r], 32 * turns(k, i))
                    dve.tensor_tensor(x1[r][:, :, :], rows[r][:, :, :], x[r][:, :, :], ALU.add).then_inc(x1_made, 1)

                def take_stats(k, i):
                    dve.wait_ge(x1_made, i * NB + k + 1)
                    norm.take_stats(dve, x1[k % RING], k % RING)

                pipeline(dve, nb, NB, [
                    (0, add),
                    (1, lambda k, i: norm.moments(dve, k % RING, i * NB + k + 1)),
                    (3, lambda k, i: norm.scales(dve, k % RING, i * NB + k + 1)),
                    (0, take_stats)])

            @block.scalar
            def _(act):
                act.wait_ge(eps_set, 1)

                def batch_norm(k, i):
                    r, n = k % RING, i * NB + k
                    act.wait_ge(tile_in[r], 32 * (turns(k, i) + 1))
                    past(act, rows_done, n + 1 - RING)
                    act.activation(bT[r][:, :], yT[r][:, :], ACT.Identity, bias=g.bn_shift[:, :], scale=g.bn_scale[:, :]).then_inc(bT_made, 1)

                def normalize(k, i):
                    r = k % RING
                    act.wait_ge(norm.shift_done, i * NB + k + 1)
                    past(act, out[r], 32 * turns(k, i))
                    norm.apply(act, h1[r], x1[r], r, ACT.Relu).then_inc(h1_made, 1)

                pipeline(act, nb, NB, [
                    (0, batch_norm),
                    (3, lambda k, i: norm.root(act, k % RING, i * NB + k + 1, eps)),
                    (5, normalize)])


def conv_logits(nc, g, layer):
    nb = g.NTE // K
    with Phase(nc, f"conv_logits{layer}_") as m:
        ident, wr, att = m.sb("ident", [P, P]), m.sb("wr", [D, H * D]), m.sb("att", [D, H, 32])
        idx = m.sbs("idx", [P, 16], I32)
        hs, hd, hdT = m.sbs("hs", [P, SUB, D]), m.sbs("hd", [P, SUB, D]), m.sbs("hdT", [P, TILE], n=3)
        sloped, leaky = m.sbs("sloped", [P, TILE], n=2 * H), m.sbs("leaky", [P, TILE], n=2 * H)
        logit = [m.sbs(f"logit{j}_", [P, TILE], n=3) for j in range(2)]
        hsT_ps, hdT_ps = m.ps("hsT_ps", [P, TILE]), m.ps("hdT_ps", [P, TILE])
        z = [m.ps(f"z{h}", [P, TILE]) for h in range(H)]
        dots = [m.ps(f"dots{j}", [P, TILE]) for j in range(2)]
        idx_in, rows_in, own = m.sems("idx_in"), g.gathered, m.sem("own")
        rows0 = g.start(rows_in, nb * 128)
        logit_out = [m.sems(f"logit_out{j}_", 3) for j in range(2)]
        cleared, ident_made, weights_in, att_set, weights_made = (
            m.sem(n) for n in ("cleared", "ident_made", "weights_in", "att_set", "weights_made"))
        turned_done, hdT_made, diff_made, mean_step = (m.sem(n) for n in ("turned_done", "hdT_made", "diff_made", "mean_step"))
        z_done, sloped_made = ([m.sem(f"{n}{j}") for j in range(2)] for n in ("z_done", "sloped_made"))
        leaky_made, dots_done, logit_made = ([m.sem(f"{n}{j}") for j in range(2)] for n in ("leaky_made", "dots_done", "logit_made"))
        with nc.Block() as block:
            @block.sync
            def _(sp):
                wl_in, wr_in, att_in = g.conv_weights[layer]
                sp.dma_start(g.wl[:, :], wl_in).then_inc(weights_in, 16)
                sp.dma_start(wr[:, :], wr_in).then_inc(weights_in, 16)
                sp.wait_ge(att_set, 1)
                with nc.allow_non_contiguous_dma("a column of each head"):
                    sp.dma_start(att[:, :, 0:1], att_in.rearrange("d (h o) -> d h o", o=1)).then_inc(weights_in, 16)

                def load(k, i):
                    sp.dma_start(idx[k][:, :], g.IDX[bass.ds(i * K + k, 1), :, :].rearrange("t p s -> (t p) s")).then_inc(idx_in[k], 16)

                def store(j, k, i):
                    sp.wait_ge(logit_made[j], i * K + k + 1)
                    sp.dma_start(g.LOGIT[j][:, bass.ds((i * K + k) * TILE, TILE)], logit[j][slot(k)][0:P:32, :]).then_inc(logit_out[j][slot(k)], 16)

                def body(i, more):
                    for k in range(K):
                        store(0, k, i)
                        store(1, k, i)
                        if more:
                            load(k, i + 1)

                for k in range(K):
                    load(k, 0)
                if nb > 1:
                    with sp.Fori(0, nb - 1) as i:
                        body(i, True)
                body(nb - 1, False)
                for j in range(2):
                    for k in (0, 1, K - 1):
                        sp.wait_ge(logit_out[j][slot(k)], 16 * slot_uses(k, nb) - 16 * slot_uses(k, 0))

            @block.gpsimd
            def _(pool):
                make_identity(pool, ident, ident_made, cleared)

                def gather_tile(k, i):
                    wait_alone(pool, idx_in[k], (i + 1) * 16, own)
                    for s in range(SUB):
                        gather(pool, hd[k][:, s, :], g.H[:, :], idx[k][:, 4 + s:5 + s]).then_inc(rows_in[k], 16)
                        gather(pool, hs[k][:, s, :], g.H[:, :], idx[k][:, s:s + 1]).then_inc(rows_in[k], 16)

                for k in range(K):
                    gather_tile(k, 0)
                if nb > 1:
                    with pool.Fori(1, nb) as i:
                        for k in range(K):
                            pool.wait_ge(turned_done, (i - 1) * K + k + 1)
                            gather_tile(k, i)

            @block.tensor
            def _(pe):
                pe.wait_ge(ident_made, 1)
                pe.wait_ge(weights_made, 1)

                def turn(k, i):
                    pe.wait_ge(rows_in[k], i * 128 + (128 + rows0))
                    past(pe, diff_made, i * K + k)
                    for s in range(SUB):
                        pe.transpose(hdT_ps[:, s * P:(s + 1) * P], hd[k][:, s, :], ident[:, :])
                    for s in range(SUB):
                        last = pe.transpose(hsT_ps[:, s * P:(s + 1) * P], hs[k][:, s, :], ident[:, :])
                    last.then_inc(turned_done, 1)

                def z_self(k, i):
                    n = i * K + k
                    pe.wait_ge(hdT_made, n + 1)
                    for h in range(H):
                        past(pe, leaky_made[1], H * (n - 1) + h + 1)
                        pe.matmul(z[h][:, :], g.wsum[:, h * D:(h + 1) * D], hdT[slot(k)][:, :],
                                  start=True, stop=True).then_inc(z_done[0], 1)

                def z_edge(k, i):
                    n = i * K + k
                    pe.wait_ge(diff_made, n + 1)
                    for h in range(H):
                        pe.wait_ge(leaky_made[0], H * n + h + 1)
                        pe.matmul(z[h][:, :], g.wl[:, h * D:(h + 1) * D], g.diffT[:, bass.ds(n * TILE, TILE)],
                                  start=False, stop=True, skip_group_check=True).then_inc(z_done[1], 1)

                def dot(j):
                    def step(k, i):
                        n = i * K + k
                        pe.wait_ge(leaky_made[j], H * n + H)
                        past(pe, logit_made[j], n)
                        for h in range(H):
                            last = pe.matmul(dots[j][32 * h:32 * h + 32, :], att[:, h, :], leaky[H * j + h][:, :],
                                             start=True, stop=True, tile_position=(0, 32 * h))
                        last.then_inc(dots_done[j], 1)
                    return step

                pipeline(pe, nb, K, [(1, z_self), (2, dot(1)), (0, turn), (1, z_edge), (1, dot(0))])

            @block.scalar
            def _(act):
                def copy_dst(k, i):
                    n = i * K + k
                    act.wait_ge(turned_done, n + 1)
                    past(act, z_done[0], H * (n - 1))
                    past(act, diff_made, n - 1)
                    act.activation(hdT[slot(k)][:, :], hdT_ps[:, :], ACT.Copy).then_inc(hdT_made, 1)

                def slope(j):
                    def step(k, i):
                        for h in range(H):
                            act.wait_ge(z_done[j], H * (i * K + k) + h + 1)
                            act.activation(sloped[H * j + h][:, :], z[h][:, :], ACT.Copy, scale=SLOPE).then_inc(sloped_made[j], 1)
                    return step

                def copy_dots(j):
                    def step(k, i):
                        act.wait_ge(dots_done[j], i * K + k + 1)
                        past(act, logit_out[j][slot(k)], 16 * slot_uses(k, i))
                        act.activation(logit[j][slot(k)][:, :], dots[j][:, :], ACT.Copy).then_inc(logit_made[j], 1)
                    return step

                pipeline(act, nb, K, [(1, slope(0)), (2, copy_dots(1)), (0, copy_dst), (1, slope(1)), (1, copy_dots(0))])

            @block.vector
            def _(dve):
                dve.memset(att[:, :, :], 0.0).then_inc(att_set, 1)
                dve.wait_ge(weights_in, 48)
                dve.tensor_tensor(g.wmean[:, :], g.wl[:, 0:D], g.wl[:, D:2 * D], ALU.add).then_inc(mean_step, 1)
                for h in range(2, H):
                    dve.wait_ge(mean_step, h - 1)
                    dve.tensor_tensor(g.wmean[:, :], g.wmean[:, :], g.wl[:, h * D:(h + 1) * D], ALU.add).then_inc(mean_step, 1)
                dve.wait_ge(mean_step, H - 1)
                dve.tensor_scalar(g.wmean[:, :], g.wmean[:, :], 1.0 / H, None, ALU.mult)
                dve.tensor_tensor(g.wsum[:, :], g.wl[:, :], wr[:, :], ALU.add).then_inc(weights_made, 1)

                def diff(k, i):
                    n = i * K + k
                    dve.wait_ge(hdT_made, n + 1)
                    dve.tensor_tensor(g.diffT[:, bass.ds(n * TILE, TILE)], hsT_ps[:, :], hdT[slot(k)][:, :],
                                      ALU.subtract).then_inc(diff_made, 1)

                def leak(j):
                    def step(k, i):
                        n = i * K + k
                        for h in range(H):
                            dve.wait_ge(sloped_made[j], H * n + h + 1)
                            if h == 0:
                                past(dve, dots_done[j], n)
                            dve.tensor_tensor(leaky[H * j + h][:, :], z[h][:, :], sloped[H * j + h][:, :],
                                              ALU.max).then_inc(leaky_made[j], 1)
                    return step

                pipeline(dve, nb, K, [(1, leak(0)), (0, diff), (1, leak(1))])


def edge_softmax(nc, g, layer, self_loops, share):
    J = g.EP // CH
    with Phase(nc, f"edge_softmax{layer}_") as m:
        ident, zero = m.sb("ident", [P, P]), m.sb("zero", [P, J])
        e, es, ex, exs, top, run, total, weight = (m.sb(n, [P, J]) for n in ("e", "es", "ex", "exs", "top", "run", "total", "weight"))
        keep = [m.sb(f"keep{b}", [P, J]) for b in range(2)]
        cut = [m.sb(f"cut{b}", [P, J]) for b in range(2)]
        lead = [m.sb(f"lead{b}", [P, J]) for b in range(2)]
        leadcut = [m.sb(f"leadcut{b}", [P, J]) for b in range(2)]
        whole, wholecut = m.sb("whole", [1, 2, P]), m.sb("wholecut", [1, 2, P])
        ends, carry = m.sb("ends", [1, P + 2]), m.sb("carry", [P, 1])
        row, col = m.ps("row", [1, P]), m.ps("col", [P, 1])
        loaded, cleared, ident_made, steps, turn_done, diff_done, exp_done, asked, alpha_made, alpha_out = (
            m.sem(n) for n in ("loaded", "cleared", "ident_made", "steps", "turn_done", "diff_done", "exp_done", "asked", "alpha_made", "alpha_out"))
        n_loads = 8 + 1 + self_loops
        flat = lambda table: table.rearrange("h (c j) -> (h c) j", j=J)
        end = lambda b: 0 if b else J - 1
        with nc.Block() as block:
            @block.sync
            def _(sp):
                for b, table in enumerate((g.KEEP, g.KEEPN)):
                    for h in range(H):
                        sp.dma_start(keep[b][CH * h:CH * (h + 1), :], table.rearrange("o (c j) -> (o c) j", j=J)).then_inc(loaded, 16)
                sp.dma_start(e[:, :], flat(g.LOGIT[1])).then_inc(loaded, 16)
                if self_loops:
                    sp.dma_start(es[:, :], flat(g.LOGIT[0])).then_inc(loaded, 16)
                sp.wait_ge(alpha_made, 1)
                sp.dma_start(flat(g.ALPHA), weight[:, :]).then_inc(alpha_out, 16)
                sp.wait_ge(alpha_out, 16)

            @block.gpsimd
            def _(pool):
                make_identity(pool, ident, ident_made, cleared)

            @block.vector
            def _(dve):
                count, turned = [0], [0]

                def step(instruction):
                    count[0] += 1
                    instruction.then_inc(steps, 1)
                    dve.wait_ge(steps, count[0])

                def turn():
                    dve.sem_inc(asked, 1)
                    turned[0] += 1
                    dve.wait_ge(turn_done, turned[0])

                order = lambda x, b: x[:, ::-1] if b else x[:, :]
                def join(b, local, op_carry, op_in, out):
                    turn()
                    inner = ends[:, 1:P + 1]
                    data0 = wholecut[:, b, :] if op_carry == ALU.add else whole[:, b, :]
                    step(dve.tensor_tensor_scan(inner[:, ::-1] if b else inner, data0[:, ::-1] if b else data0,
                                                row[:, ::-1] if b else row[:, :], -BIG if op_carry == ALU.add else 0.0, op_carry, op_in))
                    turn()
                    step(dve.tensor_copy(carry[:, :], col[:, :]))
                    step(dve.scalar_tensor_tensor(out=out[:, :], in0=(leadcut if op_carry == ALU.add else lead)[b][:, :], scalar=carry[:, :],
                                                  in1=local[:, :], op0=op_carry, op1=op_in))

                step(dve.memset(zero[:, :], 0.0))
                step(dve.memset(ends[:, :], 0.0))
                dve.wait_ge(loaded, 16 * n_loads)
                for b in range(2):
                    dve.tensor_scalar(cut[b][:, :], keep[b][:, :], -1.0, BIG, ALU.add, ALU.mult)
                    step(dve.tensor_tensor_scan(order(lead[b], b), order(keep[b], b), zero[:, :], 1.0, ALU.mult, ALU.add))
                    dve.tensor_scalar(leadcut[b][:, :], lead[b][:, :], -1.0, BIG, ALU.add, ALU.mult)
                    turn()
                    step(dve.tensor_copy(whole[:, b, :], row[:, :]))
                    step(dve.tensor_scalar(wholecut[:, b, :], whole[:, b, :], -1.0, BIG, ALU.add, ALU.mult))
                if self_loops:
                    step(dve.tensor_tensor(top[:, :], e[:, :], es[:, :], ALU.max))
                    most = top
                else:
                    most = e
                step(dve.tensor_tensor_scan(run[:, :], cut[0][:, :], most[:, :], -BIG, ALU.add, ALU.max))
                join(0, run, ALU.add, ALU.max, total)
                step(dve.tensor_tensor_scan(order(run, 1), order(cut[1], 1), order(total, 1), -BIG, ALU.add, ALU.max))
                join(1, run, ALU.add, ALU.max, top)
                if self_loops:
                    dve.tensor_tensor(es[:, :], es[:, :], top[:, :], ALU.subtract)
                dve.tensor_tensor(e[:, :], e[:, :], top[:, :], ALU.subtract).then_inc(diff_done, 1)
                dve.wait_ge(exp_done, 1 + self_loops)
                step(dve.tensor_tensor_scan(run[:, :], keep[0][:, :], ex[:, :], 0.0, ALU.mult, ALU.add))
                join(0, run, ALU.mult, ALU.add, total)
                step(dve.scalar_tensor_tensor(out=total[:, :], in0=keep[1][:, :], scalar=-1.0, in1=total[:, :],
                                              op0=ALU.add, op1=ALU.mult))
                step(dve.tensor_tensor_scan(order(run, 1), order(keep[1], 1), order(total, 1), 0.0, ALU.mult, ALU.add))
                join(1, run, ALU.mult, ALU.add, total)
                if self_loops:
                    step(dve.tensor_tensor(total[:, :], exs[:, :], total[:, :], ALU.subtract))
                else:
                    step(dve.tensor_scalar(total[:, :], total[:, :], -1.0, None, ALU.mult))
                step(dve.reciprocal(total[:, :], total[:, :]))
                dve.scalar_tensor_tensor(out=weight[:, :], in0=ex[:, :], scalar=share, in1=total[:, :],
                                         op0=ALU.mult, op1=ALU.mult).then_inc(alpha_made, 1)

            @block.scalar
            def _(act):
                act.wait_ge(diff_done, 1)
                act.activation(ex[:, :], e[:, :], ACT.Exp).then_inc(exp_done, 1)
                if self_loops:
                    act.activation(exs[:, :], es[:, :], ACT.Exp).then_inc(exp_done, 1)

            @block.tensor
            def _(pe):
                pe.wait_ge(ident_made, 1)
                count = [0]

                def column(source, b):
                    count[0] += 1
                    pe.wait_ge(asked, count[0])
                    pe.matmul(row[:, :], source[:, end(b):end(b) + 1], ident[:, :], start=True, stop=True).then_inc(turn_done, 1)

                def carries(b):
                    count[0] += 1
                    pe.wait_ge(asked, count[0])
                    pe.matmul(col[:, :], ends[:, 2 * b:2 * b + P], ident[0:1, 0:1], start=True, stop=True).then_inc(turn_done, 1)

                for b in range(2):
                    column(lead[b], b)
                for _ in ("maximum", "sum"):
                    for b in range(2):
                        column(run, b)
                        carries(b)


def conv_aggregate(nc, g, layer):
    nb = g.NTE // K
    fills = g.EP // (TILE * K) if layer == 0 else 0
    with Phase(nc, f"conv_aggregate{layer}_") as m:
        ident = m.sb("ident", [P, P])
        idx = m.sbs("idx", [P, 16], I32)
        alphaT, keep = m.sbs("alphaT", [H, TILE]), m.sbs("keep", [P, TILE])
        alpha, diff = m.sbs("alpha", [P, SUB * H], n=3), m.sbs("diff", [P, TILE], n=3)
        part, sumT, rows = m.sbs("part", [P, SUB, D], n=3), m.sbs("sumT", [P, TILE], n=3), m.sbs("rows", [P, TILE])
        y = [m.ps(f"y{s}", [P, H * D]) for s in range(SUB)]
        alpha_ps, partT, back = m.ps("alpha_ps", [P, SUB * H]), m.ps("partT", [P, TILE]), m.ps("back", [P, TILE])
        tile_in, agg_out, own = m.sems("tile_in"), g.scattered, m.sem("own")
        agg0 = g.start(agg_out, nb * 64)
        cleared, ident_made, tail_set, zero_set, zeros_out = (
            m.sem(n) for n in ("cleared", "ident_made", "tail_set", "zero_set", "zeros_out"))
        zero = m.sb("zero", [P, K * TILE]) if fills else None
        alpha_turned, alpha_made, diff_copied, y_done, part_step, part_made = (
            m.sem(n) for n in ("alpha_turned", "alpha_made", "diff_copied", "y_done", "part_step", "part_made"))
        partT_done, scanned, back_done, rows_made = (m.sem(n) for n in ("partT_done", "scanned", "back_done", "rows_made"))
        with nc.Block() as block:
            @block.sync
            def _(sp):
                def load(k, i):
                    n = i * K + k
                    sp.dma_start(idx[k][:, :], g.IDX[bass.ds(n, 1), :, :].rearrange("t p s -> (t p) s")).then_inc(tile_in[k], 16)
                    sp.dma_start(alphaT[k][:, :], g.ALPHA[:, bass.ds(n * TILE, TILE)]).then_inc(tile_in[k], 16)
                    sp.dma_start(keep[k][:, :], edge_span(g.KEEP, n, P)).then_inc(tile_in[k], 16)

                for k in range(K):
                    load(k, 0)
                if fills:
                    sp.wait_ge(zero_set, 1)
                for f in range(fills):
                    sp.dma_start(g.out[g.NP + f * K * TILE:g.NP + (f + 1) * K * TILE, :].rearrange("(p a) d -> p (a d)", p=P),
                                 zero[:, :]).then_inc(zeros_out, 16)
                if nb > 1:
                    with sp.Fori(1, nb) as i:
                        for k in range(K):
                            sp.wait_ge(agg_out[k], i * 64 + agg0)
                            load(k, i)
                if fills:
                    sp.wait_ge(zeros_out, 16 * fills)

            @block.gpsimd
            def _(pool):
                make_identity(pool, ident, ident_made, cleared)
                if fills:
                    pool.memset(zero[:, :], 0.0).then_inc(zero_set, 1)

                def body(i):
                    for k in range(K):
                        wait_alone(pool, rows_made, i * K + k + 1, own)
                        for s in range(SUB):
                            scatter_last(pool, g.AGG[:, :], idx[k][:, 8 + s:9 + s], rows[k][:, s * P:(s + 1) * P],
                                         g.NP - 1).then_inc(agg_out[k], 16)

                run_bodies(pool, nb, body)
                for k in range(K):
                    pool.wait_ge(agg_out[k], nb * 64 + agg0)

            @block.tensor
            def _(pe):
                pe.wait_ge(ident_made, 1)

                def turn_alpha(k, i):
                    pe.wait_ge(tile_in[k], (i + 1) * 48)
                    past(pe, alpha_made, i * K + k)
                    for s in range(SUB):
                        last = pe.matmul(alpha_ps[:, s * H:(s + 1) * H], alphaT[k][:, s * P:(s + 1) * P], ident[0:H, 0:H],
                                         start=True, stop=True)
                    last.then_inc(alpha_turned, 1)

                def project(k, i):
                    n = i * K + k
                    pe.wait_ge(diff_copied, n + 1)
                    for s in range(SUB):
                        if s % 2 == 0:
                            past(pe, part_made, 2 * (n - 1) + s // 2 + 1)
                        pe.matmul(y[s][:, :], diff[slot(k)][:, s * P:(s + 1) * P], g.wl[:, :], start=True, stop=True).then_inc(y_done, 1)

                def turn(k, i):
                    n = i * K + k
                    pe.wait_ge(part_made, 2 * n + 2)
                    past(pe, scanned, n)
                    for s in range(SUB):
                        last = pe.transpose(partT[:, s * P:(s + 1) * P], part[slot(k)][:, s, :], ident[:, :])
                    last.then_inc(partT_done, 1)

                def turn_back(k, i):
                    n = i * K + k
                    pe.wait_ge(scanned, n + 1)
                    past(pe, rows_made, n)
                    for s in range(SUB):
                        last = pe.transpose(back[:, s * P:(s + 1) * P], sumT[slot(k)][:, s * P:(s + 1) * P], ident[:, :])
                    last.then_inc(back_done, 1)

                pipeline(pe, nb, K, [(0, turn_alpha), (1, project), (2, turn), (3, turn_back)])

            @block.scalar
            def _(act):
                def copy_alpha(k, i):
                    n = i * K + k
                    act.wait_ge(alpha_turned, n + 1)
                    past(act, part_made, 2 * (n - 1))
                    act.activation(alpha[slot(k)][:, :], alpha_ps[:, :], ACT.Copy).then_inc(alpha_made, 1)

                def copy_diff(k, i):
                    n = i * K + k
                    past(act, y_done, SUB * (n - 1))
                    act.activation(diff[slot(k)][:, :], g.diffT[:, bass.ds(n * TILE, TILE)], ACT.Copy).then_inc(diff_copied, 1)

                def copy_rows(k, i):
                    act.wait_ge(back_done, i * K + k + 1)
                    past(act, agg_out[k], i * 64 + agg0)
                    act.activation(rows[k][:, :], back[:, :], ACT.Copy).then_inc(rows_made, 1)

                pipeline(act, nb, K, [(0, copy_alpha), (0, copy_diff), (4, copy_rows)])

            @block.vector
            def _(dve):
                for j in range(3):
                    dve.memset(sumT[j][:, TILE - 1:TILE], 0.0).then_inc(tail_set, 1)
                dve.wait_ge(tail_set, 3)

                def weigh(k, i):
                    n = i * K + k
                    dve.wait_ge(alpha_made, n + 1)
                    past(dve, partT_done, n - 1)
                    for pair in range(2):
                        for h in range(H):
                            if h:
                                dve.wait_ge(part_step, (H - 1) * (2 * n + pair) + h)
                            for s in (2 * pair, 2 * pair + 1):
                                if h == 0:
                                    dve.wait_ge(y_done, SUB * n + s + 1)
                                a = alpha[slot(k)][:, s * H + h:s * H + h + 1]
                                yh, out = y[s][:, h * D:(h + 1) * D], part[slot(k)][:, s, :]
                                if h == 0:
                                    last = dve.tensor_scalar(out, yh, a, None, ALU.mult)
                                else:
                                    last = dve.scalar_tensor_tensor(out=out, in0=yh, scalar=a, in1=out, op0=ALU.mult, op1=ALU.add)
                            last.then_inc(part_made if h == H - 1 else part_step, 1)

                def scan(k, i):
                    n = i * K + k
                    dve.wait_ge(partT_done, n + 1)
                    past(dve, scanned, n)
                    past(dve, back_done, n - 1)
                    before = sumT[slot(k - 1 if k else K - 1)]
                    dve.tensor_tensor_scan(sumT[slot(k)][:, :], keep[k][:, :], partT[:, :], before[:, TILE - 1:TILE],
                                           ALU.mult, ALU.add).then_inc(scanned, 1)

                pipeline(dve, nb, K, [(3, scan), (1, weigh)])


def conv_nodes(nc, g, layer, final):
    nb = g.NTN // NB
    bias_in, gamma_in, beta_in = g.conv_norms[layer]
    flat = lambda t: t[:, :, :].rearrange("p a d -> p (a d)")
    with Phase(nc, f"conv_nodes{layer}_") as m:
        ident, eps = m.sb("ident", [P, P]), m.sb("eps", [P, 1])
        gamma, beta, bias = m.sb("gamma", [P, TILE]), None if final else m.sb("beta", [P, TILE]), m.sb("bias", [P, TILE])
        h, agg = m.sbs("h", [P, SUB, D]), m.sbs("agg", [P, SUB, D])
        x = m.sbs("x", [P, SUB, D]) if final else None
        hT = m.sbs("hT", [P, TILE], n=2)
        base, o, scaled, res = (m.sbs(n, [P, SUB, D]) for n in ("base", "o", "scaled", "res"))
        h_out = m.sbs("h_out", [P, SUB, D]) if final else res
        turned = [m.ps(f"turned{j}", [P, TILE]) for j in range(2)]
        o_ps = [m.ps(f"o_ps{j}", [P, SUB, D]) for j in range(2)]
        norm = Norm(m, "norm")
        last_norm = Norm(m, "last_norm") if final else None
        tile_in, out = m.sems("tile_in"), m.sems("out")
        cleared, ident_made, set_once, weights_in = (m.sem(n) for n in ("cleared", "ident_made", "set_once", "weights_in"))
        turned_done, hT_made, o_done, o_made, base_made, agg_made = (
            m.sem(n) for n in ("turned_done", "hT_made", "o_done", "o_made", "base_made", "agg_made"))
        normed, scaled_made, sum_made, all_made = (m.sem(n) for n in ("normed", "scaled_made", "sum_made", "all_made"))
        own = m.sem("own")
        n_in, n_out = (48, 32) if final else (32, 16)
        n_weights = 2 * SUB if final else 3 * SUB
        with nc.Block() as block:
            @block.sync
            def _(sp):
                for a in range(SUB):
                    broadcast_rows(sp, gamma[:, a * D:(a + 1) * D], gamma_in, weights_in)
                    if not final:
                        broadcast_rows(sp, beta[:, a * D:(a + 1) * D], beta_in, weights_in)
                    broadcast_rows(sp, bias[:, a * D:(a + 1) * D], bias_in, weights_in)

                def load(k, i):
                    r, n = k % RING, i * NB + k
                    sp.dma_start(h[r][:, :, :], node_rows(g.H, n)).then_inc(tile_in[r], 16)
                    sp.dma_start(agg[r][:, :, :], node_rows(g.AGG, n)).then_inc(tile_in[r], 16)
                    if final:
                        sp.dma_start(x[r][:, :, :], node_rows(g.X, n)).then_inc(tile_in[r], 16)

                def freed(k, i):
                    sp.wait_ge(base_made, i * NB + k + 1)
                    sp.wait_ge(o_made, i * NB + k + 1)

                def store(k, i):
                    r, n = k % RING, i * NB + k
                    sp.wait_ge(all_made, n + 1)
                    sp.dma_start(node_rows(g.H, n), h_out[r][:, :, :]).then_inc(out[r], 16)
                    if final:
                        sp.dma_start(node_rows(g.X, n), res[r][:, :, :]).then_inc(out[r], 16)

                node_stream(sp, nb, load, freed, store, 10 if final else 6)
                for r in range(RING):
                    sp.wait_ge(out[r], n_out * turns(r, nb))

            @block.gpsimd
            def _(pool):
                make_identity(pool, ident, ident_made, cleared)
                pool.wait_ge(weights_in, 16 * n_weights)

                def make_base(k, i):
                    r, n = k % RING, i * NB + k
                    past(pool, sum_made, n + 1 - RING)
                    wait_alone(pool, tile_in[r], n_in * (turns(k, i) + 1), own)
                    pool.tensor_tensor(flat(agg[r]), flat(agg[r]), bias[:, :], ALU.add).then_inc(agg_made, 1)
                    pool.tensor_tensor(flat(base[r]), flat(h[r]), flat(x[r]) if final else beta[:, :], ALU.add).then_inc(base_made, 1)

                def scale(k, i):
                    r, n = k % RING, i * NB + k
                    pool.wait_ge(normed, n + 1)
                    pool.tensor_tensor(flat(o[r]), flat(scaled[r]), gamma[:, :], ALU.mult).then_inc(scaled_made, 1)

                pipeline(pool, nb, NB, [(0, make_base)] + ([(5, scale)] if final else []))

            @block.tensor
            def _(pe):
                pe.wait_ge(ident_made, 1)

                def turn(k, i):
                    r, n = k % RING, i * NB + k
                    pe.wait_ge(tile_in[r], n_in * (turns(k, i) + 1))
                    past(pe, hT_made, n - 1)
                    for a in range(SUB):
                        last = pe.transpose(turned[k % 2][:, a * P:(a + 1) * P], h[r][:, a, :], ident[:, :])
                    last.then_inc(turned_done, 1)

                def project(k, i):
                    n = i * NB + k
                    past(pe, o_made, n - 1)
                    pe.wait_ge(hT_made, n + 1)
                    for a in range(SUB):
                        last = pe.matmul(o_ps[k % 2][:, a, :], hT[k % 2][:, a * P:(a + 1) * P], g.wmean[:, :],
                                         start=True, stop=True)
                    last.then_inc(o_done, 1)

                pipeline(pe, nb, NB, [(0, turn), (1, project)])

            @block.vector
            def _(dve):
                dve.memset(eps[:, :], EPS).then_inc(set_once, 1)
                dve.wait_ge(weights_in, 16 * n_weights)

                def start(k, i):
                    r, n = k % RING, i * NB + k
                    dve.wait_ge(o_done, n + 1)
                    dve.wait_ge(agg_made, n + 1)
                    past(dve, normed, n + 1 - RING)
                    dve.tensor_tensor(o[r][:, :, :], o_ps[k % 2][:, :, :], agg[r][:, :, :], ALU.add).then_inc(o_made, 1)

                def take_stats(k, i):
                    dve.wait_ge(o_made, i * NB + k + 1)
                    norm.take_stats(dve, o[k % RING], k % RING)

                def scale(k, i):
                    r, n = k % RING, i * NB + k
                    dve.wait_ge(normed, n + 1)
                    dve.tensor_tensor(flat(o[r]), flat(scaled[r]), gamma[:, :], ALU.mult).then_inc(scaled_made, 1)

                def finish(k, i):
                    r, n = k % RING, i * NB + k
                    dve.wait_ge(base_made, n + 1)
                    dve.wait_ge(scaled_made, n + 1)
                    if final:
                        past(dve, out[r], n_out * turns(k, i))
                    dve.tensor_tensor(flat(res[r]) if final else flat(scaled[r]), flat(o[r]), flat(base[r]), ALU.add).then_inc(sum_made, 1)

                def last_stats(k, i):
                    dve.wait_ge(sum_made, i * NB + k + 1)
                    last_norm.take_stats(dve, res[k % RING], k % RING)

                steps = [
                    (0, start),
                    (3, lambda k, i: norm.invert(dve, k % RING, i * NB + k + 1)),
                    (1, lambda k, i: norm.moments(dve, k % RING, i * NB + k + 1)),
                    (3, lambda k, i: norm.shifts(dve, k % RING, i * NB + k + 1)),
                    (0, take_stats)]
                if final:
                    steps += [
                        (6, finish),
                        (9, lambda k, i: last_norm.invert(dve, k % RING, i * NB + k + 1)),
                        (7, lambda k, i: last_norm.moments(dve, k % RING, i * NB + k + 1)),
                        (9, lambda k, i: last_norm.shifts(dve, k % RING, i * NB + k + 1)),
                        (6, last_stats)]
                else:
                    steps = steps[:3] + [(5, scale)] + steps[3:] + [(5, finish)]
                pipeline(dve, nb, NB, steps)

            @block.scalar
            def _(act):
                act.wait_ge(set_once, 1)

                def copy_turned(k, i):
                    n = i * NB + k
                    act.wait_ge(turned_done, n + 1)
                    past(act, o_done, n - 1)
                    act.activation(hT[k % 2][:, :], turned[k % 2][:, :], ACT.Copy).then_inc(hT_made, 1)

                def normalize(k, i):
                    r, n = k % RING, i * NB + k
                    act.wait_ge(norm.shift_done, n + 1)
                    past(act, sum_made, n + 1 - RING)
                    norm.apply(act, scaled[r], o[r], r, ACT.Identity).then_inc(normed, 1)

                def relu(k, i):
                    r, n = k % RING, i * NB + k
                    act.wait_ge(sum_made, n + 1)
                    past(act, out[r], n_out * turns(k, i))
                    act.activation(res[r][:, :, :], scaled[r][:, :, :], ACT.Relu).then_inc(all_made, 1)

                def last_normalize(k, i):
                    r, n = k % RING, i * NB + k
                    act.wait_ge(last_norm.shift_done, n + 1)
                    past(act, out[r], n_out * turns(k, i))
                    last_norm.apply(act, h_out[r], res[r], r, ACT.Relu).then_inc(all_made, 1)

                steps = [
                    (0, copy_turned),
                    (3, lambda k, i: norm.root(act, k % RING, i * NB + k + 1, eps)),
                    (5, normalize)]
                if final:
                    steps += [
                        (9, lambda k, i: last_norm.root(act, k % RING, i * NB + k + 1, eps)),
                        (11, last_normalize)]
                else:
                    steps += [(7, relu)]
                pipeline(act, nb, NB, steps)




def gat_logits(nc, g):
    nb = g.NTE // K
    with Phase(nc, "gat_logits_") as m:
        ident = m.sb("ident", [P, P])
        a_rows, product, wa = m.sb("a_rows", [P, 2, HID]), m.sb("product", [D, 2, HID]), m.sb("wa", [D, 2, H])
        idx = m.sbs("idx", [P, 16], I32)
        hs, hd, hdT = m.sbs("hs", [P, SUB, D]), m.sbs("hd", [P, SUB, D]), m.sbs("hdT", [P, TILE], n=2)
        sloped, logit = m.sbs("sloped", [H, TILE], n=2), m.sbs("logit", [H, TILE], n=2)
        hsT_ps, hdT_ps = ([m.ps(f"{n}{j}", [P, TILE]) for j in range(2)] for n in ("hsT_ps", "hdT_ps"))
        e_ps = [m.ps(f"e_ps{j}", [H, TILE]) for j in range(2)]
        idx_in, rows_in, logit_out, own = m.sems("idx_in"), g.gathered, m.sems("logit_out", 2), m.sem("own")
        rows0 = g.start(rows_in, nb * 128)
        cleared, ident_made, weights_in, product_made, weights_made = (
            m.sem(n) for n in ("cleared", "ident_made", "weights_in", "product_made", "weights_made"))
        turned_done, hdT_made, hsT_made, e_done, sloped_made, logit_made = (
            m.sem(n) for n in ("turned_done", "hdT_made", "hsT_made", "e_done", "sloped_made", "logit_made"))
        with nc.Block() as block:
            @block.sync
            def _(sp):
                sp.dma_start(g.wn[:, :], g.wnT).then_inc(weights_in, 16)
                broadcast_rows(sp, a_rows[:, 0, :], g.a_src, weights_in)
                broadcast_rows(sp, a_rows[:, 1, :], g.a_dst, weights_in)

                def load(k, i):
                    sp.dma_start(idx[k][:, :], g.IDX[bass.ds(i * K + k, 1), :, :].rearrange("t p s -> (t p) s")).then_inc(idx_in[k], 16)

                def body(i, more):
                    for k in range(K):
                        sp.wait_ge(logit_made, i * K + k + 1)
                        sp.dma_start(g.LOGIT[1][:, bass.ds((i * K + k) * TILE, TILE)], logit[k % 2][:, :]).then_inc(logit_out[k % 2], 16)
                        if more:
                            load(k, i + 1)

                for k in range(K):
                    load(k, 0)
                if nb > 1:
                    with sp.Fori(0, nb - 1) as i:
                        body(i, True)
                body(nb - 1, False)
                for slot in range(2):
                    sp.wait_ge(logit_out[slot], 16 * nb * slot_tiles(slot))

            @block.gpsimd
            def _(pool):
                make_identity(pool, ident, ident_made, cleared)

                def gather_tile(k, i):
                    wait_alone(pool, idx_in[k], (i + 1) * 16, own)
                    for s in range(SUB):
                        gather(pool, hd[k][:, s, :], g.H[:, :], idx[k][:, 4 + s:5 + s]).then_inc(rows_in[k], 16)
                        gather(pool, hs[k][:, s, :], g.H[:, :], idx[k][:, s:s + 1]).then_inc(rows_in[k], 16)

                for k in range(K):
                    gather_tile(k, 0)
                if nb > 1:
                    with pool.Fori(1, nb) as i:
                        for k in range(K):
                            pool.wait_ge(turned_done, (i - 1) * K + k + 1)
                            gather_tile(k, i)

            @block.tensor
            def _(pe):
                pe.wait_ge(ident_made, 1)
                pe.wait_ge(weights_made, 1)

                def body(i):
                    n = i * K
                    for k in range(K + 1):
                        if k < K:
                            pe.wait_ge(rows_in[k], i * 128 + (128 + rows0))
                            pe.wait_ge(hdT_made, n + max(k - 1, 0))
                            pe.wait_ge(hsT_made, n + max(k - 1, 0))
                            for s in range(SUB):
                                pe.transpose(hdT_ps[k % 2][:, s * P:(s + 1) * P], hd[k][:, s, :], ident[:, :])
                            for s in range(SUB):
                                last = pe.transpose(hsT_ps[k % 2][:, s * P:(s + 1) * P], hs[k][:, s, :], ident[:, :])
                            last.then_inc(turned_done, 1)
                        if k:
                            j = k - 1
                            pe.wait_ge(hdT_made, n + j + 1)
                            pe.wait_ge(logit_made, n + max(j - 1, 0))
                            pe.matmul(e_ps[j % 2][:, :], wa[:, 1, :], hdT[j % 2][:, :], start=True, stop=False)
                            pe.wait_ge(hsT_made, n + j + 1)
                            pe.matmul(e_ps[j % 2][:, :], wa[:, 0, :], g.srcT[:, bass.ds((n + j) * TILE, TILE)],
                                      start=False, stop=True).then_inc(e_done, 1)

                run_bodies(pe, nb, body)

            @block.scalar
            def _(act):
                def body(i):
                    n = i * K
                    for k in range(K + 1):
                        if k < K:
                            act.wait_ge(turned_done, n + k + 1)
                            act.wait_ge(e_done, n + max(k - 1, 0))
                            act.activation(hdT[k % 2][:, :], hdT_ps[k % 2][:, :], ACT.Copy).then_inc(hdT_made, 1)
                        if k:
                            j = k - 1
                            act.wait_ge(e_done, n + j + 1)
                            act.wait_ge(logit_made, n + max(j - 1, 0))
                            act.activation(sloped[j % 2][:, :], e_ps[j % 2][:, :], ACT.Copy, scale=SLOPE).then_inc(sloped_made, 1)

                run_bodies(act, nb, body)

            @block.vector
            def _(dve):
                dve.wait_ge(weights_in, 48)
                for j in range(2):
                    dve.tensor_tensor(product[:, j, :], g.wn[:, :], a_rows[:, j, :], ALU.mult).then_inc(product_made, 1)
                dve.wait_ge(product_made, 2)
                dve.tensor_reduce(out=wa[:, :, :].rearrange("p j h -> p (j h)"),
                                  in_=product[:, :, :].rearrange("p j (h d) -> p (j h) d", h=H), axis=AX.X, op=ALU.add).then_inc(weights_made, 1)

                def body(i):
                    n = i * K
                    for k in range(K + 1):
                        if k < K:
                            dve.wait_ge(turned_done, n + k + 1)
                            dve.tensor_copy(g.srcT[:, bass.ds((n + k) * TILE, TILE)], hsT_ps[k % 2][:, :]).then_inc(hsT_made, 1)
                        if k:
                            j = k - 1
                            dve.wait_ge(sloped_made, n + j + 1)
                            dve.wait_ge(logit_out[j % 2], i * (16 * slot_tiles(j % 2)) + 16 * (j // 2))
                            dve.tensor_tensor(logit[j % 2][:, :], e_ps[j % 2][:, :], sloped[j % 2][:, :], ALU.max).then_inc(logit_made, 1)

                run_bodies(dve, nb, body)


def gat_aggregate(nc, g):
    nb = g.NTE // K
    with Phase(nc, "gat_aggregate_") as m:
        ident = m.sb("ident", [P, P])
        w1, w2, b1 = m.sb("w1", [P, 2, HID]), m.sb("w2", [P, 2, D]), m.sb("b1", [P, 2])
        above, below = m.sb("above", [P, 2]), m.sb("below", [P, 2])
        idx, alphaT, keep = m.sbs("idx", [P, 16], I32), m.sbs("alphaT", [H, TILE]), m.sbs("keep", [P, TILE])
        alpha, src = m.sbs("alpha", [P, SUB * H], n=3), m.sbs("src", [P, TILE], n=3)
        part, sumT = m.sbs("part", [P, SUB, HID], n=3), m.sbs("sumT", [P, 2, TILE], n=3)
        headsT, hidT, rows = m.sbs("headsT", [P, 2, TILE], n=3), m.sb("hidT", [P, 2, TILE]), m.sbs("rows", [P, TILE], n=3)
        y = [m.ps(f"y{j}", [P, 2, HID]) for j in range(2)]
        partT, hid = ([m.ps(f"{n}{j}", [P, TILE]) for j in range(2)] for n in ("partT", "hid"))
        o, alpha_ps = m.ps("o", [P, TILE]), m.ps("alpha_ps", [P, SUB * H])
        tile_in, weights_in = m.sems("tile_in"), m.sem("weights_in")
        agg_out, own = g.scattered, m.sem("own")
        agg0 = g.start(agg_out, nb * 64)
        cleared, ident_made, tail_set, bias_ready = (m.sem(n) for n in ("cleared", "ident_made", "tail_set", "bias_ready"))
        alpha_turned, alpha_made, src_copied, y_done, part_made = (
            m.sem(n) for n in ("alpha_turned", "alpha_made", "src_copied", "y_done", "part_made"))
        partT_done, scanned, headsT_made, hid_done, hidT_made, o_done, rows_made = (
            m.sem(n) for n in ("partT_done", "scanned", "headsT_made", "hid_done", "hidT_made", "o_done", "rows_made"))
        with nc.Block() as block:
            @block.sync
            def _(sp):
                sp.dma_start(w1[:, :, :], g.mw1.rearrange("(j p) n -> p j n", p=P)).then_inc(weights_in, 16)
                sp.dma_start(w2[:, :, :], g.mw2.rearrange("(j p) n -> p j n", p=P)).then_inc(weights_in, 16)
                with nc.allow_non_contiguous_dma("256 biases"):
                    sp.dma_start(b1[:, :], g.mb1.rearrange("o (j p) -> p (o j)", p=P)).then_inc(weights_in, 16)

                def load(k, i):
                    n = i * K + k
                    sp.dma_start(idx[k][:, :], g.IDX[bass.ds(n, 1), :, :].rearrange("t p s -> (t p) s")).then_inc(tile_in[k], 16)
                    sp.dma_start(alphaT[k][:, :], g.ALPHA[:, bass.ds(n * TILE, TILE)]).then_inc(tile_in[k], 16)
                    sp.dma_start(keep[k][:, :], edge_span(g.KEEP, n, P)).then_inc(tile_in[k], 16)

                for k in range(K):
                    load(k, 0)
                if nb > 1:
                    with sp.Fori(1, nb) as i:
                        for k in range(K):
                            sp.wait_ge(agg_out[k], i * 64 + agg0)
                            load(k, i)

            @block.gpsimd
            def _(pool):
                make_identity(pool, ident, ident_made, cleared)

                def body(i):
                    for k in range(K):
                        wait_alone(pool, rows_made, i * K + k + 1, own)
                        for s in range(SUB):
                            scatter_last(pool, g.AGG[:, :], idx[k][:, 8 + s:9 + s], rows[slot(k)][:, s * P:(s + 1) * P],
                                         g.NP - 1).then_inc(agg_out[k], 16)

                run_bodies(pool, nb, body)
                for k in range(K):
                    pool.wait_ge(agg_out[k], nb * 64 + agg0)

            @block.tensor
            def _(pe):
                pe.wait_ge(ident_made, 1)
                pe.wait_ge(weights_in, 48)

                def turn_alpha(k, i):
                    n = i * K + k
                    pe.wait_ge(tile_in[k], (i + 1) * 48)
                    past(pe, alpha_made, n)
                    for s in range(SUB):
                        last = pe.matmul(alpha_ps[:, s * H:(s + 1) * H], alphaT[k][:, s * P:(s + 1) * P], ident[0:H, 0:H],
                                         start=True, stop=True)
                    last.then_inc(alpha_turned, 1)

                def project(k, i):
                    n = i * K + k
                    pe.wait_ge(src_copied, n + 1)
                    past(pe, part_made, 2 * n)
                    for s in range(SUB):
                        pe.matmul(y[s // 2][:, s % 2, :], src[slot(k)][:, s * P:(s + 1) * P], g.wn[:, :],
                                  start=True, stop=True).then_inc(y_done, 1)

                def turn(k, i):
                    n = i * K + k
                    pe.wait_ge(part_made, 2 * n + 2)
                    past(pe, scanned, 2 * n)
                    for j in range(2):
                        for s in range(SUB):
                            last = pe.transpose(partT[j][:, s * P:(s + 1) * P], part[slot(k)][:, s, j * P:(j + 1) * P], ident[:, :])
                    last.then_inc(partT_done, 1)

                def first(k, i):
                    n = i * K + k
                    pe.wait_ge(headsT_made, n + 1)
                    for j in range(2):
                        past(pe, hidT_made, 2 * n + j - 1)
                        for c in range(2):
                            last = pe.matmul(hid[j][:, :], w1[:, c, j * P:(j + 1) * P], headsT[slot(k)][:, c, :],
                                             start=(c == 0), stop=(c == 1))
                        last.then_inc(hid_done, 1)

                def second(k, i):
                    n = i * K + k
                    past(pe, rows_made, n)
                    pe.wait_ge(hidT_made, 2 * n + 2)
                    for s in range(SUB):
                        for c in range(2):
                            last = pe.matmul(o[:, s * D:(s + 1) * D], hidT[:, c, s * P:(s + 1) * P], w2[:, c, :],
                                             start=(c == 0), stop=(c == 1))
                    last.then_inc(o_done, 1)

                pipeline(pe, nb, K, [(0, turn_alpha), (1, project), (2, turn), (3, first), (4, second)])

            @block.scalar
            def _(act):
                def copy_alpha(k, i):
                    n = i * K + k
                    act.wait_ge(alpha_turned, n + 1)
                    past(act, part_made, 2 * (n - 1))
                    act.activation(alpha[slot(k)][:, :], alpha_ps[:, :], ACT.Copy).then_inc(alpha_made, 1)

                def copy_src(k, i):
                    n = i * K + k
                    past(act, y_done, SUB * (n - 1))
                    act.activation(src[slot(k)][:, :], g.srcT[:, bass.ds(n * TILE, TILE)], ACT.Copy).then_inc(src_copied, 1)

                def copy_rows(k, i):
                    act.wait_ge(o_done, i * K + k + 1)
                    rows_freed(act, agg_out, agg0, k, i)
                    act.activation(rows[slot(k)][:, :], o[:, :], ACT.Copy).then_inc(rows_made, 1)

                def relu_heads(k, i):
                    n = i * K + k
                    act.wait_ge(scanned, 2 * n + 2)
                    past(act, hid_done, 2 * (n - 1))
                    act.activation(headsT[slot(k)][:, :, :], sumT[slot(k)][:, :, :], ACT.Relu).then_inc(headsT_made, 1)

                pipeline(act, nb, K, [(0, copy_alpha), (0, copy_src), (5, copy_rows), (2, relu_heads)])

            @block.vector
            def _(dve):
                dve.wait_ge(weights_in, 48)
                dve.tensor_scalar(above[:, :], b1[:, :], 0.0, None, ALU.min).then_inc(bias_ready, 1)
                dve.tensor_scalar(below[:, :], b1[:, :], 0.0, -1.0, ALU.max, ALU.mult).then_inc(bias_ready, 1)
                for j in range(3):
                    dve.memset(sumT[j][:, :, TILE - 1:TILE], 0.0).then_inc(tail_set, 1)
                dve.wait_ge(tail_set, 3)
                dve.wait_ge(bias_ready, 2)

                def hidden(k, i):
                    n = i * K + k
                    for j in range(2):
                        dve.wait_ge(hid_done, 2 * n + j + 1)
                        if j == 0:
                            past(dve, o_done, n)
                        dve.tensor_scalar(hidT[:, j, :], hid[j][:, :], above[:, j:j + 1], below[:, j:j + 1],
                                          ALU.add, ALU.max).then_inc(hidT_made, 1)

                def weigh(k, i):
                    n = i * K + k
                    dve.wait_ge(alpha_made, n + 1)
                    past(dve, partT_done, n - 1)
                    for j in range(2):
                        dve.wait_ge(y_done, SUB * n + 2 * (j + 1))
                        weights = alpha[slot(k)][:, 2 * H * j:2 * H * (j + 1)].unsqueeze(2).to_broadcast([P, 2 * H, HD])
                        dve.tensor_tensor(part[slot(k)][:, 2 * j:2 * j + 2, :].rearrange("p s (h d) -> p (s h) d", h=H),
                                          y[j][:, :, :].rearrange("p s (h d) -> p (s h) d", h=H), weights, ALU.mult).then_inc(part_made, 1)

                def scan(k, i):
                    n = i * K + k
                    dve.wait_ge(partT_done, n + 1)
                    past(dve, scanned, 2 * n)
                    past(dve, headsT_made, n - 1)
                    before = sumT[slot(k - 1 if k else K - 1)]
                    for j in range(2):
                        dve.tensor_tensor_scan(sumT[slot(k)][:, j, :], keep[k][:, :], partT[j][:, :],
                                               before[:, j, TILE - 1:TILE], ALU.mult, ALU.add).then_inc(scanned, 1)

                pipeline(dve, nb, K, [(4, hidden), (1, weigh), (2, scan)])


def gat_nodes(nc, g):
    nb = g.NTN // NB
    flat = lambda t: t[:, :, :].rearrange("p a d -> p (a d)")
    with Phase(nc, "gat_nodes_") as m:
        eps, ones = m.sb("eps", [P, 1]), m.sb("ones", [P, P])
        b1, relu_b1, w2 = m.sb("b1", [P, 2]), m.sb("relu_b1", [P, 2, P]), m.sb("w2", [P, 2, D])
        b2, c = m.sb("b2", [P, D]), m.sb("c", [P, TILE])
        x, agg, base, x3, h4, total = (m.sbs(n, [P, SUB, D]) for n in ("x", "agg", "base", "x3", "h4", "total"))
        c_ps = m.ps("c_ps", [P, D])
        norm = Norm(m, "norm")
        tile_in, out, own = m.sems("tile_in"), m.sems("out"), m.sem("own")
        weights_in, ones_set, relu_made, c_done, c_made, eps_set = (
            m.sem(n) for n in ("weights_in", "ones_set", "relu_made", "c_done", "c_made", "eps_set"))
        base_made, x3_made, h4_made, total_made = (m.sem(n) for n in ("base_made", "x3_made", "h4_made", "total_made"))
        with nc.Block() as block:
            @block.sync
            def _(sp):
                sp.dma_start(w2[:, :, :], g.mw2.rearrange("(j p) n -> p j n", p=P)).then_inc(weights_in, 16)
                with nc.allow_non_contiguous_dma("256 biases"):
                    sp.dma_start(b1[:, :], g.mb1.rearrange("o (j p) -> p (o j)", p=P)).then_inc(weights_in, 16)
                broadcast_rows(sp, b2[:, :], g.mb2, weights_in)

                def load(k, i):
                    r, n = k % RING, i * NB + k
                    sp.dma_start(x[r][:, :, :], node_rows(g.X, n)).then_inc(tile_in[r], 16)
                    sp.dma_start(agg[r][:, :, :], node_rows(g.AGG, n)).then_inc(tile_in[r], 16)

                def freed(k, i):
                    sp.wait_ge(x3_made, i * NB + k + 1)

                def store(k, i):
                    r, n = k % RING, i * NB + k
                    sp.wait_ge(total_made, n + 1)
                    sp.dma_start(node_rows(g.H, n), h4[r][:, :, :]).then_inc(out[r], 16)
                    sp.dma_start(node_rows(g.out, n), total[r][:, :, :]).then_inc(out[r], 16)

                node_stream(sp, nb, load, freed, store, 5)
                for r in range(RING):
                    sp.wait_ge(out[r], 32 * turns(r, nb))

            @block.tensor
            def _(pe):
                pe.wait_ge(relu_made, 2)
                for j in range(2):
                    last = pe.matmul(c_ps[:, :], relu_b1[:, j, :], w2[:, j, :], start=(j == 0), stop=(j == 1))
                last.then_inc(c_done, 1)

            @block.gpsimd
            def _(pool):
                pool.wait_ge(c_made, SUB)

                def make_base(k, i):
                    r, n = k % RING, i * NB + k
                    past(pool, x3_made, n + 1 - RING)
                    wait_alone(pool, tile_in[r], 32 * (turns(k, i) + 1), own)
                    pool.tensor_tensor(flat(base[r]), flat(x[r]), c[:, :], ALU.add).then_inc(base_made, 1)

                pipeline(pool, nb, NB, [(0, make_base)])

            @block.vector
            def _(dve):
                dve.memset(eps[:, :], EPS).then_inc(eps_set, 1)
                dve.memset(ones[:, :], 1.0).then_inc(ones_set, 1)
                dve.wait_ge(ones_set, 1)
                dve.wait_ge(weights_in, 48)
                for j in range(2):
                    dve.tensor_scalar(relu_b1[:, j, :], ones[:, :], b1[:, j:j + 1], 0.0, ALU.mult, ALU.max).then_inc(relu_made, 1)
                dve.wait_ge(c_done, 1)
                for a in range(SUB):
                    dve.tensor_tensor(c[:, a * D:(a + 1) * D], c_ps[:, :], b2[:, :], ALU.add).then_inc(c_made, 1)

                def add(k, i):
                    r, n = k % RING, i * NB + k
                    dve.wait_ge(base_made, n + 1)
                    dve.tensor_tensor(flat(x3[r]), flat(base[r]), flat(agg[r]), ALU.add).then_inc(x3_made, 1)

                def take_stats(k, i):
                    dve.wait_ge(x3_made, i * NB + k + 1)
                    norm.take_stats(dve, x3[k % RING], k % RING)

                def add_h4(k, i):
                    r, n = k % RING, i * NB + k
                    dve.wait_ge(h4_made, n + 1)
                    past(dve, out[r], 32 * turns(k, i))
                    dve.tensor_tensor(flat(total[r]), flat(x3[r]), flat(h4[r]), ALU.add).then_inc(total_made, 1)

                pipeline(dve, nb, NB, [
                    (0, add),
                    (1, lambda k, i: norm.moments(dve, k % RING, i * NB + k + 1)),
                    (0, take_stats),
                    (3, lambda k, i: norm.scales(dve, k % RING, i * NB + k + 1)),
                    (5, add_h4)])

            @block.scalar
            def _(act):
                act.wait_ge(eps_set, 1)

                def normalize(k, i):
                    r = k % RING
                    act.wait_ge(norm.shift_done, i * NB + k + 1)
                    past(act, out[r], 32 * turns(k, i))
                    norm.apply(act, h4[r], x3[r], r, ACT.Relu).then_inc(h4_made, 1)

                pipeline(act, nb, NB, [
                    (0, lambda k, i: norm.root(act, k % RING, i * NB + k + 1, eps)),
                    (2, normalize)])


def mean_edges(nc, g):
    nb = g.NTE // K
    with Phase(nc, "mean_edges_") as m:
        ident = m.sb("ident", [P, P])
        idx = m.sbs("idx", [P, 16], I32)
        hs, keep, sumT, rows = m.sbs("hs", [P, SUB, D]), m.sbs("keep", [P, TILE]), m.sbs("sumT", [P, TILE]), m.sbs("rows", [P, SUB, D])
        two, counts, half = m.sb("two", [1, TILE]), m.sbs("counts", [1, TILE], n=2), m.sbs("half", [P, SUB], n=2)
        turned, back, counts_ps = ([m.ps(f"{n}{j}", [P, TILE]) for j in range(2)] for n in ("turned", "back", "counts_ps"))
        idx_in, keep_in, hs_in, added = m.sems("idx_in"), m.sems("keep_in"), g.gathered, g.scattered
        hs0, added0 = g.start(hs_in, nb * 64), g.start(added, nb * 64)
        cleared, ident_made, set_once, own = (m.sem(n) for n in ("cleared", "ident_made", "set_once", "own"))
        turned_done, scanned, counted, half_made, back_done, rows_made = (
            m.sem(n) for n in ("turned_done", "scanned", "counted", "half_made", "back_done", "rows_made"))
        with nc.Block() as block:
            @block.sync
            def _(sp):
                def load(k, i):
                    sp.dma_start(idx[k][:, :], g.IDX[bass.ds(i * K + k, 1), :, :].rearrange("t p s -> (t p) s")).then_inc(idx_in[k], 16)
                    sp.dma_start(keep[k][:, :], edge_span(g.KEEP, i * K + k, P)).then_inc(keep_in[k], 16)

                for k in range(K):
                    load(k, 0)
                if nb > 1:
                    with sp.Fori(1, nb) as i:
                        for k in range(K):
                            sp.wait_ge(added[k], i * 64 + added0)
                            load(k, i)

            @block.gpsimd
            def _(pool):
                make_identity(pool, ident, ident_made, cleared)

                def gather_tile(k, i):
                    wait_alone(pool, idx_in[k], (i + 1) * 16, own)
                    for s in range(SUB):
                        gather(pool, hs[k][:, s, :], g.H[:, :], idx[k][:, s:s + 1]).then_inc(hs_in[k], 16)

                def body(i, more):
                    for k in range(K):
                        wait_alone(pool, rows_made, i * K + k + 1, own)
                        for s in range(SUB):
                            pool.indirect_dma_start(out=g.out[:, :], out_offset=bass.IndirectOffsetOnAxis(ap=idx[k][:, 12 + s:13 + s], axis=0),
                                                    in_=rows[k][:, s, :], in_offset=None, compute_op=ALU.add).then_inc(added[k], 16)
                        if more and k >= BEHIND:
                            gather_tile(k - BEHIND, i + 1)
                    if more:
                        for k in range(K - BEHIND, K):
                            gather_tile(k, i + 1)

                for k in range(K):
                    gather_tile(k, 0)
                if nb > 1:
                    with pool.Fori(0, nb - 1) as i:
                        body(i, True)
                body(nb - 1, False)
                for k in range(K):
                    pool.wait_ge(added[k], nb * 64 + added0)

            @block.tensor
            def _(pe):
                pe.wait_ge(ident_made, 1)

                def body(i):
                    n = i * K
                    for k in range(K + 1):
                        if k < K:
                            pe.wait_ge(hs_in[k], i * 64 + (64 + hs0))
                            pe.wait_ge(scanned, 2 * n + 2 * max(k - 1, 0))
                            for s in range(SUB):
                                last = pe.transpose(turned[k % 2][:, s * P:(s + 1) * P], hs[k][:, s, :], ident[:, :])
                            last.then_inc(turned_done, 1)
                        if k:
                            j = k - 1
                            pe.wait_ge(scanned, 2 * n + 2 * (j + 1))
                            pe.wait_ge(half_made, n + max(j - 1, 0))
                            for s in range(SUB):
                                last = pe.matmul(counts_ps[j % 2][:, s:s + 1], counts[j % 2][:, s * P:(s + 1) * P], ident[0:1, 0:1],
                                                 start=True, stop=True)
                            last.then_inc(counted, 1)
                            pe.wait_ge(rows_made, n + max(j - 1, 0))
                            for s in range(SUB):
                                last = pe.transpose(back[j % 2][:, s * P:(s + 1) * P], sumT[j][:, s * P:(s + 1) * P], ident[:, :])
                            last.then_inc(back_done, 1)

                run_bodies(pe, nb, body)

            @block.vector
            def _(dve):
                dve.memset(sumT[K - 1][:, TILE - 1:TILE], 0.0).then_inc(set_once, 1)
                for j in range(2):
                    dve.memset(counts[j][:, TILE - 1:TILE], 0.0).then_inc(set_once, 1)
                dve.memset(two[:, :], 2.0).then_inc(set_once, 1)
                dve.wait_ge(set_once, 4)

                def body(i):
                    n = i * K
                    for k in range(K + 1):
                        if k < K:
                            dve.wait_ge(keep_in[k], (i + 1) * 16)
                            dve.wait_ge(turned_done, n + k + 1)
                            dve.wait_ge(scanned, 2 * n + 2 * k)
                            dve.wait_ge(back_done, n)
                            dve.tensor_tensor_scan(sumT[k][:, :], keep[k][:, :], turned[k % 2][:, :],
                                                   sumT[k - 1][:, TILE - 1:TILE], ALU.mult, ALU.add).then_inc(scanned, 1)
                            dve.wait_ge(counted, n + max(k - 1, 0))
                            before = counts[(k - 1) % 2 if k else (K - 1) % 2]
                            dve.tensor_tensor_scan(counts[k % 2][:, :], keep[k][0:1, :], two[:, :],
                                                   before[:, TILE - 1:TILE], ALU.mult, ALU.add).then_inc(scanned, 1)
                        if k:
                            dve.wait_ge(counted, n + k)
                            dve.wait_ge(rows_made, n + max(k - 2, 0))
                            dve.reciprocal(half[(k - 1) % 2][:, :], counts_ps[(k - 1) % 2][:, 0:SUB]).then_inc(half_made, 1)

                run_bodies(dve, nb, body)

            @block.scalar
            def _(act):
                def body(i):
                    n = i * K
                    for k in range(K):
                        act.wait_ge(half_made, n + k + 1)
                        act.wait_ge(back_done, n + k + 1)
                        act.wait_ge(added[k], i * 64 + added0)
                        for s in range(SUB):
                            last = act.activation(rows[k][:, s, :], back[k % 2][:, s * P:(s + 1) * P], ACT.Copy, scale=half[k % 2][:, s:s + 1])
                        last.then_inc(rows_made, 1)

                run_bodies(act, nb, body)


class Graph:

    def start(self, sems, count):
        before = self.counted.get(id(sems), 0)
        self.counted[id(sems)] = before + count
        return before


def build(nc, g, phases=99):
    g.NTN, g.NTE = g.NP // TILE, g.EP // TILE
    dram = lambda name, shape, dt=F32: nc.dram_tensor(name, shape, dt).ap()
    g.H, g.AGG = dram("H", (g.NP, D)), dram("AGG", (g.NP, D))
    g.KEEP, g.KEEPN = dram("KEEP", (1, g.EP)), dram("KEEPN", (1, g.EP))
    g.IDX = dram("IDX", (g.NTE, P, 16), I32)
    g.YT, g.X = dram("YT", (g.NTN, P, TILE)), dram("X", (g.NP, D))
    g.LOGIT = [dram("LOGIT_SELF", (H, g.EP)), dram("LOGIT_EDGE", (H, g.EP))]
    g.ALPHA = dram("ALPHA", (H, g.EP))
    with ExitStack() as kept:
        sems = lambda name, n: [kept.enter_context(nc.semaphore(f"{name}{k}")) for k in range(n)]
        g.gathered, g.scattered = sems("gathered", K), sems("scattered", K)
        g.counted = {}
        keep = lambda name, shape: kept.enter_context(nc.sbuf_tensor(name, shape, F32))
        g.bn_scale, g.bn_shift = keep("bn_scale", [D, 1]), keep("bn_shift", [D, 1])
        g.wn = keep("wn", [D, HID])
        g.wl, g.wsum, g.wmean = keep("wl", [D, H * D]), keep("wsum", [D, H * D]), keep("wmean", [D, D])
        steps = [prepare_indices, gine_edges, gine_mlp, gine_finish,
                 lambda nc, g: convolution(nc, g, 0), lambda nc, g: convolution(nc, g, 1),
                 attention, gat_nodes, mean_edges]
        for step in steps[:phases]:
            step(nc, g)


def attention(nc, g):
    with nc.sbuf_tensor("srcT", [D, g.EP], F32) as g.srcT:
        gat_logits(nc, g)
        edge_softmax(nc, g, 2, 0, 1.0)
        gat_aggregate(nc, g)


def convolution(nc, g, layer):
    with nc.sbuf_tensor(f"diffT{layer}", [D, g.EP], F32) as g.diffT:
        conv_logits(nc, g, layer)
        edge_softmax(nc, g, layer, 1, 1.0 / H)
        conv_aggregate(nc, g, layer)
    conv_nodes(nc, g, layer, layer == 1)


def as_column(a):
    return a.reshape(-1, 1)


def as_row(a):
    return a.reshape(1, -1)


_WEIGHTS = {
    "w1T": ("L0_gnn_W1", np.transpose), "w2T": ("L0_gnn_W2", np.transpose),
    "b1": ("L0_gnn_b1", as_column), "b2": ("L0_gnn_b2", as_column),
    "gamma": ("L0_gnn_gamma", as_column), "beta": ("L0_gnn_beta", as_column),
    "wnT": ("L2_gnn_W_n", lambda a: a.transpose(1, 0, 2).reshape(D, HID)),
    "a_src": ("L2_gnn_a_src", as_row), "a_dst": ("L2_gnn_a_dst", as_row),
    "mw1": ("L2_gnn_mlp_W1", np.asarray), "mb1": ("L2_gnn_mlp_b1", as_row),
    "mw2": ("L2_gnn_mlp_W2", np.asarray), "mb2": ("L2_gnn_mlp_b2", as_row),
    "wl1": ("L1_gnn_Wl1", np.asarray), "wr1": ("L1_gnn_Wr1", np.asarray), "att1T": ("L1_gnn_att1", np.transpose),
    "cb1": ("L1_gnn_b1", as_row), "cg1": ("L1_gnn_g1", as_row), "cbe1": ("L1_gnn_be1", as_row),
    "wl2": ("L1_gnn_Wl2", np.asarray), "wr2": ("L1_gnn_Wr2", np.asarray), "att2T": ("L1_gnn_att2", np.transpose),
    "cb2": ("L1_gnn_b2", as_row), "cg2": ("L1_gnn_g2", as_row), "cbe2": ("L1_gnn_be2", as_row),
}


def layout(inputs):
    x, src, dst, ea = (np.asarray(inputs[k]) for k in ("x", "src", "dst", "edge_attr_128"))
    n, e = len(x), len(src)
    npad, epad = padded(n, NB), padded(e, K)

    def pad(a, rows, value=0):
        return np.concatenate([a, np.full((rows - len(a), *a.shape[1:]), value, a.dtype)])

    def tiles(a):
        return np.ascontiguousarray(a.reshape(-1, SUB, P).transpose(0, 2, 1))

    src, dst = pad(src, epad, n), pad(dst, epad, n)
    before, after = np.append(np.int32(-1), dst[:-1]), np.append(dst[1:], np.int32(-1))
    arrays = {
        "x": pad(x, npad), "ea": pad(ea, epad),
        "src_t": tiles(src), "dst_t": tiles(dst), "nxt_t": tiles(after),
        "dst_r": dst[None], "prev_r": before[None], "next_r": after[None],
    }
    for name, (source, turn) in _WEIGHTS.items():
        arrays[name] = np.ascontiguousarray(turn(np.asarray(inputs[source])))
    return arrays, (n, npad, epad)


def declare_and_build(nc, arrays, sizes, phases=99):
    g = Graph()
    g.N, g.NP, g.EP = sizes
    given = {name: nc.dram_tensor(name, a.shape, mybir.dt.from_np(a.dtype), kind="ExternalInput").ap()
             for name, a in arrays.items()}
    g.x, g.ea, g.src_t, g.dst_t, g.nxt_t, g.dst_r, g.prev_r, g.next_r = (
        given[n] for n in ("x", "ea", "src_t", "dst_t", "nxt_t", "dst_r", "prev_r", "next_r"))
    g.w1T, g.w2T, g.b1, g.b2, g.gamma, g.beta = (
        given[n] for n in ("w1T", "w2T", "b1", "b2", "gamma", "beta"))
    g.wnT, g.a_src, g.a_dst, g.mw1, g.mb1, g.mw2, g.mb2 = (
        given[n] for n in ("wnT", "a_src", "a_dst", "mw1", "mb1", "mw2", "mb2"))
    g.conv_weights = [tuple(given[f"{n}{j}{t}"] for n, t in (("wl", ""), ("wr", ""), ("att", "T"))) for j in (1, 2)]
    g.conv_norms = [tuple(given[f"{n}{j}"] for n in ("cb", "cg", "cbe")) for j in (1, 2)]
    g.out = nc.dram_tensor("out", (g.NP + g.EP, D), F32, kind="ExternalOutput").ap()
    build(nc, g, phases)


def kernel(**inputs):
    import concourse.bacc as bacc
    from concourse.bass_utils import run_bass_kernel_spmd

    arrays, sizes = layout(inputs)
    nc = bacc.Bacc("TRN2", target_bir_lowering=False, num_devices=1)
    declare_and_build(nc, arrays, sizes)
    result = run_bass_kernel_spmd(nc, [arrays], core_ids=[0])
    return result.results[0]["out"][:sizes[0]]
```
